# Optimizing a Trainium2 kernel written in Bass

```python
import numpy as np
import jax
import jax.numpy as jnp

def _softmax(x, axis=-1):
    return jax.nn.softmax(x, axis=axis)

def _gelu(x):
    return jax.nn.gelu(x, approximate=True)

def _silu(x):
    return jax.nn.silu(x)

def _sigmoid(x):
    return jax.nn.sigmoid(x)

def _layernorm(x, axis=-1, eps=1e-05):
    m = jnp.mean(x, axis=axis, keepdims=True)
    v = jnp.var(x, axis=axis, keepdims=True)
    return (x - m) / jnp.sqrt(v + eps)

def _scatter_add(tgt, idx, src, axis=0):
    return tgt.at[idx].add(src)

def _segment_sum(src, seg, n):
    return jax.ops.segment_sum(src, seg, n)
kernel_name = 'mk_flamingo_gated_d4_seqx_r8_e3a90e'

def setup_inputs(seed: int=0):
    np.random.seed(seed)
    _w = jnp.asarray

    def _rec_inputs():
        import jax
        import jax.numpy as jnp
        _rk = jax.random.key(seed)
        x = 7.22e-05 + 1 * jax.random.normal(jax.random.fold_in(_rk, 1), (8, 128, 256), jnp.float32)
        _lenS = 128 - jax.random.randint(jax.random.fold_in(_rk, 7), (8,), 0, max(1, 128 // 4) + 1, jnp.int32)
        _lenS2 = 128 - jax.random.randint(jax.random.fold_in(_rk, 8), (8,), 0, max(1, 128 // 4) + 1, jnp.int32)
        _ctx_2048P = jax.random.normal(jax.random.fold_in(_rk, 11), (8, 16, 256), jnp.float32)
        _ctx_2048c = jax.random.dirichlet(jax.random.fold_in(_rk, 511), 0.3 * jnp.ones((16,), jnp.float32), (8, 128))
        _ctx_2048t = jnp.einsum('bsk,bkd->bsd', _ctx_2048c, _ctx_2048P)
        _ctx_2048t = _ctx_2048t * jax.lax.rsqrt(jnp.mean(jnp.square(_ctx_2048t)) + 1e-12) * 0.953939
        ctx_2048 = 4.13588e-05 + 0.999923 * (_ctx_2048t + 0.3 * jax.random.normal(jax.random.fold_in(_rk, 611), (8, 128, 256), jnp.float32))
        _validS = jnp.arange(128)[None, :] < _lenS[:, None]
        _validS2 = jnp.arange(128)[None, :] < _lenS2[:, None]
        _causal = jnp.tril(jnp.ones((128, 128), dtype=bool))
        mask_BxS2_ik0 = jnp.where(jnp.broadcast_to(_validS2[:, :], (8, 128)), 0, 1).astype(jnp.int32)
        _g = jax.random.normal(jax.random.fold_in(_rk, 9001), (2, 4), jnp.float32)
        _g = jnp.sign(_g) * jnp.maximum(jnp.abs(_g), 1.0) + (_g == 0) * 1.0
        g_xattn = _g[0]
        g_ffn = _g[1]
        return (x, ctx_2048, mask_BxS2_ik0, g_xattn, g_ffn)
    x, ctx_2048, mask_BxS2_ik0, g_xattn, g_ffn = _rec_inputs()

    def _L0_xattn_setup():
        import jax, jax.numpy as jnp
        import numpy as np
        N_HEADS = 16
        K_CH = 128 // N_HEADS
        SCALE = 1.0 / np.sqrt(K_CH)
        key = jax.random.key(seed)
        ks = jax.random.split(key, 10)
        B, C, T = (4, 128, 256)
        Cout = 128
        xavier = lambda k, o, i: jax.random.uniform(k, (o, i), jnp.float32, -1.0, 1.0) * np.sqrt(6.0 / (o + i))
        return {'x': jax.random.normal(ks[0], (B, C, T), jnp.float32), 'c': jax.random.normal(ks[1], (B, C, T), jnp.float32), 'Wq': xavier(ks[2], C, C), 'bq': jnp.zeros((C,), jnp.float32), 'Wk': xavier(ks[3], C, C), 'bk': jnp.zeros((C,), jnp.float32), 'Wv': xavier(ks[4], C, C), 'bv': jnp.zeros((C,), jnp.float32), 'Wo': xavier(ks[5], Cout, C), 'bo': jnp.zeros((Cout,), jnp.float32)}
    _L0_xattn_all = _L0_xattn_setup()
    _L0_xattn_in = {k: v for k, v in _L0_xattn_all.items() if k in ('Wq', 'bq', 'Wk', 'bk', 'Wv', 'bv', 'Wo', 'bo')}
    del _L0_xattn_all

    def _L0_ffn_setup():
        import jax, jax.numpy as jnp
        import numpy as np
        CAPACITY_FACTOR = 1.0

        def _top1_gate(x, w_gate):
            S, E = (x.shape[0], w_gate.shape[1])
            capacity = int(CAPACITY_FACTOR * S / E)
            logits = x @ w_gate
            gates = jax.nn.softmax(logits, axis=-1)
            idx1 = jnp.argmax(gates, axis=-1)
            mask1 = jax.nn.one_hot(idx1, E, dtype=gates.dtype)
            locations1 = jnp.cumsum(mask1, axis=0) - mask1
            mask1 = mask1 * (locations1 < capacity)
            locations1_s = jnp.sum(locations1 * mask1, axis=1).astype(jnp.int32)
            gates_masked = gates * mask1
            loc_oh = jax.nn.one_hot(locations1_s, capacity, dtype=gates.dtype) * jnp.sum(mask1, axis=1, keepdims=True)
            combine_weights = jnp.einsum('se,sc->sec', gates_masked, loc_oh)
            dispatch_mask = (combine_weights > 0).astype(gates.dtype)
            return (combine_weights, dispatch_mask)
        key = jax.random.key(seed)
        k1, k2, k3, k4 = jax.random.split(key, 4)
        B, T, D, E, F = (4, 256, 256, 8, 1024)
        hidden_states = jax.random.normal(k1, (B, T, D), dtype=jnp.float32)
        w_gate = jax.random.normal(k2, (D, E), dtype=jnp.float32) * 0.02
        w1 = jax.random.normal(k3, (E, D, F), dtype=jnp.float32) * 0.02
        w2 = jax.random.normal(k4, (E, F, D), dtype=jnp.float32) * 0.02
        return {'hidden_states': hidden_states, 'w_gate': w_gate, 'w1': w1, 'w2': w2}
    _L0_ffn_all = _L0_ffn_setup()
    _L0_ffn_in = {k: v for k, v in _L0_ffn_all.items() if k in ('w_gate', 'w1', 'w2')}
    del _L0_ffn_all

    def _L1_xattn_setup():
        import jax, jax.numpy as jnp
        import numpy as np
        N_HEAD = 8
        key = jax.random.key(seed)
        k1, k2, k3 = jax.random.split(key, 3)
        B, D, L = (4, 128, 256)
        q = jax.random.normal(k1, (B, D, L), dtype=jnp.float32)
        k = jax.random.normal(k2, (B, D, L), dtype=jnp.float32)
        v = jax.random.normal(k3, (B, D, L), dtype=jnp.float32)
        gamma = jnp.ones((), dtype=jnp.float32)
        return {'q': q, 'k': k, 'v': v, 'gamma': gamma}
    _L1_xattn_all = _L1_xattn_setup()
    _L1_xattn_in = {k: v for k, v in _L1_xattn_all.items() if k in ('gamma',)}
    del _L1_xattn_all

    def _L1_ffn_setup():
        import jax, jax.numpy as jnp
        import numpy as np
        HIDDEN = 256
        INTER = 704
        B, S = (2, 256)

        def _ternary(key, shape):
            return jax.random.randint(key, shape, -1, 2).astype(jnp.float32)
        key = jax.random.key(seed)
        ks = jax.random.split(key, 7)
        x = jax.random.normal(ks[0], (B, S, HIDDEN), dtype=jnp.float32)
        gate_w = _ternary(ks[1], (INTER, HIDDEN))
        up_w = _ternary(ks[2], (INTER, HIDDEN))
        down_w = _ternary(ks[3], (HIDDEN, INTER))
        gate_s = jax.random.uniform(ks[4], (INTER,), minval=0.01, maxval=0.1, dtype=jnp.float32)
        up_s = jax.random.uniform(ks[5], (INTER,), minval=0.01, maxval=0.1, dtype=jnp.float32)
        down_s = jax.random.uniform(ks[6], (HIDDEN,), minval=0.01, maxval=0.1, dtype=jnp.float32)
        return {'x': x, 'gate_w': gate_w, 'up_w': up_w, 'down_w': down_w, 'gate_s': gate_s, 'up_s': up_s, 'down_s': down_s}
    _L1_ffn_all = _L1_ffn_setup()
    _L1_ffn_in = {k: v for k, v in _L1_ffn_all.items() if k in ('gate_w', 'up_w', 'down_w', 'gate_s', 'up_s', 'down_s')}
    del _L1_ffn_all

    def _L2_xattn_setup():
        import jax, jax.numpy as jnp
        import numpy as np
        import math
        H = 256
        NH = 16
        HD = H // NH
        EPS_LN = 1e-05
        RES_SCALE_MAX = 0.3

        def _nan_clean(x, lim=10000.0):
            return jnp.nan_to_num(x, nan=0.0, posinf=lim, neginf=-lim)
        key = jax.random.key(seed)
        ks = jax.random.split(key, 12)
        B, S, T = (4, 256, 32)
        std = 1.0 / math.sqrt(H)
        return {'hidden_states': jax.random.normal(ks[0], (B, S, H), jnp.float32), 'audio_tokens': jax.random.normal(ks[1], (B, T, H), jnp.float32), 'attention_mask': jax.random.randint(ks[2], (B, T), 0, 2, jnp.int32), 'Wq': jax.random.normal(ks[3], (H, H), jnp.float32) * std, 'bq': jnp.zeros((H,), jnp.float32), 'Wk': jax.random.normal(ks[4], (H, H), jnp.float32) * std, 'bk': jnp.zeros((H,), jnp.float32), 'Wv': jax.random.normal(ks[5], (H, H), jnp.float32) * std, 'bv': jnp.zeros((H,), jnp.float32), 'Wo': jax.random.normal(ks[6], (H, H), jnp.float32) * std, 'bo': jnp.zeros((H,), jnp.float32), 'ln_gamma': jnp.ones((H,), jnp.float32), 'ln_beta': jnp.zeros((H,), jnp.float32), 'residual_scale': jnp.float32(0.05)}
    _L2_xattn_all = _L2_xattn_setup()
    _L2_xattn_in = {k: v for k, v in _L2_xattn_all.items() if k in ('Wq', 'bq', 'Wk', 'bk', 'Wv', 'bv', 'Wo', 'bo', 'ln_gamma', 'ln_beta', 'residual_scale')}
    del _L2_xattn_all

    def _L2_ffn_setup():
        import jax, jax.numpy as jnp
        import numpy as np
        B, S, H = (4, 128, 256)
        E = 16
        K = 2
        I = 128
        N_SHARED = 2
        I_SHARED = I * N_SHARED
        RATIO = 0.1
        EPS = 1e-09

        def _swiglu(x, wg, wu, wd):
            return jax.nn.silu(x @ wg) * (x @ wu) @ wd
        key = jax.random.key(seed)
        ks = jax.random.split(key, 9)
        scale = 0.02
        x = jax.random.normal(ks[0], (B, S, H), dtype=jnp.float32)
        centroids = jax.random.normal(ks[1], (E, H), dtype=jnp.float32)
        gate_bias = jnp.zeros((E,), dtype=jnp.float32)
        wg_s = jax.random.normal(ks[2], (H, I_SHARED), dtype=jnp.float32) * scale
        wu_s = jax.random.normal(ks[3], (H, I_SHARED), dtype=jnp.float32) * scale
        wd_s = jax.random.normal(ks[4], (I_SHARED, H), dtype=jnp.float32) * scale
        wg = jax.random.normal(ks[5], (E, H, I), dtype=jnp.float32) * scale
        wu = jax.random.normal(ks[6], (E, H, I), dtype=jnp.float32) * scale
        wd = jax.random.normal(ks[7], (E, I, H), dtype=jnp.float32) * scale
        return {'x': x, 'centroids': centroids, 'gate_bias': gate_bias, 'wg_s': wg_s, 'wu_s': wu_s, 'wd_s': wd_s, 'wg': wg, 'wu': wu, 'wd': wd}
    _L2_ffn_all = _L2_ffn_setup()
    _L2_ffn_in = {k: v for k, v in _L2_ffn_all.items() if k in ('centroids', 'gate_bias', 'wg_s', 'wu_s', 'wd_s', 'wg', 'wu', 'wd')}
    del _L2_ffn_all

    def _L3_xattn_setup():
        import jax, jax.numpy as jnp
        import numpy as np
        D_MODEL = 256
        NUM_HEADS = 16
        HEAD_DIM = D_MODEL // NUM_HEADS

        def _fq_sym(x, axis):
            s = jnp.max(jnp.abs(x), axis=axis, keepdims=True) / 127.0
            s = jnp.maximum(s, 1e-08)
            q = jnp.clip(jnp.round(x / s), -127.0, 127.0) * s
            return x + jax.lax.stop_gradient(q - x)

        def _fq_unsigned(x, axis):
            s = jnp.max(x, axis=axis, keepdims=True) / 255.0
            s = jnp.maximum(s, 1e-08)
            q = jnp.clip(jnp.round(x / s), 0.0, 255.0) * s
            return x + jax.lax.stop_gradient(q - x)
        key = jax.random.key(seed)
        ks = jax.random.split(key, 8)
        B, N, M, C = (2, 256, 64, D_MODEL)
        return {'x': jax.random.normal(ks[0], (B, N, C), jnp.float32), 'cond': jax.random.normal(ks[1], (B, M, C), jnp.float32), 'Wq': jax.random.normal(ks[2], (C, C), jnp.float32) * 0.02, 'bq': jnp.zeros((C,), jnp.float32), 'Wkv': jax.random.normal(ks[3], (C, 2 * C), jnp.float32) * 0.02, 'bkv': jnp.zeros((2 * C,), jnp.float32), 'Wp': jax.random.normal(ks[4], (C, C), jnp.float32) * 0.02, 'bp': jnp.zeros((C,), jnp.float32)}
    _L3_xattn_all = _L3_xattn_setup()
    _L3_xattn_in = {k: v for k, v in _L3_xattn_all.items() if k in ('Wq', 'bq', 'Wkv', 'bkv', 'Wp', 'bp')}
    del _L3_xattn_all

    def _L3_ffn_setup():
        import jax, jax.numpy as jnp
        import numpy as np
        D_MODEL = 256
        D_FF = 1024
        N_EXPERTS = 4
        B, S = (2, 256)
        key = jax.random.key(seed)
        ks = jax.random.split(key, 6)
        scale = 0.02
        return {'hidden_states': jax.random.normal(ks[0], (B, S, D_MODEL), dtype=jnp.float32), 'Wr': jax.random.normal(ks[1], (D_MODEL, N_EXPERTS), dtype=jnp.float32) * scale, 'br': jnp.zeros((N_EXPERTS,), dtype=jnp.float32), 'Wg': jax.random.normal(ks[2], (N_EXPERTS, D_MODEL, D_FF), dtype=jnp.float32) * scale, 'Wu': jax.random.normal(ks[3], (N_EXPERTS, D_MODEL, D_FF), dtype=jnp.float32) * scale, 'Wd': jax.random.normal(ks[4], (N_EXPERTS, D_FF, D_MODEL), dtype=jnp.float32) * scale}
    _L3_ffn_all = _L3_ffn_setup()
    _L3_ffn_in = {k: v for k, v in _L3_ffn_all.items() if k in ('Wr', 'br', 'Wg', 'Wu', 'Wd')}
    del _L3_ffn_all
    return {'x': x, 'ctx_2048': ctx_2048, 'mask_BxS2_ik0': mask_BxS2_ik0, 'g_xattn': g_xattn, 'g_ffn': g_ffn, 'L0_xattn_Wq': _L0_xattn_in['Wq'], 'L0_xattn_bq': _L0_xattn_in['bq'], 'L0_xattn_Wk': _L0_xattn_in['Wk'], 'L0_xattn_bk': _L0_xattn_in['bk'], 'L0_xattn_Wv': _L0_xattn_in['Wv'], 'L0_xattn_bv': _L0_xattn_in['bv'], 'L0_xattn_Wo': _L0_xattn_in['Wo'], 'L0_xattn_bo': _L0_xattn_in['bo'], 'L0_ffn_w_gate': _L0_ffn_in['w_gate'], 'L0_ffn_w1': _L0_ffn_in['w1'], 'L0_ffn_w2': _L0_ffn_in['w2'], 'L1_xattn_gamma': _L1_xattn_in['gamma'], 'L1_ffn_gate_w': _L1_ffn_in['gate_w'], 'L1_ffn_up_w': _L1_ffn_in['up_w'], 'L1_ffn_down_w': _L1_ffn_in['down_w'], 'L1_ffn_gate_s': _L1_ffn_in['gate_s'], 'L1_ffn_up_s': _L1_ffn_in['up_s'], 'L1_ffn_down_s': _L1_ffn_in['down_s'], 'L2_xattn_Wq': _L2_xattn_in['Wq'], 'L2_xattn_bq': _L2_xattn_in['bq'], 'L2_xattn_Wk': _L2_xattn_in['Wk'], 'L2_xattn_bk': _L2_xattn_in['bk'], 'L2_xattn_Wv': _L2_xattn_in['Wv'], 'L2_xattn_bv': _L2_xattn_in['bv'], 'L2_xattn_Wo': _L2_xattn_in['Wo'], 'L2_xattn_bo': _L2_xattn_in['bo'], 'L2_xattn_ln_gamma': _L2_xattn_in['ln_gamma'], 'L2_xattn_ln_beta': _L2_xattn_in['ln_beta'], 'L2_xattn_residual_scale': _L2_xattn_in['residual_scale'], 'L2_ffn_centroids': _L2_ffn_in['centroids'], 'L2_ffn_gate_bias': _L2_ffn_in['gate_bias'], 'L2_ffn_wg_s': _L2_ffn_in['wg_s'], 'L2_ffn_wu_s': _L2_ffn_in['wu_s'], 'L2_ffn_wd_s': _L2_ffn_in['wd_s'], 'L2_ffn_wg': _L2_ffn_in['wg'], 'L2_ffn_wu': _L2_ffn_in['wu'], 'L2_ffn_wd': _L2_ffn_in['wd'], 'L3_xattn_Wq': _L3_xattn_in['Wq'], 'L3_xattn_bq': _L3_xattn_in['bq'], 'L3_xattn_Wkv': _L3_xattn_in['Wkv'], 'L3_xattn_bkv': _L3_xattn_in['bkv'], 'L3_xattn_Wp': _L3_xattn_in['Wp'], 'L3_xattn_bp': _L3_xattn_in['bp'], 'L3_ffn_Wr': _L3_ffn_in['Wr'], 'L3_ffn_br': _L3_ffn_in['br'], 'L3_ffn_Wg': _L3_ffn_in['Wg'], 'L3_ffn_Wu': _L3_ffn_in['Wu'], 'L3_ffn_Wd': _L3_ffn_in['Wd']}

def reference(x, ctx_2048, mask_BxS2_ik0, g_xattn, g_ffn, L0_xattn_Wq, L0_xattn_bq, L0_xattn_Wk, L0_xattn_bk, L0_xattn_Wv, L0_xattn_bv, L0_xattn_Wo, L0_xattn_bo, L0_ffn_w_gate, L0_ffn_w1, L0_ffn_w2, L1_xattn_gamma, L1_ffn_gate_w, L1_ffn_up_w, L1_ffn_down_w, L1_ffn_gate_s, L1_ffn_up_s, L1_ffn_down_s, L2_xattn_Wq, L2_xattn_bq, L2_xattn_Wk, L2_xattn_bk, L2_xattn_Wv, L2_xattn_bv, L2_xattn_Wo, L2_xattn_bo, L2_xattn_ln_gamma, L2_xattn_ln_beta, L2_xattn_residual_scale, L2_ffn_centroids, L2_ffn_gate_bias, L2_ffn_wg_s, L2_ffn_wu_s, L2_ffn_wd_s, L2_ffn_wg, L2_ffn_wu, L2_ffn_wd, L3_xattn_Wq, L3_xattn_bq, L3_xattn_Wkv, L3_xattn_bkv, L3_xattn_Wp, L3_xattn_bp, L3_ffn_Wr, L3_ffn_br, L3_ffn_Wg, L3_ffn_Wu, L3_ffn_Wd):
    import jax
    import jax.numpy as jnp

    def _L0_xattn_ref(x, c, Wq, bq, Wk, bk, Wv, bv, Wo, bo):
        import jax, jax.numpy as jnp
        import numpy as np
        N_HEADS = 16
        K_CH = 128 // N_HEADS
        SCALE = 1.0 / np.sqrt(K_CH)
        B, C, T = x.shape
        H, K = (N_HEADS, K_CH)
        q = jnp.einsum('oc,bct->bot', Wq, x) + bq[None, :, None]
        k = jnp.einsum('oc,bct->bot', Wk, c) + bk[None, :, None]
        v = jnp.einsum('oc,bct->bot', Wv, c) + bv[None, :, None]
        q = q.reshape(B, H, K, T)
        k = k.reshape(B, H, K, -1)
        v = v.reshape(B, H, K, -1)
        scores = jnp.einsum('bhkt,bhks->bhts', q, k) * SCALE
        p = jax.nn.softmax(scores, axis=-1)
        out = jnp.einsum('bhts,bhks->bhkt', p, v)
        out = out.reshape(B, H * K, T)
        return jnp.einsum('oc,bct->bot', Wo, out) + bo[None, :, None]

    def _L0_ffn_ref(hidden_states, w_gate, w1, w2):
        import jax, jax.numpy as jnp
        import numpy as np
        CAPACITY_FACTOR = 1.0

        def _top1_gate(x, w_gate):
            S, E = (x.shape[0], w_gate.shape[1])
            capacity = int(CAPACITY_FACTOR * S / E)
            logits = x @ w_gate
            gates = jax.nn.softmax(logits, axis=-1)
            idx1 = jnp.argmax(gates, axis=-1)
            mask1 = jax.nn.one_hot(idx1, E, dtype=gates.dtype)
            locations1 = jnp.cumsum(mask1, axis=0) - mask1
            mask1 = mask1 * (locations1 < capacity)
            locations1_s = jnp.sum(locations1 * mask1, axis=1).astype(jnp.int32)
            gates_masked = gates * mask1
            loc_oh = jax.nn.one_hot(locations1_s, capacity, dtype=gates.dtype) * jnp.sum(mask1, axis=1, keepdims=True)
            combine_weights = jnp.einsum('se,sc->sec', gates_masked, loc_oh)
            dispatch_mask = (combine_weights > 0).astype(gates.dtype)
            return (combine_weights, dispatch_mask)
        B, T, D = hidden_states.shape
        x = hidden_states.reshape(-1, D)
        combine_weights, dispatch_mask = _top1_gate(x, w_gate)
        dispatched = jnp.einsum('sec,sm->ecm', dispatch_mask, x)
        h = jax.nn.gelu(jnp.einsum('ecd,edf->ecf', dispatched, w1))
        expert_out = jnp.einsum('ecf,efd->ecd', h, w2)
        combined = jnp.einsum('sec,ecm->sm', combine_weights, expert_out)
        return combined.reshape(B, T, D)

    def _L1_xattn_ref(q, k, v, gamma):
        import jax, jax.numpy as jnp
        import numpy as np
        N_HEAD = 8
        B, Dq, Lq = q.shape
        Dv, Lk = (v.shape[-2], v.shape[-1])
        h = N_HEAD
        dq = Dq // h
        dv = Dv // h
        qh = q.reshape(B, h, dq, Lq)
        kh = k.reshape(B, h, dq, Lk)
        vh = v.reshape(B, h, dv, Lk)
        scale = 1.0 / jnp.sqrt(jnp.asarray(dq, dtype=q.dtype))
        qk = jnp.einsum('bhdq,bhdl->bhql', qh, kh) * scale
        sm = jax.nn.softmax(qk, axis=-1)
        ret = jnp.einsum('bhql,bhdl->bhdq', sm, vh)
        ret = ret.reshape(B, Dv, Lq)
        return gamma * ret

    def _L1_ffn_ref(x, gate_w, up_w, down_w, gate_s, up_s, down_s):
        import jax, jax.numpy as jnp
        import numpy as np
        HIDDEN = 256
        INTER = 704
        B, S = (2, 256)

        def _ternary(key, shape):
            return jax.random.randint(key, shape, -1, 2).astype(jnp.float32)
        b, s, h = x.shape
        xf = x.reshape(b * s, h)
        g = jnp.einsum('th,ih->ti', xf, gate_w) * gate_s
        u = jnp.einsum('th,ih->ti', xf, up_w) * up_s
        hdn = jax.nn.silu(g) * u
        out = jnp.einsum('ti,hi->th', hdn, down_w) * down_s
        return out.reshape(b, s, -1)

    def _L2_xattn_ref(hidden_states, audio_tokens, attention_mask, Wq, bq, Wk, bk, Wv, bv, Wo, bo, ln_gamma, ln_beta, residual_scale):
        import jax, jax.numpy as jnp
        import numpy as np
        import math
        H = 256
        NH = 16
        HD = H // NH
        EPS_LN = 1e-05
        RES_SCALE_MAX = 0.3

        def _nan_clean(x, lim=10000.0):
            return jnp.nan_to_num(x, nan=0.0, posinf=lim, neginf=-lim)
        B, S, _ = hidden_states.shape
        T = audio_tokens.shape[1]
        hs = _nan_clean(hidden_states).astype(jnp.float32)
        at = _nan_clean(audio_tokens).astype(jnp.float32)

        def proj(x, W, b, L):
            y = x @ W.T + b
            return y.reshape(B, L, NH, HD).transpose(0, 2, 1, 3)
        q = _nan_clean(proj(hs, Wq, bq, S))
        k = _nan_clean(proj(at, Wk, bk, T))
        v = _nan_clean(proj(at, Wv, bv, T))
        scale = max(math.sqrt(HD), 1e-08)
        scores = jnp.einsum('bhsd,bhtd->bhst', q, k) / scale
        scores = jnp.clip(scores, -50.0, 50.0)
        scores = jnp.nan_to_num(scores, nan=0.0, posinf=50.0, neginf=-50.0)
        attend = (attention_mask.astype(jnp.float32) > 0.5)[:, None, None, :]
        scores = jnp.where(attend, scores, -10000.0)
        scores = jnp.clip(scores, -50.0, 50.0)
        probs = jax.nn.softmax(scores, axis=-1)
        probs = jnp.nan_to_num(probs, nan=0.0, posinf=1.0, neginf=0.0)
        probs = probs / (probs.sum(axis=-1, keepdims=True) + 1e-08)
        ctx = jnp.einsum('bhst,bhtd->bhsd', probs, v)
        ctx = ctx.transpose(0, 2, 1, 3).reshape(B, S, H)
        delta = _nan_clean(ctx @ Wo.T + bo)
        rs = jnp.clip(residual_scale, 0.0, RES_SCALE_MAX)
        delta = rs * delta
        mu = delta.mean(axis=-1, keepdims=True)
        var = jnp.mean((delta - mu) ** 2, axis=-1, keepdims=True)
        delta = (delta - mu) / jnp.sqrt(var + EPS_LN) * ln_gamma + ln_beta
        return delta

    def _L2_ffn_ref(x, centroids, gate_bias, wg_s, wu_s, wd_s, wg, wu, wd):
        import jax, jax.numpy as jnp
        import numpy as np
        B, S, H = (4, 128, 256)
        E = 16
        K = 2
        I = 128
        N_SHARED = 2
        I_SHARED = I * N_SHARED
        RATIO = 0.1
        EPS = 1e-09

        def _swiglu(x, wg, wu, wd):
            return jax.nn.silu(x @ wg) * (x @ wu) @ wd
        shared = _swiglu(x, wg_s, wu_s, wd_s) * RATIO
        affinity = jax.nn.sigmoid(jnp.einsum('bsh,eh->bse', x, centroids))
        biased = affinity + gate_bias
        _, top_idx = jax.lax.top_k(biased, K)
        top_aff = jnp.take_along_axis(affinity, top_idx, axis=-1)
        weights = top_aff / (top_aff.sum(-1, keepdims=True) + EPS)
        mask = (jax.nn.one_hot(top_idx, E, dtype=x.dtype) * weights[..., None]).sum(-2)
        routed = jnp.zeros_like(x)
        for e in range(E):
            routed = routed + mask[..., e:e + 1] * _swiglu(x, wg[e], wu[e], wd[e])
        return shared + routed

    def _L3_xattn_ref(x, cond, Wq, bq, Wkv, bkv, Wp, bp):
        import jax, jax.numpy as jnp
        import numpy as np
        D_MODEL = 256
        NUM_HEADS = 16
        HEAD_DIM = D_MODEL // NUM_HEADS

        def _fq_sym(x, axis):
            s = jnp.max(jnp.abs(x), axis=axis, keepdims=True) / 127.0
            s = jnp.maximum(s, 1e-08)
            q = jnp.clip(jnp.round(x / s), -127.0, 127.0) * s
            return x + jax.lax.stop_gradient(q - x)

        def _fq_unsigned(x, axis):
            s = jnp.max(x, axis=axis, keepdims=True) / 255.0
            s = jnp.maximum(s, 1e-08)
            q = jnp.clip(jnp.round(x / s), 0.0, 255.0) * s
            return x + jax.lax.stop_gradient(q - x)
        B, N, C = x.shape
        H, hd = (NUM_HEADS, HEAD_DIM)
        q = (x @ Wq + bq).reshape(1, B * N, H, hd)
        kv = (cond @ Wkv + bkv).reshape(1, -1, 2, H, hd)
        k, v = (kv[:, :, 0], kv[:, :, 1])
        scale = 1.0 / np.sqrt(hd).astype(np.float32)
        q = jnp.transpose(q * scale, (0, 2, 1, 3))
        k = jnp.transpose(k, (0, 2, 1, 3))
        v = jnp.transpose(v, (0, 2, 1, 3))
        q = _fq_sym(q, axis=-1)
        k = _fq_sym(k, axis=-1)
        v = _fq_sym(v, axis=2)
        attn = jnp.einsum('bhqd,bhkd->bhqk', q, k)
        attn = jax.nn.softmax(attn.astype(jnp.float32), axis=-1)
        attn = _fq_unsigned(attn, axis=-1)
        out = jnp.einsum('bhqk,bhkd->bhqd', attn, v)
        out = jnp.transpose(out, (0, 2, 1, 3)).reshape(B, N, C)
        return out @ Wp + bp

    def _L3_ffn_ref(hidden_states, Wr, br, Wg, Wu, Wd):
        import jax, jax.numpy as jnp
        import numpy as np
        D_MODEL = 256
        D_FF = 1024
        N_EXPERTS = 4
        B, S = (2, 256)
        b, s, d = hidden_states.shape
        x = hidden_states.reshape(-1, d)
        logits = x @ Wr + br
        probs = jax.nn.softmax(logits, axis=-1)
        top_w, top_idx = jax.lax.top_k(probs, 1)
        g = jnp.einsum('td,edf->tef', x, Wg)
        u = jnp.einsum('td,edf->tef', x, Wu)
        h = jax.nn.silu(g) * u
        y = jnp.einsum('tef,efd->ted', h, Wd)
        sel = jnp.take_along_axis(y, top_idx[:, :, None], axis=1)[:, 0]
        out = sel * top_w
        return out.reshape(b, s, d)
    x = x + jnp.tanh(g_xattn[0]) * _L0_xattn_ref(_layernorm(x, axis=-1), ctx_2048, L0_xattn_Wq, L0_xattn_bq, L0_xattn_Wk, L0_xattn_bk, L0_xattn_Wv, L0_xattn_bv, L0_xattn_Wo, L0_xattn_bo)
    x = x + jnp.tanh(g_ffn[0]) * _L0_ffn_ref(_layernorm(x, axis=-1), L0_ffn_w_gate, L0_ffn_w1, L0_ffn_w2)
    x = x + jnp.tanh(g_xattn[1]) * _L1_xattn_ref(_layernorm(x, axis=-1), ctx_2048, ctx_2048, L1_xattn_gamma)
    x = x + jnp.tanh(g_ffn[1]) * _L1_ffn_ref(_layernorm(x, axis=-1), L1_ffn_gate_w, L1_ffn_up_w, L1_ffn_down_w, L1_ffn_gate_s, L1_ffn_up_s, L1_ffn_down_s)
    x = x + jnp.tanh(g_xattn[2]) * _L2_xattn_ref(_layernorm(x, axis=-1), ctx_2048, mask_BxS2_ik0, L2_xattn_Wq, L2_xattn_bq, L2_xattn_Wk, L2_xattn_bk, L2_xattn_Wv, L2_xattn_bv, L2_xattn_Wo, L2_xattn_bo, L2_xattn_ln_gamma, L2_xattn_ln_beta, L2_xattn_residual_scale)
    x = x + jnp.tanh(g_ffn[2]) * _L2_ffn_ref(_layernorm(x, axis=-1), L2_ffn_centroids, L2_ffn_gate_bias, L2_ffn_wg_s, L2_ffn_wu_s, L2_ffn_wd_s, L2_ffn_wg, L2_ffn_wu, L2_ffn_wd)
    x = x + jnp.tanh(g_xattn[3]) * _L3_xattn_ref(_layernorm(x, axis=-1), ctx_2048, L3_xattn_Wq, L3_xattn_bq, L3_xattn_Wkv, L3_xattn_bkv, L3_xattn_Wp, L3_xattn_bp)
    x = x + jnp.tanh(g_ffn[3]) * _L3_ffn_ref(_layernorm(x, axis=-1), L3_ffn_Wr, L3_ffn_br, L3_ffn_Wg, L3_ffn_Wu, L3_ffn_Wd)
    return x

_drawn_inputs = setup_inputs


def setup_inputs(seed=0):
    import zlib

    import numpy as np

    out = dict(_drawn_inputs(seed))
    spreads = {'L0_xattn_bq': (0.0, 0.454),
     'L0_xattn_bk': (0.0, 2.0),
     'L0_xattn_bv': (0.0, 0.8),
     'L0_xattn_bo': (0.0, 0.8),
     'L2_xattn_bq': (0.0, 0.301),
     'L2_xattn_bk': (0.0, 2.0),
     'L2_xattn_bv': (0.0, 0.1),
     'L2_xattn_bo': (0.0, 0.1),
     'L2_xattn_ln_gamma': (1.0, 0.2),
     'L2_xattn_ln_beta': (0.0, 0.1),
     'L2_ffn_gate_bias': (0.0, 0.8),
     'L3_xattn_bq': (0.0, 0.8),
     'L3_xattn_bkv': (0.0, 0.464),
     'L3_xattn_bp': (0.0, 0.1),
     'L3_ffn_br': (0.0, 0.8)}
    factors = {'g_ffn': 28.664,
     'L0_ffn_w_gate': 4.167,
     'L0_ffn_w1': 3.972,
     'L0_ffn_w2': 3.894,
     'L2_ffn_centroids': 8.0,
     'L2_ffn_wg_s': 8.0,
     'L2_ffn_wu_s': 8.0,
     'L2_ffn_wd_s': 8.0,
     'L2_ffn_wg': 8.0,
     'L2_ffn_wu': 8.0,
     'L2_ffn_wd': 8.0,
     'L3_xattn_Wq': 8.0,
     'L3_xattn_Wkv': 5.858,
     'L3_xattn_Wp': 2.954,
     'L3_ffn_Wr': 8.0,
     'L3_ffn_Wg': 6.983,
     'L3_ffn_Wu': 6.965,
     'L3_ffn_Wd': 6.936}
    for name, (base, spread) in spreads.items():
        noise = np.random.default_rng([zlib.crc32(name.encode()), seed]).standard_normal(out[name].shape)
        drawn = base * np.exp(spread * noise) if base else spread * noise
        out[name] = jnp.asarray(drawn.astype(out[name].dtype))
    for name, factor in factors.items():
        out[name] = (out[name] * factor).astype(out[name].dtype)
    return out
```

```python
from contextlib import ExitStack

import concourse.bass as bass
from concourse import mybir

F32 = mybir.dt.float32
BF16 = mybir.dt.bfloat16
I32 = mybir.dt.int32
U32 = mybir.dt.uint32
ALU = mybir.AluOpType
ACT = mybir.ActivationFunctionType
AX = mybir.AxisListType


class Layer:

    def __init__(self, layer=None, H=None, d=None, U=None, nb=None, TC=None, T=None, NC=None,
                 has_max=None, G=None, halves=None):
        self.layer, self.H, self.d, self.U, self.nb, self.TC, self.T, self.NC = layer, H, d, U, nb, TC, T, NC
        self.has_max, self.G, self.halves = has_max, G, halves


class Blk:

    def __init__(self, widths=None, item=None, off=None, F=None, mask=None):
        self.widths, self.item, self.off, self.F, self.mask = widths, item, off, F, mask


class Norm:

    def __init__(self, b=None, stat=None, i=None):
        self.b, self.stat, self.i = b, stat, i


class Record:

    def __init__(self, kind=None, A=None, u=None, b=None, i=None, g=None, c=None, j=None, tc=None,
                 e=None, h=None, k=None, m=None, n=None, o=None, p=None, s=None, q=None, sg=None,
                 clip=None, un=None, item=None, free=None, stats=None, last_P=None, last_S=None,
                 neg=None, layer=None, xn=None, lm=None, first=None, blk=None, tg=None, ch=None,
                 width=None, h_free=None, last_T=None, last_m=None, done_before=None, m_prev=None,
                 m_prev2=None, m_last_norm=None, prev_m=None, prev_turned=None, k_quant=None,
                 q_quant=None, clip3=None, lms=None, exp_i=None, after=None, x_after=None):
        self.kind, self.A, self.u, self.b, self.i, self.g, self.c, self.j = kind, A, u, b, i, g, c, j
        self.tc, self.e, self.h, self.k, self.m, self.n, self.o, self.p = tc, e, h, k, m, n, o, p
        self.s, self.q, self.sg, self.clip, self.un, self.item, self.free, self.stats = s, q, sg, clip, un, item, free, stats
        self.last_P, self.last_S, self.neg, self.layer, self.xn, self.lm, self.first, self.blk = last_P, last_S, neg, layer, xn, lm, first, blk
        self.tg, self.ch, self.width, self.h_free, self.last_T, self.last_m, self.done_before, self.m_prev = tg, ch, width, h_free, last_T, last_m, done_before, m_prev
        self.m_prev2, self.m_last_norm, self.prev_m, self.prev_turned, self.k_quant, self.q_quant, self.clip3, self.lms = m_prev2, m_last_norm, prev_m, prev_turned, k_quant, q_quant, clip3, lms
        self.exp_i, self.after, self.x_after = exp_i, after, x_after


P = 128
NB = 8
D = 256
S = 128
NT = NB * S
EPS = 1e-5
EW = 32
SUMCOL = 16
MAGIC = 12582912.0
LN255 = 5.541263545158426
FIRST_PARTS = (0, 1, 2, 0, 1, 0)
SECOND_PARTS = (0, 0, 0, 1, 1, 2)
SLOTW = 6144
TRASH = NT

ROWS = [("g_xattn", 4), ("g_ffn", 4), ("gamma", 1), ("rscale", 1), ("bv0", 128), ("bv2", 256),
        ("bo2", 256), ("lng", 256), ("lnb", 256), ("bq3", 256), ("bk3", 256), ("bp3", 256),
        ("ds1", 256), ("br3", 4), ("gb2", 16)]
COLS = [("bq0", 1), ("bk0", 1), ("bo0", 1), ("bq2", 2), ("bk2", 2), ("bv3", 2), ("gs1", 6), ("us1", 6)]
CONST = [("ident", 128), ("before", 128), ("ones", 128), ("desc", 16), ("base", 8), ("trash", 8),
         ("mhalf", 1), ("sumsel", 32)]


def offsets(items):
    at, out = 0, {}
    for name, n in items:
        out[name] = (at, at + n)
        at += n
    return out, at


def attn(layer, heads, d, units, batches, tcs, chunks, has_max):
    return Layer(layer=layer, H=heads, d=d, U=units, nb=batches, TC=tcs, T=tcs * P,
                           NC=chunks, has_max=has_max, G=heads // 4, halves=heads * d // P)


ATT = [attn(0, 16, 8, 8, 1, 2, 2, True), attn(1, 8, 16, 8, 1, 2, 2, True),
       attn(2, 16, 16, 8, 1, 1, 1, False), attn(3, 16, 16, 4, 2, 2, 8, True)]


def ffn_blocks(layer):
    if layer == 1:
        return [Blk(widths=[128] * 5 + [64], item=8, off=0, F=704, mask=None)]
    if layer == 2:
        out = [Blk(widths=[128] * 2, item=9, off=0, F=256, mask=None)]
        return out + [Blk(widths=[128], item=10 + e // 8, off=768 * (e % 8), F=128, mask=e)
                      for e in range(16)]
    return [Blk(widths=[128] * 8, item=12 + e, off=0, F=1024, mask=e) for e in range(4)]


def plan():
    steps, n = [], dict(M=0, S=0, T=0, P=0, O=0, unit=0, stat=0, xn=0, q=0, k=0, neg=0, sg=0, clip=0, bar=0)

    def take(ring, count=1):
        at = n[ring]
        n[ring] += count
        return list(range(at, at + count)) if count > 1 else at

    def add(kind, **k):
        s = Record(kind=kind, **k)
        steps.append(s)
        return s

    stat_of = {}

    def stats(b):
        stat_of[b] = take("stat")
        add("stats", b=b, i=stat_of[b])

    def normed(b):
        take("xn")
        return Norm(b=b, stat=stat_of[b], i=n["xn"] - 1)

    def barrier():
        n["bar"] += 1
        add("barrier", stats=n["stat"])

    item_free = {}

    def wload(i):
        add("wload", item=i, free=item_free.get(i - 2))

    def attention(A):
        barrier()
        add("attn_begin", A=A)
        if A.layer == 3:
            for u in range(A.U):
                add("kprep", A=A, u=u, m=take("M", 6), k=take("k"))
            add("vscale", A=A, last_m=n["M"] - 1)
            for c in range(NB):
                add("vturn", A=A, c=c, m=take("M"))
        units = []

        def front(u):
            s = Record(A=A, u=u, g=take("unit"), q=take("q"), k=None,
                                xn=[normed(u * A.nb + j) for j in range(A.nb)])
            if A.layer < 3:
                s.k = take("k")
            s.m = take("M", {0: 3, 1: 1, 2: 6 - 2, 3: 6}[A.layer]) if A.layer != 1 else []
            s.kind = "front"
            s.done_before = units[-3].last_P if len(units) >= 3 else n["P"] - 1
            steps.append(s)
            units.append(s)
            s.last_P = None

        def maxes(s):
            out = []
            for tc in range(A.TC):
                per = A.H * A.NC * P // 512
                for j in range(per):
                    out.append(dict(kind="smax", A=A, un=s, tc=tc, j=j, first=(tc == 0 and j == 0)))
            return out

        def body(s):
            out, prev = [], None
            for g in range(A.G):
                for c in range(A.NC):
                    st = dict(kind="st", A=A, un=s, g=g, c=c, first=(g == 0 and c == 0))
                    out.append([st])
                    if prev is not None:
                        out[-1].append(dict(kind="pv", of=prev))
                        if prev["c"] == A.NC - 1:
                            out[-1].append(dict(kind="onorm", A=A, un=s, g=prev["g"]))
                    prev = st
            out.append([dict(kind="pv", of=prev), dict(kind="onorm", A=A, un=s, g=A.G - 1)])
            return out

        def emit(dct):
            kind = dct["kind"]
            if kind == "smax":
                s = add(**dct, n=take("S"))
                dct["un"].last_S = s.n
            elif kind == "st":
                s = add(**dct, n=take("T"), p=take("P"))
                s.clip = take("clip") if A.layer == 2 else None
                dct["step"] = s
            elif kind == "pv":
                s = dct["of"]["step"]
                if s.c == 0:
                    s.un.o = take("O")
                add("pv", A=A, un=s.un, g=s.g, c=s.c, n=s.n, p=s.p, o=s.un.o, clip=s.clip)
                s.un.last_P = s.p
            else:
                u = dct["un"]
                add("onorm", A=A, un=u, g=dct["g"], o=u.o, p=u.last_P, m=take("M"))

        lag = 2 if A.has_max else 1
        for i in range(A.U + lag):
            if i < A.U:
                front(i)
            first = maxes(units[i - 1]) if A.has_max and 0 <= i - 1 < A.U else []
            second = body(units[i - lag]) if i >= lag else []
            done = 0
            for k, group in enumerate(second or [[]]):
                upto = len(first) * (k + 1) // max(len(second), 1)
                for f in first[done:upto]:
                    emit(f)
                done = upto
                for f in group:
                    emit(f)
            if first:
                add("negmax", A=A, un=units[i - 1], i=take("neg"), m=take("M"))
                units[i - 1].neg = n["neg"] - 1
            if i >= lag:
                u = units[i - lag]
                add("out", A=A, un=u, m=take("M", {0: 2, 1: 1, 2: 2, 3: 4}[A.layer]))
                for j in range(A.nb):
                    stats(u.u * A.nb + j)

    def turned(layer):
        for b in range(NB):
            add("xt", layer=layer, xn=normed(b), m=take("M"), lm=take("M") if layer != 1 else None)

    def moe_capacity():
        barrier()
        wload(1)
        turned(0)
        add("route", layer=0, m=take("M"))
        for b in range(NB):
            add("scatter", b=b)
        for e in range(8):
            s = add("expert", e=e, m=take("M"), n=take("T"), s=take("S"))
            item_free[e] = s.s
            if e + 2 <= 8:
                wload(e + 2)
        for b in range(NB):
            add("combine", b=b)
            stats(b)

    def dense(layer):
        barrier()
        if layer == 2:
            wload(9)
        if layer == 3:
            wload(13)
        turned(layer)
        if layer > 1:
            add("route", layer=layer, m=None)
        blocks = ffn_blocks(layer)
        pending, hcount, h_free = None, 0, {}

        def down(work):
            blk, tg, h, last_T = work
            final = blk is blocks[-1]
            for tc in range(4):
                s = add("down", layer=layer, blk=blk, tg=tg, tc=tc, h=h, last_T=last_T, n=take("S"))
                if final:
                    stats(tg * 4 + tc)
            h_free[h] = s.n
            item_free[blk.item] = s.n
            if tg == 1:
                after = {(2, 9): 11, (2, 10): 12, (3, 12): 14, (3, 13): 15, (1, 8): 10}.get((layer, blk.item))
                last_of_item = blk is [x for x in blocks if x.item == blk.item][-1]
                if after is not None and last_of_item:
                    wload(after)

        for blk in blocks:
            for tg in range(2):
                h = hcount
                hcount += 1
                for ch, width in enumerate(blk.widths):
                    s = add("gu", layer=layer, blk=blk, tg=tg, ch=ch, width=width, h=h,
                            h_free=h_free.get(h - 2), n=take("T"), sg=take("sg"))
                if pending:
                    down(pending)
                pending = (blk, tg, h, s.n)
        down(pending)

    wload(0)
    for b in range(NB):
        stats(b)
    for i, A in enumerate(ATT):
        attention(A)
        moe_capacity() if i == 0 else dense(i)
    return steps


def flamingo(nc, t, out):
    steps = plan()
    row_at, row_n = offsets(ROWS)
    col_at, col_n = offsets(COLS)
    cst_at, cst_n = offsets(CONST)

    with ExitStack() as ctx:
        def sb(name, shape, dt=F32):
            return ctx.enter_context(nc.sbuf_tensor(name, shape, dt))

        def pb(name, shape, dt=F32):
            return ctx.enter_context(nc.psum_tensor(name, shape, dt))

        def sem(name):
            return ctx.enter_context(nc.semaphore(name))

        def pair(name):
            return [sem(f"{name}{i}") for i in range(2)]

        x = sb("x", [P, NB, D])
        xn = sb("xn", [P, NB, D])
        ctx_s = sb("ctx_s", [P, NB, D])
        ctx_t = sb("ctx_t", [P, 2, NT])
        xn_t = sb("xn_t", [P, 2, NT])
        arena = sb("arena", [P, 17408])
        QP = arena[:, 0:6144].bitcast(BF16).rearrange("p (r n) -> p r n", r=3)
        KP = arena[:, 6144:14336].bitcast(BF16)
        VA = arena[:, 14336:17408].rearrange("p (r w e) -> p r w e", r=3, e=EW)
        VQ = arena[:, 14336:16384].bitcast(BF16).rearrange("p (w e) -> p w e", e=EW)
        Hb = arena[:, 0:8192].rearrange("p (r c n) -> p r c n", r=2, c=8)
        vf = arena[:, 0:2048].rearrange("p (m n) -> p m n", m=2)
        vr = arena[:, 2048:4096].rearrange("p (m n) -> p m n", m=2)
        vi = arena[:, 4096:5120].bitcast(BF16).rearrange("p (m n) -> p m n", m=2)
        w0 = sb("w0", [P, SLOTW])
        Wslot = [w0[:, :], arena[:, 8192:8192 + SLOTW]]
        Pt = sb("Pt", [P, 3, 1024])
        nb_t = sb("nb_t", [P, 2, 512])
        nb16 = nb_t[:, :, :].rearrange("p r n -> p (r n)").bitcast(BF16).rearrange("p (r n) -> p r n", r=2)
        sq = sb("sq", [P, 2, 3, 512], BF16)
        sk = sb("sk", [P, 2, 3, 512], BF16)
        qf = sb("qf", [P, 2, 512])
        kf = sb("kf", [P, 2, 512])
        rem = sb("rem", [P, 512])
        Oe = sb("Oe", [P, 2, 256])
        On = sb("On", [P, 2, 512])
        OnT = sb("OnT", [P, 2, 256])
        w_at0 = sb("w_at0", [P, 4, 128])
        w_at2 = sb("w_at2", [P, 4, 2, 256])
        wr = sb("wr", [P, 2, 28])
        rows = sb("rows", [P, row_n])
        cols = sb("cols", [P, col_n])
        cst = sb("cst", [P, cst_n])
        ident16 = sb("ident16", [P, P], BF16)
        mask_i = sb("mask_i", [P, NB], I32)
        att = sb("att", [P, NB])
        att_b = sb("att_b", [P, NB])
        tg = sb("tg", [P, 16])
        colx = sb("colx", [P, 4])
        st6 = sb("st6", [P, 6])
        mv = sb("mv", [P, NB, 2])
        vare = sb("vare", [P, NB])
        rstd = sb("rstd", [P, NB])
        mv2 = sb("mv2", [P, 2])
        vare2 = sb("vare2", [P, 1])
        rstd2 = sb("rstd2", [P, 1])
        mxp = sb("mxp", [P, 2, 64])
        nm = sb("nm", [P, 2, 32])
        npt = sb("npt", [P, 2, 2 * 3 * 16], BF16)
        nmT = sb("nmT", [48, 2, 256], BF16)
        rden = sb("rden", [P, 2, 4])
        tmp = sb("tmp", [P, 512])
        tmp2 = sb("tmp2", [P, 512])
        qs = sb("qs", [P, 3, 32])
        vs = sb("vs", [P, 3, 2])
        r8 = sb("r8", [P, 6, NB])
        idx = sb("idx", [P, 2, NB], I32)

        psS = pb("psS", [P, 2, 512])
        psT = pb("psT", [P, 2, 1024])
        psO = pb("psO", [P, 2, 256])
        psM = pb("psM", [P, 2, 256])

        lg, ra, rb, rc, oh, cm = [Pt[:, 2, 128 * i:128 * (i + 1)].rearrange("p (b e) -> p b e", b=NB)
                                  for i in range(6)]
        sg = Pt[:, 0:2, 0:512]
        xe = qf
        xeT = kf[:, :, 0:256].rearrange("p r (k n) -> p r k n", k=2)
        eo = Oe
        ge = On[:, :, 0:256]

        dq = [nc.dram_tensor(f"scr_q{i}", [3, 2 * P, 256], BF16).ap() for i in range(2)]
        dk = [nc.dram_tensor(f"scr_k{i}", [3, 2 * P, 256], BF16).ap() for i in range(2)]
        xd = nc.dram_tensor("scr_dispatched", [2 * NT, D], F32).ap()
        eod = nc.dram_tensor("scr_expert_out", [NT, D], F32).ap()

        def row(name):
            return rows[:, row_at[name][0]:row_at[name][1]]

        def col(name, j=0, n=P):
            return cols[0:n, col_at[name][0] + j:col_at[name][0] + j + 1]

        def const(name):
            return cst[:, cst_at[name][0]:cst_at[name][1]]

        x_in = sem("x_in")
        const_in = sem("const_in")
        w_in = pair("w_in")
        w3_in = sem("w3_in")
        var_ready = sem("var_ready")
        rstd_ready = sem("rstd_ready")
        xn_ready = sem("xn_ready")
        misc_ready, misc_used = pair("misc_ready"), pair("misc_used")
        S_ready, S_used = pair("S_ready"), pair("S_used")
        T_ready, T_used = pair("T_ready"), pair("T_used")
        O_used = pair("O_used")
        PV_done = sem("PV_done")
        parts_q = sem("parts_q")
        parts_k = sem("parts_k")
        V_copied = sem("V_copied")
        q_stored, k_stored = pair("q_stored"), pair("k_stored")
        q_packed, k_packed = pair("q_packed"), pair("k_packed")
        k_ones = sem("k_ones")
        neg_split = sem("neg_split")
        neg_in = pair("neg_in")
        exp_done = sem("exp_done")
        clipped = sem("clipped")
        rounded = sem("rounded")
        quant_q = sem("quant_q")
        v_quant = sem("v_quant")
        delta_var = sem("delta_var")
        delta_rstd = sem("delta_rstd")
        silu_done = sem("silu_done")
        gates_done = sem("gates_done")
        route_a = sem("route_a")
        route_b = sem("route_b")
        route_pe = sem("route_pe")
        routed = sem("routed")
        zero_in = sem("zero_in")
        zeros_made = sem("zeros_made")
        scattered = sem("scattered")
        xe_in = pair("xe_in")
        eo_out = pair("eo_out")
        gathered = pair("gathered")
        combined = sem("combined")
        out_done = sem("out_done")
        memset_done = sem("memset_done")
        dve_chain = sem("dve_chain")
        pool_chain = sem("pool_chain")

        N_CONST = 12

        def turn(eng, ready, n):
            eng.wait_ge(ready[n % 2], n // 2 + 1)

        def free(eng, used, n):
            if n >= 2:
                eng.wait_ge(used[n % 2], n // 2)

        def m_slot(n):
            return psM[:, n % 2, :]

        def kslot(A, u):
            return KP[:, :] if A.layer == 3 else KP[:, 4096 * (u.g % 3):4096 * (u.g % 3 + 1)]

        def wait_packs(pe, s, q_packed, k_packed):
            u = s.un
            pe.wait_ge(q_packed[u.q % 2], q_total(steps, u.q))
            if u.k is not None:
                pe.wait_ge(k_packed[u.k % 2], k_total(steps, u.k))
            elif u.u == 0:
                for k in last_ks(steps):
                    pe.wait_ge(k_packed[k % 2], k_total(steps, k))

        block = ctx.enter_context(nc.Block())

        @block.sync
        def _(sp):
            sp.dma_start(x[:, :, :], t["x"].rearrange("b p d -> p b d")).then_inc(x_in, 16)
            sp.dma_start(rows[:, :], t["rows"].partition_broadcast(P)).then_inc(const_in, 16)
            sp.dma_start(cols[:, :], t["cols"]).then_inc(const_in, 16)
            sp.dma_start(cst[:, :], t["cst"]).then_inc(const_in, 16)
            sp.dma_start(w_at0[:, :, :], t["w_at0"]).then_inc(const_in, 16)
            sp.dma_start(ctx_s[:, :, :], t["ctx"].rearrange("b p d -> p b d")).then_inc(const_in, 16)
            sp.dma_start(ident16[:, :], t["ident16"]).then_inc(const_in, 16)
            sp.dma_start(mask_i[:, :], t["mask"]).then_inc(const_in, 16)
            sp.dma_start(wr[:, :, :], t["wr"]).then_inc(const_in, 16)
            for kd in range(2):
                sp.dma_start(ctx_t[:, kd, :], t["ctx_t"][:, kd, :]).then_inc(const_in, 16)
            sp.dma_start(w_at2[:, :, :, :], t["w_at2"]).then_inc(w3_in, 16)
            sp.wait_ge(zeros_made, 1)
            for r in range(0, NT, P):
                sp.dma_start(xd[r:r + P, :], On[:, 0, 0:256]).then_inc(zero_in, 16)
            for s in steps:
                if s.kind == "barrier":
                    sp.wait_ge(rstd_ready, s.stats)
                elif s.kind == "attn_begin":
                    A = s.A
                    if A.layer == 3:
                        sp.dma_start(w_at2[:, :, :, :], t["w_at3"]).then_inc(w3_in, 16)
                    if A.has_max:
                        for r in range(4):
                            sp.dma_start(KP[6 * A.d:6 * A.d + 3, 4096 * r:4096 * (r + 1)],
                                         t["ones3"]).then_inc(k_ones, 16)
                elif s.kind == "wload":
                    i, slot = s.item, s.item % 2
                    if s.free is not None:
                        turn(sp, S_ready, s.free)
                    w = t[f"w{i}"]
                    sp.dma_start(Wslot[slot][:, 0:w.shape[1]], w).then_inc(w_in[slot], 16)
                elif s.kind in ("front", "kprep"):
                    A, gap = s.A, s.A.halves * s.A.T
                    if s.kind == "front":
                        i = s.q
                        sp.wait_ge(parts_q, i + 1)
                        if i >= 2:
                            sp.wait_ge(q_packed[i % 2], q_total(steps, i - 2))
                        for m in range(A.halves):
                            sp.dma_start(dq[i % 2][:, m * P:(m + 1) * P, 0:A.T].rearrange("c p n -> p c n"),
                                         sq[:, i % 2, :, m * A.T:(m + 1) * A.T]).then_inc(q_stored[i % 2], 16)
                    if s.k is not None:
                        j = s.k
                        sp.wait_ge(parts_k, j + 1)
                        if j >= 2:
                            sp.wait_ge(k_packed[j % 2], k_total(steps, j - 2))
                        for m in range(A.halves):
                            sp.dma_start(dk[j % 2][:, m * P:(m + 1) * P, 0:A.T].rearrange("c p n -> p c n"),
                                         sk[:, j % 2, :, m * A.T:(m + 1) * A.T]).then_inc(k_stored[j % 2], 16)
                    if s.kind == "front":
                        if s.done_before >= 0:
                            sp.wait_ge(PV_done, s.done_before + 1)
                        sp.wait_ge(q_stored[i % 2], stored_total(steps, "q", i))
                        for c, part in enumerate(FIRST_PARTS):
                            pack(sp, A, QP[:, s.g % 3, :], dq[i % 2], c, part, 0, A.T, q_packed[i % 2])
                    if s.k is not None:
                        sp.wait_ge(k_stored[j % 2], stored_total(steps, "k", j))
                        for c, part in enumerate(SECOND_PARTS):
                            if s.kind == "front":
                                pack(sp, A, KP[:, 4096 * (s.g % 3):4096 * (s.g % 3 + 1)], dk[j % 2], c, part,
                                     0, A.T, k_packed[j % 2])
                            else:
                                pack(sp, A, KP[:, :], dk[j % 2], c, part, s.u * A.T, NT, k_packed[j % 2])
                elif s.kind == "negmax":
                    A = s.A
                    turn(sp, misc_used, s.m)
                    for p3 in range(3):
                        r = 6 * A.d + p3
                        sp.dma_start(QP[r:r + 1, s.un.g % 3, 0:A.H * A.T],
                                     nmT[p3 * A.H:(p3 + 1) * A.H, s.i % 2, 0:A.T]).then_inc(neg_in[s.i % 2], 16)
                elif s.kind == "expert":
                    e = s.e
                    if e == 0:
                        sp.wait_ge(scattered, 16 * NB)
                    load_expert = [e, e + 1] if e == 0 else ([e + 1] if e + 1 < 8 else [])
                    for k in load_expert:
                        if k >= 2:
                            turn(sp, misc_ready, expert_m(steps, k - 2))
                        sp.dma_start(xe[:, k % 2, 0:256], xd[k * P:(k + 1) * P, :]).then_inc(xe_in[k % 2], 16)
                    turn(sp, S_used, s.s)
                    sp.dma_start(eod[e * P:(e + 1) * P, :], eo[:, e % 2, :]).then_inc(eo_out[e % 2], 16)
            sp.wait_ge(rstd_ready, last_stats(steps))
            sp.dma_start(out.rearrange("b p d -> p b d"), x[:, :, :]).then_inc(out_done, 16)
            sp.wait_ge(out_done, 16)

        @block.tensor
        def _(pe):
            ident = const("ident")

            def m_begin(n):
                if n >= 1:
                    turn(pe, misc_used, n - 1)
                return m_slot(n)

            def project(dst, lhs, rhs, halves):
                for kd in range(halves):
                    ins = pe.matmul(dst, lhsT=lhs(kd), rhs=rhs(kd), start=(kd == 0), stop=(kd == halves - 1))
                return ins

            def turn_x(n, xs):
                dst = m_begin(n)
                pe.wait_ge(xn_ready, xs.i + 1)
                for kd in range(2):
                    ins = pe.transpose(dst[:, kd * P:(kd + 1) * P], xn[:, xs.b, kd * P:(kd + 1) * P], ident)
                ins.then_inc(misc_ready[n % 2], 1)

            w_seen = set()

            def weights(item):
                if item not in w_seen:
                    w_seen.add(item)
                    pe.wait_ge(w_in[item % 2], 16 * (item // 2 + 1))

            pe.wait_ge(const_in, 16 * 10)
            for s in steps:
                if s.kind == "barrier":
                    pe.wait_ge(rstd_ready, s.stats)
                elif s.kind == "attn_begin":
                    if s.A.layer == 2:
                        pe.wait_ge(w3_in, 16)
                    if s.A.layer == 3:
                        pe.wait_ge(w3_in, 32)
                    if s.A.has_max:
                        seen = len([x for x in steps if x.kind == "attn_begin" and x.A.has_max and x.A.layer <= s.A.layer])
                        pe.wait_ge(k_ones, 64 * seen)
                elif s.kind == "kprep":
                    for j in range(2):
                        dst = m_begin(s.m[j])
                        tok = (2 * s.u + j) * P
                        project(dst, lambda kd: ctx_t[:, kd, tok:tok + P], lambda kd: w_at2[:, 1, kd, :], 2
                                ).then_inc(misc_ready[s.m[j] % 2], 1)
                    for m in range(2):
                        dst = m_begin(s.m[2 + m])
                        pe.wait_ge(quant_q, s.k_quant)
                        for j in range(2):
                            ins = pe.transpose(dst[:, j * P:(j + 1) * P], tmp2[:, j * 256 + m * P:j * 256 + (m + 1) * P], ident)
                        ins.then_inc(misc_ready[s.m[2 + m] % 2], 1)
                    for m in range(2):
                        dst = m_begin(s.m[4 + m])
                        tok = 2 * s.u * P
                        project(dst, lambda kd: w_at2[:, 2, kd, m * P:(m + 1) * P],
                                lambda kd: ctx_t[:, kd, tok:tok + 256], 2).then_inc(misc_ready[s.m[4 + m] % 2], 1)
                elif s.kind == "vturn":
                    dst = m_begin(s.m).bitcast(BF16)
                    pe.wait_ge(v_quant, 1)
                    for m in range(2):
                        ins = pe.transpose(dst[:, m * P:(m + 1) * P], vi[:, m, s.c * P:(s.c + 1) * P], ident16[:, :])
                    ins.then_inc(misc_ready[s.m % 2], 1)
                elif s.kind == "front":
                    A, b = s.A, s.u
                    if A.layer == 0:
                        pe.wait_ge(xn_ready, s.xn[0].i + 1)
                        for k, src in ((0, xn), (1, ctx_s)):
                            dst = m_begin(s.m[k])
                            pe.matmul(dst, lhsT=w_at0[:, k, :], rhs=src[:, b, :], start=True, stop=True
                                      ).then_inc(misc_ready[s.m[k] % 2], 1)
                        dst = m_begin(s.m[2])
                        for c in range(2):
                            ins = pe.matmul(dst[:, c * P:(c + 1) * P], lhsT=ctx_s[:, b, c * P:(c + 1) * P],
                                            rhs=w_at0[:, 2, :], start=True, stop=True)
                        ins.then_inc(misc_ready[s.m[2] % 2], 1)
                    elif A.layer == 2:
                        turn_x(s.m[0], s.xn[0])
                        tok = b * P
                        for k, src in ((1, xn_t), (2, ctx_t)):
                            dst = m_begin(s.m[k])
                            if k == 1:
                                turn(pe, misc_used, s.m[0])
                            for m in range(2):
                                ins = project(dst[:, m * P:(m + 1) * P], lambda kd: w_at2[:, k - 1, kd, m * P:(m + 1) * P],
                                              lambda kd: src[:, kd, tok:tok + P], 2)
                            ins.then_inc(misc_ready[s.m[k] % 2], 1)
                        dst = m_begin(s.m[3])
                        project(dst, lambda kd: ctx_t[:, kd, tok:tok + P], lambda kd: w_at2[:, 2, kd, :], 2
                                ).then_inc(misc_ready[s.m[3] % 2], 1)
                    elif A.layer == 3:
                        for j in range(2):
                            turn_x(s.m[j], s.xn[j])
                        for j in range(2):
                            dst = m_begin(s.m[2 + j])
                            turn(pe, misc_used, s.m[j])
                            tok = (2 * s.u + j) * P
                            project(dst, lambda kd: xn_t[:, kd, tok:tok + P], lambda kd: w_at2[:, 0, kd, :], 2
                                    ).then_inc(misc_ready[s.m[2 + j] % 2], 1)
                        for m in range(2):
                            dst = m_begin(s.m[4 + m])
                            pe.wait_ge(quant_q, s.q_quant)
                            for j in range(2):
                                ins = pe.transpose(dst[:, j * P:(j + 1) * P],
                                                   tmp2[:, j * 256 + m * P:j * 256 + (m + 1) * P], ident)
                            ins.then_inc(misc_ready[s.m[4 + m] % 2], 1)
                elif s.kind == "smax":
                    A, u, K = s.A, s.un, 6 * s.A.d
                    if s.first:
                        wait_packs(pe, s, q_packed, k_packed)
                    free(pe, S_used, s.n)
                    dst = psS[:, s.n % 2, :]
                    q_at, k_at = QP[0:K, u.g % 3, :], kslot(A, u)[0:K, :]
                    if A.layer == 3:
                        h, half = s.j // 2, s.j % 2
                        ins = pe.matmul(dst, lhsT=q_at[:, h * A.T + s.tc * P:h * A.T + (s.tc + 1) * P],
                                        rhs=k_at[:, h * NT + half * 512:h * NT + (half + 1) * 512],
                                        start=True, stop=True)
                    else:
                        for i in range(2):
                            h = 2 * s.j + i
                            ins = pe.matmul(dst[:, i * 256:(i + 1) * 256],
                                            lhsT=q_at[:, h * A.T + s.tc * P:h * A.T + (s.tc + 1) * P],
                                            rhs=k_at[:, h * A.T:(h + 1) * A.T], start=True, stop=True)
                    ins.then_inc(S_ready[s.n % 2], 1)
                elif s.kind == "negmax":
                    A = s.A
                    dst = m_begin(s.m).bitcast(BF16)
                    pe.wait_ge(neg_split, s.i + 1)
                    w = 3 * A.H
                    for tc in range(A.TC):
                        ins = pe.transpose(dst[0:w, tc * P:(tc + 1) * P], npt[:, s.i % 2, tc * w:(tc + 1) * w],
                                           ident16[:, :])
                    ins.then_inc(misc_ready[s.m % 2], 1)
                elif s.kind == "st":
                    A, u = s.A, s.un
                    K = 6 * A.d + (3 if A.has_max else 0)
                    if s.first:
                        if A.has_max:
                            pe.wait_ge(neg_in[u.neg % 2], 48 * (u.neg // 2 + 1))
                        else:
                            wait_packs(pe, s, q_packed, k_packed)
                    free(pe, T_used, s.n)
                    q_at, k_at = QP[0:K, u.g % 3, :], kslot(A, u)[0:K, :]
                    kw = NT if A.layer == 3 else A.T if A.layer < 2 else P
                    for i in range(4):
                        h = 4 * s.g + i
                        ins = pe.matmul(psT[:, s.n % 2, i * A.T:(i + 1) * A.T],
                                        lhsT=k_at[:, h * kw + s.c * P:h * kw + (s.c + 1) * P],
                                        rhs=q_at[:, h * A.T:(h + 1) * A.T], start=True, stop=True)
                    ins.then_inc(T_ready[s.n % 2], 1)
                elif s.kind == "pv":
                    A, u = s.A, s.un
                    if A.layer == 2:
                        pe.wait_ge(exp_done, s.clip + 1)
                    else:
                        turn(pe, T_used, s.n)
                    if A.layer == 3:
                        pe.wait_ge(rounded, s.clip3 + 1)
                    if s.g == 0 and s.c == 0:
                        if A.layer == 0:
                            turn(pe, misc_used, u.m[2])
                        elif A.layer == 1:
                            pe.wait_ge(V_copied, u.u + 1)
                        elif A.layer == 2:
                            turn(pe, misc_used, u.m[3])
                        else:
                            for m in last_vturns(steps):
                                turn(pe, misc_used, m)
                    if s.c == 0 and s.o >= 1:
                        turn(pe, O_used, s.o - 1)
                    for i in range(4):
                        h = 4 * s.g + i
                        dst = psO[32 * i:32 * (i + 1), s.o % 2, 0:A.T]
                        pr = Pt[:, s.p % 3, i * A.T:(i + 1) * A.T]
                        first, last = s.c == 0, s.c == A.NC - 1
                        if A.layer < 3:
                            ins = pe.matmul(dst, lhsT=VA[:, u.g % 3, s.c * A.H + h, :], rhs=pr, start=first, stop=last)
                        else:
                            pe.matmul(dst, lhsT=VQ[:, s.c * A.H + h, :], rhs=nb16[:, s.p % 2, i * A.T:(i + 1) * A.T],
                                      start=first, stop=False)
                    if A.layer == 3:
                        for i in range(4):
                            dst = psO[32 * i:32 * (i + 1), s.o % 2, 0:A.T]
                            pr = Pt[:, s.p % 3, i * A.T:(i + 1) * A.T]
                            ins = pe.matmul(dst, lhsT=const("sumsel"), rhs=pr, start=False, stop=last)
                    ins.then_inc(PV_done, 1)
                elif s.kind == "onorm":
                    A = s.A
                    turn(pe, O_used, s.o)
                    dst = m_begin(s.m)
                    for tc in range(A.TC):
                        ins = pe.transpose(dst[:, tc * P:(tc + 1) * P], Oe[:, s.o % 2, tc * P:(tc + 1) * P], ident)
                    ins.then_inc(misc_ready[s.m % 2], 1)
                elif s.kind == "out":
                    A, u = s.A, s.un
                    HD = A.H * A.d
                    ms = s.m if A.layer != 1 else [s.m]
                    turn(pe, misc_used, s.m_last_norm)
                    if A.layer in (0, 1):
                        dst = m_begin(ms[0])
                        for tc in range(2):
                            ins = pe.transpose(dst[:, tc * P:(tc + 1) * P], On[:, u.g % 2, tc * HD:(tc + 1) * HD], ident)
                        ins.then_inc(misc_ready[ms[0] % 2], 1)
                    elif A.layer == 2:
                        dst = m_begin(ms[0])
                        for m in range(2):
                            ins = pe.transpose(dst[:, m * P:(m + 1) * P], On[:, u.g % 2, m * P:(m + 1) * P], ident)
                        ins.then_inc(misc_ready[ms[0] % 2], 1)
                    else:
                        for m in range(2):
                            dst = m_begin(ms[m])
                            for tc in range(2):
                                ins = pe.transpose(dst[:, tc * P:(tc + 1) * P],
                                                   On[:, tc, m * P:(m + 1) * P], ident)
                            ins.then_inc(misc_ready[ms[m] % 2], 1)
                    if A.layer == 0:
                        dst = m_begin(ms[1])
                        turn(pe, misc_used, ms[0])
                        pe.matmul(dst, lhsT=w_at0[:, 3, :], rhs=OnT[:, 0, :], start=True, stop=True
                                  ).then_inc(misc_ready[ms[1] % 2], 1)
                    elif A.layer == 2:
                        dst = m_begin(ms[1])
                        turn(pe, misc_used, ms[0])
                        ont = OnT[:, 0, :]
                        project(dst, lambda m: ont[:, m * P:(m + 1) * P], lambda m: w_at2[:, 3, m, :], 2
                                ).then_inc(misc_ready[ms[1] % 2], 1)
                    elif A.layer == 3:
                        for j in range(2):
                            dst = m_begin(ms[2 + j])
                            for m in range(2):
                                turn(pe, misc_used, ms[m])
                            project(dst, lambda m: OnT[:, m, j * P:(j + 1) * P], lambda m: w_at2[:, 3, m, :], 2
                                    ).then_inc(misc_ready[ms[2 + j] % 2], 1)
                elif s.kind == "xt":
                    turn_x(s.m, s.xn)
                    if s.lm is not None:
                        dst = m_begin(s.lm)
                        turn(pe, misc_used, s.m)
                        a, n = {0: (0, 8), 2: (8, 16), 3: (24, 4)}[s.layer]
                        tok = s.xn.b * P
                        project(dst[:, 0:n], lambda kd: xn_t[:, kd, tok:tok + P], lambda kd: wr[:, kd, a:a + n], 2
                                ).then_inc(misc_ready[s.lm % 2], 1)
                elif s.kind == "route" and s.layer == 0:
                    dst = m_begin(s.m)
                    pe.wait_ge(route_pe, 1)
                    pe.matmul(dst[:, 0:64], lhsT=const("before"), rhs=oh[:, :, 0:8], start=True, stop=False)
                    pe.matmul(dst[:, 0:64], lhsT=const("ones"), rhs=rc[:, :, 0:8], start=False, stop=True
                              ).then_inc(misc_ready[s.m % 2], 1)
                elif s.kind == "expert":
                    e = s.e
                    dst = m_begin(s.m)
                    pe.wait_ge(xe_in[e % 2], 16 * (e // 2 + 1))
                    for kd in range(2):
                        ins = pe.transpose(dst[:, kd * P:(kd + 1) * P], xe[:, e % 2, kd * P:(kd + 1) * P], ident)
                    ins.then_inc(misc_ready[s.m % 2], 1)
                    W = Wslot[e % 2]
                    weights(e)
                    free(pe, T_used, s.n)
                    turn(pe, misc_used, s.m)
                    for ch in range(8):
                        ins = project(psT[:, s.n % 2, ch * P:(ch + 1) * P],
                                      lambda kd: W[:, kd * 1024 + ch * P:kd * 1024 + (ch + 1) * P],
                                      lambda kd: xeT[:, e % 2, kd, :], 2)
                    ins.then_inc(T_ready[s.n % 2], 1)
                    free(pe, S_used, s.s)
                    turn(pe, T_used, s.n)
                    for ch in range(8):
                        ins = pe.matmul(psS[:, s.s % 2, 0:256], lhsT=Pt[:, e % 2, ch * P:(ch + 1) * P],
                                        rhs=W[:, 2048 + ch * 256:2048 + (ch + 1) * 256], start=(ch == 0), stop=(ch == 7))
                    ins.then_inc(S_ready[s.s % 2], 1)
                elif s.kind == "gu":
                    W, F, ch, w = Wslot[s.blk.item % 2], s.blk.F, s.ch, s.width
                    weights(s.blk.item)
                    if s.ch == 0:
                        for m in xt_slots(steps, s.layer):
                            turn(pe, misc_used, m)
                    free(pe, T_used, s.n)
                    for k in range(2):
                        at = s.blk.off + k * 2 * F + ch * P
                        ins = project(psT[0:w, s.n % 2, k * 512:(k + 1) * 512],
                                      lambda kd: W[:, at + kd * F:at + kd * F + w],
                                      lambda kd: xn_t[:, kd, s.tg * 512:(s.tg + 1) * 512], 2)
                    ins.then_inc(T_ready[s.n % 2], 1)
                elif s.kind == "down":
                    W, off = Wslot[s.blk.item % 2], s.blk.off + 4 * s.blk.F
                    free(pe, S_used, s.n)
                    if s.tc == 0:
                        turn(pe, T_used, s.last_T)
                        if s.last_T >= 1:
                            turn(pe, T_used, s.last_T - 1)
                    last = len(s.blk.widths) - 1
                    for ch, w in enumerate(s.blk.widths):
                        ins = pe.matmul(psS[:, s.n % 2, 0:256], lhsT=Hb[0:w, s.h % 2, ch, s.tc * P:(s.tc + 1) * P],
                                        rhs=W[0:w, off + ch * 256:off + (ch + 1) * 256], start=(ch == 0), stop=(ch == last))
                    ins.then_inc(S_ready[s.n % 2], 1)

        @block.scalar
        def _(act):
            act.wait_ge(const_in, 16 * 10)
            act.activation(tg[:, 0:8], rows[:, 0:8], ACT.Tanh).then_inc(gates_done, 1)
            act.wait_ge(gates_done, 4)
            for s in steps:
                if s.kind == "barrier":
                    act.wait_ge(rstd_ready, s.stats)
                elif s.kind == "kprep":
                    if s.k >= 2:
                        act.wait_ge(parts_k, s.k - 1)
                    for m in range(2):
                        turn(act, misc_ready, s.m[2 + m])
                        act.activation(kf[:, s.k % 2, m * 256:(m + 1) * 256], m_slot(s.m[2 + m]), ACT.Copy
                                       ).then_inc(misc_used[s.m[2 + m] % 2], 1)
                    for m in range(2):
                        turn(act, misc_ready, s.m[4 + m])
                        act.activation(vf[:, m, s.u * 256:(s.u + 1) * 256], m_slot(s.m[4 + m]), ACT.Identity,
                                       bias=col("bv3", m)).then_inc(misc_used[s.m[4 + m] % 2], 1)
                elif s.kind == "front":
                    A, b = s.A, s.u
                    if A.layer == 0:
                        if s.q >= 2:
                            act.wait_ge(parts_q, s.q - 1)
                            act.wait_ge(parts_k, s.k - 1)
                        turn(act, misc_ready, s.m[0])
                        act.activation(qf[:, s.q % 2, 0:256], m_slot(s.m[0]), ACT.Identity, bias=colx[:, 0:1],
                                       scale=float(A.d) ** -0.5).then_inc(misc_used[s.m[0] % 2], 1)
                        turn(act, misc_ready, s.m[1])
                        act.activation(kf[:, s.k % 2, 0:256], m_slot(s.m[1]), ACT.Identity, bias=col("bk0")
                                       ).then_inc(misc_used[s.m[1] % 2], 1)
                    elif A.layer == 2:
                        turn(act, misc_ready, s.m[0])
                        act.activation(xn_t[:, :, b * P:(b + 1) * P],
                                       m_slot(s.m[0]).rearrange("p (k n) -> p k n", k=2), ACT.Copy
                                       ).then_inc(misc_used[s.m[0] % 2], 1)
                        act.wait_ge(parts_q, s.q - 1)
                        act.wait_ge(parts_k, s.k - 1)
                        for k, dst in ((1, qf), (2, kf)):
                            turn(act, misc_ready, s.m[k])
                            i = (s.q if k == 1 else s.k) % 2
                            for m in range(2):
                                ins = act.activation(dst[:, i, m * P:(m + 1) * P], m_slot(s.m[k])[:, m * P:(m + 1) * P],
                                                     ACT.Identity, bias=colx[:, 1 + m:2 + m] if k == 1 else col("bk2", m),
                                                     scale=float(A.d) ** -0.5 if k == 1 else 1.0)
                            ins.then_inc(misc_used[s.m[k] % 2], 1)
                    elif A.layer == 3:
                        for j in range(2):
                            turn(act, misc_ready, s.m[j])
                            bb = 2 * s.u + j
                            act.activation(xn_t[:, :, bb * P:(bb + 1) * P],
                                           m_slot(s.m[j]).rearrange("p (k n) -> p k n", k=2), ACT.Copy
                                           ).then_inc(misc_used[s.m[j] % 2], 1)
                        act.wait_ge(parts_q, s.q - 1)
                        for m in range(2):
                            turn(act, misc_ready, s.m[4 + m])
                            act.activation(qf[:, s.q % 2, m * 256:(m + 1) * 256], m_slot(s.m[4 + m]), ACT.Copy
                                           ).then_inc(misc_used[s.m[4 + m] % 2], 1)
                elif s.kind == "negmax":
                    A = s.A
                    turn(act, misc_ready, s.m)
                    if s.i >= 2:
                        act.wait_ge(neg_in[s.i % 2], 48 * (s.i // 2))
                    act.activation(nmT[0:3 * A.H, s.i % 2, 0:A.T], m_slot(s.m).bitcast(BF16)[0:3 * A.H, 0:A.T],
                                   ACT.Copy).then_inc(misc_used[s.m % 2], 1)
                elif s.kind == "st":
                    A = s.A
                    if s.p >= 3:
                        act.wait_ge(PV_done, s.p - 2)
                    if A.layer == 2:
                        b = s.un.u
                        act.wait_ge(clipped, s.clip + 1)
                        act.activation(Pt[:, s.p % 3, 0:512], nb_t[:, s.clip % 2, :], ACT.Exp,
                                       bias=att_b[:, b:b + 1], scale=att[:, b:b + 1]).then_inc(exp_done, 1)
                    else:
                        turn(act, T_ready, s.n)
                        act.activation(Pt[:, s.p % 3, :], psT[:, s.n % 2, :], ACT.Exp).then_inc(T_used[s.n % 2], 1)
                elif s.kind == "onorm":
                    A = s.A
                    act.wait_ge(PV_done, s.p + 1)
                    if s.m_prev2 is not None:
                        turn(act, misc_ready, s.m_prev2)
                    act.activation(Oe[:, s.o % 2, 0:A.T], psO[:, s.o % 2, 0:A.T], ACT.Copy).then_inc(O_used[s.o % 2], 1)
                elif s.kind == "out":
                    A = s.A
                    if A.layer in (0, 2):
                        turn(act, misc_ready, s.m[0])
                        if s.m_prev is not None:
                            turn(act, misc_ready, s.m_prev[-1])
                        act.activation(OnT[:, 0, :], m_slot(s.m[0]), ACT.Copy).then_inc(misc_used[s.m[0] % 2], 1)
                    elif A.layer == 3:
                        for m in range(2):
                            turn(act, misc_ready, s.m[m])
                            if m == 0 and s.m_prev is not None:
                                turn(act, misc_ready, s.m_prev[-1])
                            act.activation(OnT[:, m, :], m_slot(s.m[m]), ACT.Copy, scale=vs[:, 0, m:m + 1]
                                           ).then_inc(misc_used[s.m[m] % 2], 1)
                elif s.kind == "xt":
                    b = s.xn.b
                    turn(act, misc_ready, s.m)
                    act.activation(xn_t[:, :, b * P:(b + 1) * P], m_slot(s.m).rearrange("p (k n) -> p k n", k=2),
                                   ACT.Copy).then_inc(misc_used[s.m % 2], 1)
                elif s.kind == "route":
                    act.wait_ge(route_a, s.exp_i + 1)
                    n = {0: 8, 2: 16, 3: 4}[s.layer]
                    act.activation(ra[:, :, 0:n], ra[:, :, 0:n], ACT.Exp, scale=-1.0 if s.layer == 2 else 1.0
                                   ).then_inc(route_b, 1)
                elif s.kind == "expert":
                    e = s.e
                    turn(act, misc_ready, s.m)
                    act.activation(xeT[:, e % 2, :, :], m_slot(s.m).rearrange("p (k n) -> p k n", k=2), ACT.Copy
                                   ).then_inc(misc_used[s.m % 2], 1)
                    turn(act, T_ready, s.n)
                    act.activation(Pt[:, e % 2, :], psT[:, s.n % 2, :], ACT.Gelu_apprx_tanh).then_inc(T_used[s.n % 2], 1)
                elif s.kind == "gu":
                    w = s.width
                    turn(act, T_ready, s.n)
                    sc = col("gs1", s.ch, w) if s.layer == 1 else 1.0
                    act.activation(sg[0:w, s.sg % 2, :], psT[0:w, s.n % 2, 0:512], ACT.Silu, scale=sc
                                   ).then_inc(silu_done, 1)

        @block.vector
        def _(dve):
            chained = [0]

            def link(ins):
                chained[0] += 1
                ins.then_inc(dve_chain, 1)
                dve.wait_ge(dve_chain, chained[0])

            def normalise(xs):
                dve.wait_ge(rstd_ready, xs.stat + 1)
                dve.tensor_scalar(xn[:, xs.b, :], x[:, xs.b, :], mv[:, xs.b, 0:1], rstd[:, xs.b:xs.b + 1],
                                  ALU.subtract, ALU.mult).then_inc(xn_ready, 1)

            def bc(ap, shape):
                return ap.to_broadcast(shape)

            def quantise(src, dst, H, n):
                s4 = src.rearrange("p (j d h) -> p j h d", j=n, h=H)
                scale = qs[:, 0, 0:n * H].rearrange("p (j h) -> p j h", j=n)
                link(dve.tensor_reduce(scale, s4, AX.X, ALU.max, apply_absolute_value=True))
                link(dve.tensor_scalar(qs[:, 1, 0:n * H], qs[:, 0, 0:n * H], 1.0 / 127.0, 1e-8, ALU.mult, ALU.max))
                link(dve.reciprocal(qs[:, 2, 0:n * H], qs[:, 1, 0:n * H]))
                for j in range(n):
                    v = src[:, j * 256:(j + 1) * 256].rearrange("p (d h) -> p d h", h=H)
                    o = dst[:, j * 256:(j + 1) * 256].rearrange("p (d h) -> p d h", h=H)
                    r = qs[:, 2, j * H:(j + 1) * H].rearrange("p (o h) -> p o h", o=1)
                    ins = dve.tensor_tensor(o, v, r.to_broadcast([P, 16, H]), ALU.mult)
                link(ins)
                link(dve.tensor_scalar(dst, dst, MAGIC, MAGIC, ALU.add, ALU.subtract))
                for j in range(n):
                    o = dst[:, j * 256:(j + 1) * 256].rearrange("p (d h) -> p d h", h=H)
                    r = qs[:, 1, j * H:(j + 1) * H].rearrange("p (o h) -> p o h", o=1)
                    ins = dve.tensor_tensor(o, o, r.to_broadcast([P, 16, H]), ALU.mult)
                ins.then_inc(quant_q, 1)

            def first_max(src, E, onehot):
                link(dve.tensor_reduce(r8[:, 0, :], src, AX.X, ALU.max))
                mx = r8[:, 0, :].unsqueeze(2).to_broadcast([P, NB, E])
                link(dve.tensor_tensor(rb[:, :, 0:E], src, mx, ALU.is_equal))
                desc = const("desc")[:, 0:E].unsqueeze(1).to_broadcast([P, NB, E])
                link(dve.tensor_tensor(rb[:, :, 0:E], rb[:, :, 0:E], desc, ALU.mult))
                link(dve.tensor_reduce(r8[:, 1, :], rb[:, :, 0:E], AX.X, ALU.max))
                m2 = r8[:, 1, :].unsqueeze(2).to_broadcast([P, NB, E])
                link(dve.tensor_tensor(onehot, rb[:, :, 0:E], m2, ALU.is_equal))

            link(dve.memset(On[:, :, :], 0.0))
            dve.memset(rem[:, 0:1], 0.0).then_inc(zeros_made, 1)
            link(dve.memset(VA[:, :, :, :], 0.0))
            dve.memset(VA[:, :, :, SUMCOL:SUMCOL + 1], 1.0).then_inc(memset_done, 1)
            dve.wait_ge(memset_done, 1)
            dve.wait_ge(const_in, 16 * 10)
            dve.tensor_scalar(colx[:, 0:1], col("bq0"), float(ATT[0].d) ** -0.5, None, ALU.mult).then_inc(gates_done, 1)
            dve.tensor_scalar(colx[:, 1:3], cols[:, col_at["bq2"][0]:col_at["bq2"][1]], float(ATT[2].d) ** -0.5, None,
                              ALU.mult).then_inc(gates_done, 1)
            dve.tensor_scalar(att[:, :], mask_i[:, :], 0.5, None, ALU.is_gt).then_inc(gates_done, 1)
            dve.wait_ge(gates_done, 4)
            link(dve.tensor_scalar(att_b[:, :], att[:, :], 50.0, -50.0, ALU.mult, ALU.add))
            link(dve.tensor_scalar(tg[:, 8:9], row("gamma"), tg[:, 1:2], None, ALU.mult))
            link(dve.tensor_scalar(tg[:, 9:10], row("rscale"), 0.0, 0.3, ALU.max, ALU.min))
            link(dve.tensor_scalar(tg[:, 10:11], tg[:, 6:7], 0.1, None, ALU.mult))
            dve.wait_ge(x_in, 16)
            for s in steps:
                if s.kind == "barrier":
                    dve.wait_ge(rstd_ready, s.stats)
                elif s.kind == "stats":
                    b = s.b
                    if s.after is not None:
                        for i in range(2):
                            if s.after[i]:
                                dve.wait_ge(S_used[i], s.after[i])
                    link(dve.bn_stats(st6[:, :], x[:, b, :]))
                    link(dve.bn_aggr(mv[:, b, :], st6[:, :]))
                    dve.tensor_scalar(vare[:, b:b + 1], mv[:, b, 1:2], EPS, None, ALU.add).then_inc(var_ready, 1)
                elif s.kind == "attn_begin" and s.A.layer == 3:
                    link(dve.memset(VQ[:, :, :], 0.0))
                elif s.kind == "kprep":
                    if s.u >= 1:
                        for m in s.prev_m:
                            turn(dve, misc_ready, m)
                    for j in range(2):
                        turn(dve, misc_ready, s.m[j])
                        ins = dve.tensor_tensor(tmp[:, j * 256:(j + 1) * 256], m_slot(s.m[j]), row("bk3"), ALU.add)
                        ins.then_inc(misc_used[s.m[j] % 2], 1)
                    for j in range(2):
                        turn(dve, misc_used, s.m[j])
                    quantise(tmp[:, 0:512], tmp2[:, 0:512], 16, 2)
                elif s.kind == "vscale":
                    for m in (s.last_m, s.last_m - 1):
                        turn(dve, misc_used, m)
                    link(dve.tensor_reduce(vs[:, 2, :], vf[:, :, :], AX.X, ALU.max, apply_absolute_value=True))
                    link(dve.tensor_scalar(vs[:, 0, :], vs[:, 2, :], 1.0 / 127.0, 1e-8, ALU.mult, ALU.max))
                    link(dve.reciprocal(vs[:, 1, :], vs[:, 0, :]))
                    for m in range(2):
                        ins = dve.tensor_scalar(vr[:, m, :], vf[:, m, :], vs[:, 1, m:m + 1], MAGIC, ALU.mult, ALU.add)
                    link(ins)
                    dve.tensor_scalar(vi[:, :, :], vr[:, :, :], MAGIC, None, ALU.subtract).then_inc(v_quant, 1)
                elif s.kind == "vturn":
                    turn(dve, misc_ready, s.m)
                    src = m_slot(s.m).bitcast(BF16)[:, 0:256].rearrange("p (h d) -> p h d", d=16)
                    dve.tensor_copy(VQ[:, s.c * 16:(s.c + 1) * 16, 0:16], src).then_inc(misc_used[s.m % 2], 1)
                elif s.kind == "front":
                    A = s.A
                    for xs in s.xn:
                        normalise(xs)
                    if A.layer in (0, 2):
                        n = s.m[2] if A.layer == 0 else s.m[3]
                        turn(dve, misc_ready, n)
                        if s.done_before >= 0:
                            dve.wait_ge(PV_done, s.done_before + 1)
                        if A.layer == 0:
                            for c in range(2):
                                ins = dve.tensor_tensor(VA[:, s.g % 3, c * 16:(c + 1) * 16, 0:8],
                                                        m_slot(n)[:, c * P:(c + 1) * P].rearrange("p (h d) -> p h d", d=8),
                                                        row("bv0").rearrange("p (h d) -> p h d", d=8), ALU.add)
                        else:
                            ins = dve.tensor_tensor(VA[:, s.g % 3, 0:16, 0:16],
                                                    m_slot(n).rearrange("p (h d) -> p h d", d=16),
                                                    row("bv2").rearrange("p (h d) -> p h d", d=16), ALU.add)
                        ins.then_inc(misc_used[n % 2], 1)
                    elif A.layer == 3:
                        for m in s.prev_m:
                            turn(dve, misc_ready, m)
                        for j in range(2):
                            turn(dve, misc_ready, s.m[2 + j])
                            dve.tensor_tensor(tmp[:, j * 256:(j + 1) * 256], m_slot(s.m[2 + j]), row("bq3"), ALU.add
                                              ).then_inc(misc_used[s.m[2 + j] % 2], 1)
                        for j in range(2):
                            turn(dve, misc_used, s.m[2 + j])
                        link(dve.tensor_scalar(tmp[:, 0:512], tmp[:, 0:512], 0.25, None, ALU.mult))
                        quantise(tmp[:, 0:512], tmp2[:, 0:512], 16, 2)
                elif s.kind == "smax":
                    A = s.A
                    turn(dve, S_ready, s.n)
                    if A.layer == 3:
                        at = s.tc * 32 + s.j
                        dve.tensor_reduce(mxp[:, s.un.g % 2, at:at + 1], psS[:, s.n % 2, :], AX.X, ALU.max
                                          ).then_inc(S_used[s.n % 2], 1)
                    else:
                        at = s.tc * A.H + 2 * s.j
                        dve.tensor_reduce(mxp[:, s.un.g % 2, at:at + 2],
                                          psS[:, s.n % 2, :].rearrange("p (h n) -> p h n", h=2), AX.X, ALU.max
                                          ).then_inc(S_used[s.n % 2], 1)
                elif s.kind == "negmax":
                    A, w = s.A, s.A.TC * s.A.H
                    for k in (s.un.last_S, s.un.last_S - 1):
                        turn(dve, S_used, k)
                    mx = mxp[:, s.un.g % 2, 0:w]
                    if A.layer == 3:
                        link(dve.tensor_reduce(nm[:, 1, 0:w], mxp[:, s.un.g % 2, :].rearrange("p (h n) -> p h n", n=2),
                                               AX.X, ALU.max))
                        mx = nm[:, 1, 0:w]
                    link(dve.tensor_scalar(nm[:, 0, 0:w], mx, -1.0, LN255 if A.layer == 3 else 0.0, ALU.mult, ALU.add))
                    if s.m_prev2 is not None:
                        turn(dve, misc_ready, s.m_prev2)
                    part = npt[:, s.i % 2, 0:3 * w].rearrange("p (t c h) -> p c t h", t=A.TC, c=3)
                    src = nm[:, 0, 0:w].rearrange("p (t h) -> p t h", t=A.TC)
                    left = nm[:, 1, 0:w].rearrange("p (t h) -> p t h", t=A.TC)
                    link(dve.tensor_copy(part[:, 0], src))
                    link(dve.tensor_tensor(left, src, part[:, 0], ALU.subtract))
                    link(dve.tensor_copy(part[:, 1], left))
                    dve.tensor_tensor(part[:, 2], left, part[:, 1], ALU.subtract).then_inc(neg_split, 1)
                elif s.kind == "st" and s.A.layer == 2:
                    turn(dve, T_ready, s.n)
                    if s.clip >= 2:
                        dve.wait_ge(exp_done, s.clip - 1)
                    dve.tensor_scalar(nb_t[:, s.clip % 2, :], psT[:, s.n % 2, 0:512], 50.0, -50.0, ALU.min, ALU.max
                                      ).then_inc(T_used[s.n % 2], 1)
                    turn(dve, T_used, s.n)
                    dve.sem_inc(clipped, 1)
                elif s.kind == "st" and s.A.layer == 3:
                    turn(dve, T_used, s.n)
                    if s.p >= 2:
                        dve.wait_ge(PV_done, s.p - 1)
                    dve.tensor_scalar(nb16[:, s.p % 2, :], Pt[:, s.p % 3, :], MAGIC, MAGIC, ALU.add, ALU.subtract
                                      ).then_inc(rounded, 1)
                elif s.kind == "onorm":
                    A = s.A
                    turn(dve, misc_ready, s.m)
                    src = m_slot(s.m)[:, 0:A.T].rearrange("p (t h e) -> p t h e", t=A.TC, h=4)
                    link(dve.reciprocal(rden[:, 0:A.TC, :].unsqueeze(3), src[:, :, :, SUMCOL:SUMCOL + 1]))
                    for tc in range(A.TC):
                        HD = A.H * A.d
                        if A.layer == 3:
                            dst = On[:, tc, s.g * 4 * A.d:(s.g + 1) * 4 * A.d]
                        else:
                            dst = On[:, s.un.g % 2, tc * HD + s.g * 4 * A.d:tc * HD + (s.g + 1) * 4 * A.d]
                        if s.g == 0 and tc == 0 and s.prev_turned is not None:
                            for m in s.prev_turned:
                                turn(dve, misc_ready, m)
                        ins = dve.tensor_tensor(dst.rearrange("p (h d) -> p h d", h=4), src[:, tc, :, 0:A.d],
                                                rden[:, tc, :].unsqueeze(2).to_broadcast([P, 4, A.d]), ALU.mult)
                    ins.then_inc(misc_used[s.m % 2], 1)
                elif s.kind == "out":
                    A, u = s.A, s.un
                    if A.layer == 0:
                        turn(dve, misc_ready, s.m[1])
                        dve.tensor_scalar(tmp[:, 0:256], m_slot(s.m[1]), col("bo0"), tg[:, 0:1], ALU.add, ALU.mult
                                          ).then_inc(misc_used[s.m[1] % 2], 1)
                        turn(dve, misc_used, s.m[1])
                        link(dve.tensor_tensor(x[:, u.u, :], x[:, u.u, :], tmp[:, 0:256], ALU.add))
                    elif A.layer == 1:
                        turn(dve, misc_ready, s.m)
                        dve.scalar_tensor_tensor(out=x[:, u.u, :], in0=m_slot(s.m), scalar=tg[:, 8:9],
                                                 in1=x[:, u.u, :], op0=ALU.mult, op1=ALU.add
                                                 ).then_inc(misc_used[s.m % 2], 1)
                        turn(dve, misc_used, s.m)
                    elif A.layer == 2:
                        turn(dve, misc_ready, s.m[1])
                        dve.tensor_tensor(tmp[:, 0:256], m_slot(s.m[1]), row("bo2"), ALU.add
                                          ).then_inc(misc_used[s.m[1] % 2], 1)
                        turn(dve, misc_used, s.m[1])
                        link(dve.tensor_scalar(tmp[:, 0:256], tmp[:, 0:256], tg[:, 9:10], None, ALU.mult))
                        link(dve.bn_stats(st6[:, :], tmp[:, 0:256]))
                        link(dve.bn_aggr(mv2[:, :], st6[:, :]))
                        dve.tensor_scalar(vare2[:, :], mv2[:, 1:2], EPS, None, ALU.add).then_inc(delta_var, 1)
                        dve.wait_ge(delta_rstd, u.u + 1)
                        link(dve.tensor_scalar(tmp2[:, 0:256], tmp[:, 0:256], mv2[:, 0:1], rstd2[:, :],
                                               ALU.subtract, ALU.mult))
                        link(dve.tensor_tensor(tmp[:, 0:256], tmp2[:, 0:256], row("lng"), ALU.mult))
                        link(dve.tensor_tensor(tmp2[:, 0:256], tmp[:, 0:256], row("lnb"), ALU.add))
                        link(dve.scalar_tensor_tensor(out=x[:, u.u, :], in0=tmp2[:, 0:256], scalar=tg[:, 2:3],
                                                      in1=x[:, u.u, :], op0=ALU.mult, op1=ALU.add))
                    else:
                        for j in range(2):
                            n = s.m[2 + j]
                            turn(dve, misc_ready, n)
                            dve.tensor_tensor(tmp[:, j * 256:(j + 1) * 256], m_slot(n), row("bp3"), ALU.add
                                              ).then_inc(misc_used[n % 2], 1)
                            turn(dve, misc_used, n)
                            b = 2 * u.u + j
                            link(dve.scalar_tensor_tensor(out=x[:, b, :], in0=tmp[:, j * 256:(j + 1) * 256],
                                                          scalar=tg[:, 3:4], in1=x[:, b, :], op0=ALU.mult, op1=ALU.add))
                elif s.kind == "xt":
                    normalise(s.xn)
                    if s.lm is not None:
                        n = {0: 8, 2: 16, 3: 4}[s.layer]
                        turn(dve, misc_ready, s.lm)
                        dve.tensor_copy(lg[:, s.xn.b, 0:n], m_slot(s.lm)[:, 0:n]).then_inc(misc_used[s.lm % 2], 1)
                elif s.kind == "route":
                    for m in s.lms:
                        turn(dve, misc_used, m)
                    n = {0: 8, 2: 16, 3: 4}[s.layer]
                    L = lg[:, :, 0:n]
                    if s.layer == 3:
                        link(dve.tensor_tensor(L, L, row("br3").unsqueeze(1).to_broadcast([P, NB, n]), ALU.add))
                    if s.layer in (0, 3):
                        first_max(L, n, oh[:, :, 0:n])
                        mx = r8[:, 0, :].unsqueeze(2).to_broadcast([P, NB, n])
                        dve.tensor_tensor(ra[:, :, 0:n], L, mx, ALU.subtract).then_inc(route_a, 1)
                        dve.wait_ge(route_b, s.exp_i + 1)
                        link(dve.tensor_reduce(r8[:, 2, :], ra[:, :, 0:n], AX.X, ALU.add))
                        link(dve.reciprocal(r8[:, 3, :], r8[:, 2, :]))
                        link(dve.tensor_scalar(r8[:, 3, :], r8[:, 3, :], tg[:, 4 + s.layer:5 + s.layer], None, ALU.mult))
                    if s.layer == 3:
                        link(dve.tensor_tensor(cm[:, :, 0:n], oh[:, :, 0:n], r8[:, 3, :].unsqueeze(2).to_broadcast([P, NB, n]),
                                               ALU.mult))
                    elif s.layer == 0:
                        link(dve.memset(rc[:, 0, 0:8], 0.0))
                        for b in range(1, NB):
                            link(dve.tensor_tensor(rc[:, b, 0:8], rc[:, b - 1, 0:8], oh[:, b - 1, 0:8], ALU.add))
                        dve.sem_inc(route_pe, 1)
                        turn(dve, misc_ready, s.m)
                        dve.tensor_tensor(rb[:, :, 0:8], m_slot(s.m)[:, 0:64].rearrange("p (b e) -> p b e", b=NB),
                                          oh[:, :, 0:8], ALU.mult).then_inc(misc_used[s.m % 2], 1)
                        turn(dve, misc_used, s.m)
                        link(dve.tensor_reduce(r8[:, 4, :], rb[:, :, 0:8], AX.X, ALU.add))
                        link(dve.tensor_tensor(rb[:, :, 0:8], oh[:, :, 0:8],
                                               const("base").unsqueeze(1).to_broadcast([P, NB, 8]), ALU.mult))
                        link(dve.tensor_reduce(r8[:, 5, :], rb[:, :, 0:8], AX.X, ALU.add))
                        link(dve.tensor_tensor(r8[:, 5, :], r8[:, 5, :], r8[:, 4, :], ALU.add))
                        link(dve.tensor_scalar(r8[:, 4, :], r8[:, 4, :], float(P), None, ALU.is_lt))
                        link(dve.tensor_tensor(r8[:, 5, :], r8[:, 5, :], r8[:, 4, :], ALU.mult))
                        link(dve.tensor_copy(idx[:, 1, :], r8[:, 5, :]))
                        link(dve.tensor_scalar(r8[:, 1, :], r8[:, 4, :], -1.0, 1.0, ALU.mult, ALU.add))
                        link(dve.tensor_tensor(r8[:, 1, :], r8[:, 1, :], const("trash"), ALU.mult))
                        link(dve.tensor_tensor(r8[:, 5, :], r8[:, 5, :], r8[:, 1, :], ALU.add))
                        link(dve.tensor_tensor(r8[:, 3, :], r8[:, 3, :], r8[:, 4, :], ALU.mult))
                        dve.tensor_copy(idx[:, 0, :], r8[:, 5, :]).then_inc(routed, 1)
                    else:
                        link(dve.tensor_scalar(ra[:, :, :], L, -87.0, None, ALU.max))
                        dve.sem_inc(route_a, 1)
                        dve.wait_ge(route_b, s.exp_i + 1)
                        link(dve.tensor_scalar(rc[:, :, :], ra[:, :, :], 1.0, None, ALU.add))
                        link(dve.reciprocal(ra[:, :, :], rc[:, :, :]))
                        gb = row("gb2").unsqueeze(1).to_broadcast([P, NB, 16])
                        link(dve.tensor_tensor(rc[:, :, :], ra[:, :, :], gb, ALU.add))
                        first_max(rc[:, :, :], 16, oh[:, :, :])
                        link(dve.tensor_scalar(lg[:, :, :], oh[:, :, :], -1e30, None, ALU.mult))
                        link(dve.tensor_tensor(rc[:, :, :], rc[:, :, :], lg[:, :, :], ALU.add))
                        first_max(rc[:, :, :], 16, lg[:, :, :])
                        link(dve.tensor_tensor(oh[:, :, :], oh[:, :, :], lg[:, :, :], ALU.add))
                        link(dve.tensor_tensor(oh[:, :, :], oh[:, :, :], ra[:, :, :], ALU.mult))
                        link(dve.tensor_reduce(r8[:, 2, :], oh[:, :, :], AX.X, ALU.add))
                        link(dve.tensor_scalar(r8[:, 2, :], r8[:, 2, :], 1e-9, None, ALU.add))
                        link(dve.reciprocal(r8[:, 3, :], r8[:, 2, :]))
                        link(dve.tensor_scalar(r8[:, 3, :], r8[:, 3, :], tg[:, 6:7], None, ALU.mult))
                        link(dve.tensor_tensor(cm[:, :, :], oh[:, :, :], r8[:, 3, :].unsqueeze(2).to_broadcast([P, NB, 16]),
                                               ALU.mult))
                elif s.kind == "expert":
                    e = s.e
                    turn(dve, S_ready, s.s)
                    if e >= 2:
                        dve.wait_ge(eo_out[e % 2], 16 * (e // 2))
                    dve.tensor_copy(eo[:, e % 2, :], psS[:, s.s % 2, 0:256]).then_inc(S_used[s.s % 2], 1)
                elif s.kind == "combine":
                    b = s.b
                    dve.wait_ge(gathered[b % 2], 16 * (b // 2 + 1))
                    dve.scalar_tensor_tensor(out=x[:, b, :], in0=ge[:, b % 2, :], scalar=r8[:, 3, b:b + 1],
                                             in1=x[:, b, :], op0=ALU.mult, op1=ALU.add).then_inc(combined, 1)
                    dve.wait_ge(combined, b + 1)
                elif s.kind == "gu":
                    w = s.width
                    if s.ch == 0 and s.h_free is not None:
                        turn(dve, S_ready, s.h_free)
                    dve.wait_ge(silu_done, s.sg + 1)
                    up = psT[0:w, s.n % 2, 512:1024]
                    dst = Hb[0:w, s.h % 2, s.ch, :]
                    if s.layer == 1:
                        ins = dve.scalar_tensor_tensor(out=dst, in0=up, scalar=col("us1", s.ch, w),
                                                       in1=sg[0:w, s.sg % 2, :], op0=ALU.mult, op1=ALU.mult)
                    else:
                        ins = dve.tensor_tensor(dst, up, sg[0:w, s.sg % 2, :], ALU.mult)
                    ins.then_inc(T_used[s.n % 2], 1)
                elif s.kind == "down":
                    b = s.tg * 4 + s.tc
                    turn(dve, S_ready, s.n)
                    for i in range(2):
                        if s.x_after[i]:
                            dve.wait_ge(S_used[i], s.x_after[i])
                    src = psS[:, s.n % 2, 0:256]
                    if s.layer == 1:
                        link(dve.tensor_tensor(tmp[:, 0:256], src, row("ds1"), ALU.mult))
                        src, w = tmp[:, 0:256], tg[:, 5:6]
                    elif s.blk.mask is None:
                        w = tg[:, 10:11]
                    else:
                        w = cm[:, b, s.blk.mask:s.blk.mask + 1]
                    dve.scalar_tensor_tensor(out=x[:, b, :], in0=src, scalar=w, in1=x[:, b, :],
                                             op0=ALU.mult, op1=ALU.add).then_inc(S_used[s.n % 2], 1)

        @block.gpsimd
        def _(pool):
            chained = [0]

            def link(ins):
                chained[0] += 1
                ins.then_inc(pool_chain, 1)
                pool.wait_ge(pool_chain, chained[0])

            def split(src, dst, w, done):
                link(pool.tensor_scalar(dst[:, 0, 0:w], src, 1.0, 0.0, ALU.mult, ALU.add))
                link(pool.tensor_tensor(rem[:, 0:w], src, dst[:, 0, 0:w], ALU.subtract))
                link(pool.tensor_scalar(dst[:, 1, 0:w], rem[:, 0:w], 1.0, 0.0, ALU.mult, ALU.add))
                pool.tensor_tensor(dst[:, 2, 0:w], rem[:, 0:w], dst[:, 1, 0:w], ALU.subtract).then_inc(done, 1)

            pool.wait_ge(const_in, 16 * 10)
            pool.wait_ge(zeros_made, 1)
            for s in steps:
                if s.kind == "barrier":
                    pool.wait_ge(rstd_ready, s.stats)
                elif s.kind == "stats":
                    pool.wait_ge(var_ready, s.i + 1)
                    pool.tensor_tensor(rstd[:, s.b:s.b + 1], vare[:, s.b:s.b + 1], const("mhalf"), ALU.pow
                                       ).then_inc(rstd_ready, 1)
                elif s.kind in ("kprep", "front"):
                    A = s.A
                    w = A.halves * A.T
                    if s.kind == "front":
                        if A.layer == 1:
                            pool.wait_ge(xn_ready, s.xn[0].i + 1)
                            if s.q >= 1:
                                pool.wait_ge(parts_q, s.q)
                            link(pool.tensor_scalar(qf[:, s.q % 2, 0:256], xn[:, s.u, :], 0.25, 0.0, ALU.mult, ALU.add))
                        elif A.layer == 0:
                            turn(pool, misc_used, s.m[0])
                        elif A.layer == 2:
                            turn(pool, misc_used, s.m[1])
                        else:
                            for m in range(2):
                                turn(pool, misc_used, s.m[4 + m])
                        if s.q >= 2:
                            pool.wait_ge(q_stored[s.q % 2], stored_total(steps, "q", s.q - 2))
                        if s.q >= 1:
                            pool.wait_ge(parts_q, s.q)
                        split(qf[:, s.q % 2, 0:w], sq[:, s.q % 2], w, parts_q)
                        pool.wait_ge(parts_q, s.q + 1)
                    if s.k is not None:
                        if s.kind == "kprep":
                            for m in range(2):
                                turn(pool, misc_used, s.m[2 + m])
                        elif A.layer == 0:
                            turn(pool, misc_used, s.m[1])
                        elif A.layer == 2:
                            turn(pool, misc_used, s.m[2])
                        if s.k >= 2:
                            pool.wait_ge(k_stored[s.k % 2], stored_total(steps, "k", s.k - 2))
                        src = ctx_s[:, s.u, :] if A.layer == 1 else kf[:, s.k % 2, 0:w]
                        split(src, sk[:, s.k % 2], w, parts_k)
                        pool.wait_ge(parts_k, s.k + 1)
                    if A.layer == 1:
                        if s.done_before >= 0:
                            pool.wait_ge(PV_done, s.done_before + 1)
                        for c in range(2):
                            ins = pool.tensor_copy(VA[:, s.g % 3, c * 8:(c + 1) * 8, 0:16],
                                                   ctx_t[:, c, s.u * P:(s.u + 1) * P].rearrange("p (h d) -> p h d", d=16))
                        ins.then_inc(V_copied, 1)
                elif s.kind == "out" and s.A.layer == 2:
                    pool.wait_ge(delta_var, s.un.u + 1)
                    pool.tensor_tensor(rstd2[:, :], vare2[:, :], const("mhalf"), ALU.pow).then_inc(delta_rstd, 1)
                elif s.kind == "scatter":
                    if s.b == 0:
                        pool.wait_ge(routed, 1)
                        pool.wait_ge(zero_in, 16 * NB)
                    pool.indirect_dma_start(xd, bass.IndirectOffsetOnAxis(ap=idx[:, 0, s.b:s.b + 1].bitcast(U32), axis=0),
                                            xn[:, s.b, :], None).then_inc(scattered, 16)
                elif s.kind == "combine":
                    if s.b == 0:
                        for i in range(2):
                            pool.wait_ge(eo_out[i], 16 * 4)
                    if s.b >= 2:
                        pool.wait_ge(combined, s.b - 1)
                    pool.indirect_dma_start(ge[:, s.b % 2, :], None, eod,
                                            bass.IndirectOffsetOnAxis(ap=idx[:, 1, s.b:s.b + 1].bitcast(U32), axis=0)
                                            ).then_inc(gathered[s.b % 2], 16)


def pack(sp, A, dst, src, c, part, at, width, sem):
    rows = dst[c * A.d:(c + 1) * A.d, 0:A.H * width].rearrange("d (h n) -> d h n", h=A.H)[:, :, at:at + A.T]
    n = A.halves * P
    order = "(h d) n -> d h n" if A.layer == 1 else "(d h) n -> d h n"
    sp.dma_start(rows, src[part, 0:n, 0:A.T].rearrange(order, d=A.d)).then_inc(sem, 16)


def q_total(steps, i):
    return 16 * 6 * len([s for s in steps if s.kind == "front" and s.q <= i and s.q % 2 == i % 2])


def k_total(steps, i):
    return 16 * 6 * len([s for s in steps if s.kind in ("front", "kprep") and s.k is not None
                         and s.k <= i and s.k % 2 == i % 2])


def stored_total(steps, which, i):
    total = 0
    for s in steps:
        if s.kind == "front" or (s.kind == "kprep" and which == "k"):
            j = s.q if which == "q" else s.k
            if j is not None and j <= i and j % 2 == i % 2:
                total += 16 * s.A.halves
    return total


def last_ks(steps):
    ks = [s.k for s in steps if s.kind == "kprep"]
    return ks[-2:]


def last_vturns(steps):
    return [s.m for s in steps if s.kind == "vturn"][-2:]


def last_stats(steps):
    return len([s for s in steps if s.kind == "stats"])


def expert_m(steps, e):
    return [s.m for s in steps if s.kind == "expert" and s.e == e][0]


def xt_slots(steps, layer):
    return [s.m for s in steps if s.kind == "xt" and s.layer == layer][-2:]


_plain = plan


def plan():
    steps = _plain()
    quant = 0
    rounds = 0
    routes = 0
    s_count = [0, 0]
    norm_m, out_m, neg_m, q_ms, out3 = {}, None, {}, None, None
    last_norm, lms = None, []
    after_S = None
    for s in steps:
        if s.kind == "kprep":
            quant += 1
            s.k_quant = quant
            s.prev_m = q_ms
            q_ms = s.m[2:4]
        elif s.kind == "front" and s.A.layer == 3:
            quant += 1
            s.q_quant = quant
            s.prev_m = q_ms
            q_ms = s.m[4:6]
        elif s.kind == "pv" and s.A.layer == 3:
            s.clip3 = rounds
            rounds += 1
        elif s.kind == "onorm":
            s.m_prev2 = norm_m.get(s.o - 2)
            norm_m[s.o] = s.m
            last_norm = s.m
            s.prev_turned = out3 if s.A.layer == 3 else None
        elif s.kind == "out":
            s.m_last_norm = last_norm
            s.m_prev = out_m
            if s.A.layer != 1:
                out_m = s.m
            if s.A.layer == 3:
                out3 = s.m[0:2]
        elif s.kind == "negmax":
            s.m_prev2 = neg_m.get(s.i - 2)
            neg_m[s.i] = s.m
        elif s.kind == "xt" and s.lm is not None:
            lms.append(s.lm)
        elif s.kind == "route":
            s.lms = lms[-2:]
            s.exp_i = routes
            routes += 1
        if s.kind == "stats":
            s.after = list(s_count) if after_S else None
        if s.kind == "smax" or s.kind == "down":
            if s.kind == "down":
                s.x_after = list(s_count)
            s_count[s.n % 2] = s.n // 2 + 1
            after_S = s.kind == "down"
        if s.kind == "expert":
            s_count[s.s % 2] = s.s // 2 + 1
    return steps


def kernel(**inputs):
    import numpy as np
    import concourse.bacc as bacc
    from concourse.bass_utils import run_bass_kernel_spmd as run

    a = {k: np.asarray(v) for k, v in inputs.items()}

    def halves(w):
        k, n = w.shape
        c = -(-k // P)
        full = np.zeros((c * P, n), w.dtype)
        full[:k] = w
        return full.reshape(c, P, n).transpose(1, 0, 2)

    def flat(*ws):
        return np.ascontiguousarray(np.concatenate([halves(w).reshape(P, -1) for w in ws], axis=1))

    def d_major(w, heads):
        n = w.shape[-1] // heads
        return w.reshape(*w.shape[:-1], heads, n).swapaxes(-1, -2).reshape(w.shape)

    arrays = {"x": a["x"], "ctx": a["ctx_2048"]}
    arrays["ctx_t"] = halves(a["ctx_2048"].reshape(NT, D).T)
    arrays["mask"] = a["mask_BxS2_ik0"].T
    vals = {"g_xattn": a["g_xattn"], "g_ffn": a["g_ffn"], "gamma": a["L1_xattn_gamma"].reshape(1),
            "rscale": a["L2_xattn_residual_scale"].reshape(1), "bv0": a["L0_xattn_bv"], "bv2": a["L2_xattn_bv"],
            "bo2": a["L2_xattn_bo"], "lng": a["L2_xattn_ln_gamma"], "lnb": a["L2_xattn_ln_beta"],
            "bq3": d_major(a["L3_xattn_bq"], 16), "bk3": d_major(a["L3_xattn_bkv"][:256], 16),
            "bp3": a["L3_xattn_bp"], "ds1": a["L1_ffn_down_s"], "br3": a["L3_ffn_br"], "gb2": a["L2_ffn_gate_bias"]}
    arrays["rows"] = np.concatenate([vals[n].reshape(-1) for n, _ in ROWS])
    cvals = {"bq0": d_major(a["L0_xattn_bq"], 16), "bk0": d_major(a["L0_xattn_bk"], 16), "bo0": a["L0_xattn_bo"],
             "bq2": d_major(a["L2_xattn_bq"], 16), "bk2": d_major(a["L2_xattn_bk"], 16),
             "bv3": a["L3_xattn_bkv"][256:], "gs1": a["L1_ffn_gate_s"], "us1": a["L1_ffn_up_s"]}
    arrays["cols"] = np.concatenate([halves(cvals[n].reshape(-1, 1)).reshape(P, -1) for n, _ in COLS], axis=1)
    part = np.arange(P, dtype=np.float32)
    sumsel = np.zeros((P, EW), np.float32)
    sumsel[:, SUMCOL] = 1.0
    arrays["cst"] = np.concatenate([
        np.eye(P, dtype=np.float32), np.triu(np.ones((P, P), np.float32), 1), np.ones((P, P), np.float32),
        np.tile(16.0 - np.arange(16, dtype=np.float32), (P, 1)), np.tile(128.0 * np.arange(8, dtype=np.float32), (P, 1)),
        TRASH + part[:, None] + P * np.arange(NB, dtype=np.float32), np.full((P, 1), -0.5, np.float32), sumsel], axis=1)
    b16 = mybir.dt.np(BF16)
    arrays["ident16"] = np.eye(P).astype(b16)
    arrays["ones3"] = np.ones((3, 4096), b16)
    arrays["w_at0"] = np.stack([d_major(a["L0_xattn_Wq"].T, 16), d_major(a["L0_xattn_Wk"].T, 16),
                                a["L0_xattn_Wv"].T, a["L0_xattn_Wo"].T], axis=1)
    arrays["w_at2"] = np.stack([halves(w) for w in (d_major(a["L2_xattn_Wq"].T, 16), d_major(a["L2_xattn_Wk"].T, 16),
                                                    a["L2_xattn_Wv"].T, a["L2_xattn_Wo"].T)], axis=1)
    wkv = a["L3_xattn_Wkv"]
    arrays["w_at3"] = np.stack([halves(w) for w in (d_major(a["L3_xattn_Wq"], 16), d_major(wkv[:, :256], 16),
                                                    wkv[:, 256:], a["L3_xattn_Wp"])], axis=1)
    arrays["wr"] = np.concatenate([halves(a["L0_ffn_w_gate"]), halves(a["L2_ffn_centroids"].T), halves(a["L3_ffn_Wr"])],
                                  axis=2)
    for e in range(8):
        arrays[f"w{e}"] = flat(a["L0_ffn_w1"][e], a["L0_ffn_w2"][e])
    arrays["w8"] = flat(a["L1_ffn_gate_w"].T, a["L1_ffn_up_w"].T, a["L1_ffn_down_w"].T)
    arrays["w9"] = flat(a["L2_ffn_wg_s"], a["L2_ffn_wu_s"], a["L2_ffn_wd_s"])
    for g in range(2):
        arrays[f"w{10 + g}"] = np.concatenate([flat(a["L2_ffn_wg"][e], a["L2_ffn_wu"][e], a["L2_ffn_wd"][e])
                                               for e in range(8 * g, 8 * g + 8)], axis=1)
    for e in range(4):
        arrays[f"w{12 + e}"] = flat(a["L3_ffn_Wg"][e], a["L3_ffn_Wu"][e], a["L3_ffn_Wd"][e])

    nc = bacc.Bacc("TRN2", target_bir_lowering=False, num_devices=1)
    feeds, views = {}, {}
    for name, v in arrays.items():
        v = np.ascontiguousarray(v)
        feeds[f"in_{name}"] = v
        views[name] = nc.dram_tensor(f"in_{name}", v.shape, mybir.dt.from_np(v.dtype), kind="ExternalInput").ap()
    out = nc.dram_tensor("out_x", [NB, S, D], F32, kind="ExternalOutput").ap()
    flamingo(nc, views, out)
    r = run(nc, [feeds], core_ids=[0])
    return r.results[0]["out_x"]
```

```python
from contextlib import ExitStack

import concourse.bass as bass
from concourse import mybir

F32 = mybir.dt.float32
BF16 = mybir.dt.bfloat16
I32 = mybir.dt.int32
U32 = mybir.dt.uint32
ALU = mybir.AluOpType
ACT = mybir.ActivationFunctionType
AX = mybir.AxisListType


class Layer:

    def __init__(self, layer=None, H=None, d=None, U=None, nb=None, TC=None, T=None, NC=None,
                 has_max=None, G=None, halves=None):
        self.layer, self.H, self.d, self.U, self.nb, self.TC, self.T, self.NC = layer, H, d, U, nb, TC, T, NC
        self.has_max, self.G, self.halves = has_max, G, halves


class Blk:

    def __init__(self, widths=None, item=None, off=None, F=None, mask=None):
        self.widths, self.item, self.off, self.F, self.mask = widths, item, off, F, mask


class Norm:

    def __init__(self, b=None, stat=None, i=None):
        self.b, self.stat, self.i = b, stat, i


class Record:

    def __init__(self, kind=None, kind_of=None, A=None, u=None, b=None, i=None, g=None, c=None,
                 j=None, tc=None, h=None, k=None, m=None, n=None, o=None, p=None, s=None, q=None,
                 sg=None, clip=None, un=None, item=None, free=None, stats=None, last_P=None,
                 last_S=None, neg=None, layer=None, xn=None, lm=None, first=None, blk=None, tg=None,
                 ch=None, width=None, h_free=None, last_T=None, last_m=None, done_before=None,
                 m_prev=None, m_prev2=None, m_last_norm=None, prev_m=None, clip3=None, exp_i=None,
                 after=None, x_after=None, m_x=None, m_v=None, m_t=None, o_of=None, packed=None,
                 packed_before=None):
        self.kind, self.kind_of, self.A, self.u, self.b, self.i, self.g, self.c = kind, kind_of, A, u, b, i, g, c
        self.j, self.tc, self.h, self.k, self.m, self.n, self.o, self.p = j, tc, h, k, m, n, o, p
        self.s, self.q, self.sg, self.clip, self.un, self.item, self.free, self.stats = s, q, sg, clip, un, item, free, stats
        self.last_P, self.last_S, self.neg, self.layer, self.xn, self.lm, self.first, self.blk = last_P, last_S, neg, layer, xn, lm, first, blk
        self.tg, self.ch, self.width, self.h_free, self.last_T, self.last_m, self.done_before, self.m_prev = tg, ch, width, h_free, last_T, last_m, done_before, m_prev
        self.m_prev2, self.m_last_norm, self.prev_m, self.clip3, self.exp_i, self.after, self.x_after, self.m_x = m_prev2, m_last_norm, prev_m, clip3, exp_i, after, x_after, m_x
        self.m_v, self.m_t, self.o_of, self.packed, self.packed_before = m_v, m_t, o_of, packed, packed_before


P = 128
NB = 8
D = 256
S = 128
NT = NB * S
EPS = 1e-5
EW = 32
SUMCOL = 16
MAGIC = 12582912.0
LN255 = 5.541263545158426
SLOTW = 6144
BANKS = 3
TILES3 = NB + 3
TRASH = NT

ROWS = [("g_xattn", 4), ("g_ffn", 4), ("gamma", 1), ("rscale", 1), ("bv0", 128), ("bv2", 256),
        ("bo2", 256), ("lng", 256), ("lnb", 256), ("bq3", 256), ("bk3", 256), ("bp3", 256),
        ("ds1", 256), ("br3", 4), ("gb2", 16)]
COLS = [("bq0", 1), ("bk0", 1), ("bo0", 1), ("bq2", 2), ("bk2", 2), ("bv3", 2), ("gs1", 6), ("us1", 6)]
CONST = [("ident", 128), ("before", 128), ("ones", 128), ("desc", 16), ("base", 8), ("trash", 8),
         ("mhalf", 1), ("sumsel", 32), ("tiles", 16)]


def offsets(items):
    at, out = 0, {}
    for name, n in items:
        out[name] = (at, at + n)
        at += n
    return out, at


def attn(layer, heads, d, units, batches, tcs, chunks, has_max):
    return Layer(layer=layer, H=heads, d=d, U=units, nb=batches, TC=tcs, T=tcs * P,
                           NC=chunks, has_max=has_max, G=heads // 4, halves=heads * d // P)


ATT = [attn(0, 16, 8, 8, 1, 2, 2, True), attn(1, 8, 16, 8, 1, 2, 2, True),
       attn(2, 16, 16, 8, 1, 1, 1, False), attn(3, 16, 16, 4, 2, 2, 8, True)]


def ffn_blocks(layer):
    if layer == 1:
        return [Blk(widths=[128] * 5 + [64], item=8, off=0, F=704, mask=None)]
    out = [Blk(widths=[128] * 2, item=9, off=0, F=256, mask=None)]
    return out + [Blk(widths=[128], item=10 + e // 8, off=768 * (e % 8), F=128, mask=e) for e in range(16)]


def merge(*streams):
    order = []
    for k, (thunks, start, end) in enumerate(streams):
        for i, thunk in enumerate(thunks):
            order.append((start + (end - start) * (i + 0.5) / len(thunks), k, i, thunk))
    for _, _, _, thunk in sorted(order, key=lambda x: x[:3]):
        thunk()


TIMES = [
    dict(front=0.428, store=0.684, packs=0.8, max=1.246, max_end=1.7, neg=1.879, body=2.314, end=3.9, start=0.37, span=1.0),
    dict(front=0.071, store=0.793, packs=1.423, max=2.0, max_end=2.569, neg=2.8, body=3.358, end=5.302, start=0.1, span=1.0),
    dict(front=0.541, store=0.607, packs=0.791, body=1.546, end=3.167, start=0.1, span=1.0),
    dict(front=0.152, store=0.219, packs=0.645, max=1.101, max_end=1.85, neg=1.864, body=2.135, end=3.78, start=0.246, span=0.862)]


def plan():
    steps = []
    n = dict(sg3=0, B=0, T=0, P=0, O=0, unit=0, stat=0, xn=0, q=0, k=0, neg=0, sg=0, clip=0, round=0, quant=0, exp=0)
    stat_of, item_free, s_count, packed = {}, {}, [0] * BANKS, [0, 0]
    last = dict(onorm=None, norm={}, neg={}, out_y=None, quant_t=None)

    def take(ring):
        ring = "B" if ring in "MS" else ring
        n[ring] += 1
        if ring == "B":
            s_count[(n["B"] - 1) % BANKS] = (n["B"] - 1) // BANKS + 1
        return n[ring] - 1

    def add(kind, **k):
        s = Record(kind=kind, **k)
        steps.append(s)
        return s

    def stats(b, after=None):
        stat_of[b] = take("stat")
        add("stats", b=b, i=stat_of[b], after=after)

    def normed(b):
        return Norm(b=b, stat=stat_of[b], i=take("xn"))

    def barrier():
        add("barrier", stats=n["stat"])

    def wload(i):
        add("wload", item=i, free=item_free.get(i - 2))

    def quant(r, scaled):
        s = add("quant", un=r, s=scaled, prev_m=last["quant_t"])
        s.i = take("quant")
        return s.i

    def keys_ahead():
        A = ATT[3]
        out, mk = [], {}

        def unit(u):
            r = Record(A=A, u=u, k=take("k"))

            def kp(j):
                def f():
                    r.m_v = (r.m_v or []) + [add("kp", un=r, u=u, j=j, m=take("M")).m]
                return f

            def q():
                r.i = quant(r, False)

            def kt(m):
                def f():
                    s = add("kt", un=r, c=m, i=r.i, m=take("M"))
                    r.m = (r.m or []) + [s.m]
                    last["quant_t"] = s.m
                return f

            def vp(m):
                def f():
                    mk["v"] = add("vp", un=r, u=u, c=m, m=take("M")).m
                return f

            def ks():
                add("split", un=r, A=A, kind_of="k")

            def store():
                add("store", un=r, A=A, kind_of="k")
            return [kp(0), kp(1), q, vp(0), kt(0), vp(1), kt(1), ks, store]
        for u in range(4):
            out += unit(u)
        out.append(lambda: add("vscale", last_m=mk["v"]))
        for c in range(NB):
            def turn(c=c):
                mk["t"] = add("vturn", c=c, m=take("M")).m
            out.append(turn)
        out.append(lambda: add("vstore", m=mk["t"]))
        return out

    def attention(A, later):
        barrier()
        add("attn_begin", A=A)
        units = []

        def front(u):
            r = Record(A=A, u=u, g=take("unit"), k=take("k") if A.layer < 3 else None)
            units.append(r)
            r.packed_before = packed[r.g % 2]
            packed[r.g % 2] += 16 * (6 if A.layer == 1 else 3)
            r.packed = packed[r.g % 2]

            def fn(j):
                def f():
                    xs = normed(u * A.nb + j)
                    if A.layer >= 2:
                        s = add("fx", A=A, un=r, j=j, xn=xs, m=take("M"))
                        r.m_x = s.m
                    else:
                        add("fn", xn=xs)
                        r.xn = xs
                return f

            def proj(kind):
                def f():
                    s = add(kind, A=A, un=r, m=take("M"))
                    if kind == "fv":
                        r.m_v = s.m
                        s.done_before = done()
                    else:
                        r.m = (r.m or []) + [s.m]
                return f

            def done():
                assert u < 3 or units[u - 3].last_P is not None
                return units[u - 3].last_P if u >= 3 else -1

            def fq3(j):
                def f():
                    r.m_v = (r.m_v or []) + [add("fq3", A=A, un=r, j=j, m=take("M"), m_prev=r.m_x).m]
                return f

            def q3():
                r.i = quant(r, True)

            def fqt(m):
                def f():
                    s = add("fqt", un=r, c=m, i=r.i, m=take("M"))
                    r.m = (r.m or []) + [s.m]
                    last["quant_t"] = s.m
                return f

            def split():
                add("split", un=r, A=A, kind_of="qk")

            def store():
                add("store", un=r, A=A, kind_of="qk")

            def packs():
                add("packs", un=r, A=A, done_before=done())
            out = [fn(j) for j in range(A.nb)]
            if A.layer in (0, 2):
                out += [proj("fq"), proj("fk"), split]
            elif A.layer == 1:
                out += [split]
            else:
                out += [fq3(0), fq3(1), q3, fqt(0), fqt(1), split]
            return out, [store], [packs] + ([proj("fv")] if A.layer in (0, 2) else [])

        def maxes(r):
            out = []
            for tc in range(A.TC):
                for j in range(A.H * A.NC * P // 512):
                    def f(tc=tc, j=j):
                        r.last_S = add("smax", A=A, un=r, tc=tc, j=j, first=(tc == 0 and j == 0), n=take("S")).n
                    out.append(f)

            def split():
                r.neg = take("neg")
                add("negsplit", A=A, un=r, i=r.neg, m_prev2=last["neg"].get(r.neg - 2))

            def turn():
                last["neg"][r.neg] = add("negmax", A=A, un=r, i=r.neg, m=take("M")).m
            return out, split, turn

        def body(r):
            tiles = [(g, c) for g in range(A.G) for c in range(A.NC)]
            made, out = {}, []
            lag = 1 if A.layer < 2 else 2

            def st(i):
                g, c = tiles[i]
                s = add("st", A=A, un=r, g=g, c=c, first=(i == 0), n=take("T"), p=take("P"))
                s.clip = take("clip") if A.layer == 2 else None
                made[i] = s

            def rnd(i):
                made[i].clip3 = take("round")
                add("round", n=made[i].n, p=made[i].p)

            def pv(i):
                s = made[i]
                if s.c == 0:
                    r.o = take("O")
                add("pv", A=A, un=r, g=s.g, c=s.c, n=s.n, p=s.p, o=r.o, clip=s.clip, clip3=s.clip3)
                r.last_P = s.p if i == len(tiles) - 1 else None
                last["P3"] = s.p
                if s.c == A.NC - 1:
                    add("oev", A=A, o=r.o, p=s.p, m_prev2=last["norm"].get(r.o - 2))

            def onorm(i):
                s = made[i]
                m = take("M")
                last["norm"][s.un.o_of[s.g]] = m
                r.m_last_norm = m
                add("onorm", A=A, un=r, g=s.g, o=s.un.o_of[s.g], m=m, m_prev=last["onorm"])
                last["onorm"] = m
            r.o_of = {}
            for i in range(len(tiles) + lag + 1):
                def f(i=i):
                    if i < len(tiles):
                        st(i)
                    if A.layer == 3 and 0 <= i - 1 < len(tiles):
                        rnd(i - 1)
                    k = i - lag
                    if 0 <= k - 1 < len(tiles) and tiles[k - 1][1] == A.NC - 1:
                        onorm(k - 1)
                    if 0 <= k < len(tiles):
                        pv(k)
                        r.o_of[tiles[k][0]] = r.o
                out.append(f)
            return out

        def finish(r):
            def ot(m):
                def f():
                    s = add("ot", A=A, un=r, c=m, m=take("M"), m_last_norm=r.m_last_norm, m_prev=last["out_y"])
                    r.m_t = (r.m_t or []) + [s.m]
                return f

            def oy(j):
                def f():
                    s = add("oy", A=A, un=r, j=j, m=take("M"))
                    last["out_y"] = s.m
                    if A.layer != 2:
                        stats(r.u * A.nb + j)
                return f

            def oz():
                add("oz", un=r)
                stats(r.u)
            if A.layer == 1:
                def f():
                    add("ot", A=A, un=r, c=0, m=take("M"), m_last_norm=r.m_last_norm)
                    stats(r.u)
                return [f]
                return [f]
            return ([ot(m) for m in range(A.halves)] if A.layer == 3 else [ot(0)]) + [oy(j) for j in range(A.nb)] \
                + ([oz] if A.layer == 2 else [])

        at = TIMES[A.layer]
        streams = []
        for u in range(A.U):
            first, store, packs = front(u)
            streams += [(first, u, u + at["front"]), (store, u + at["store"], u + at["store"]),
                        (packs, u + at["packs"], u + at["packs"] + 0.02)]
            if A.has_max:
                tiles, split, turn = maxes(units[u])
                streams += [(tiles, u + at["max"], u + at["max_end"]),
                            ([split], u + at["max_end"], u + at["max_end"]),
                            ([turn], u + at["neg"], u + at["neg"])]
            streams += [(body(units[u]), u + at["body"], u + at["body"] + at["span"]),
                        (finish(units[u]), u + at["body"] + at["span"] + at["start"], u + at["end"]),
                        ([f for b in range(u * A.nb, (u + 1) * A.nb) for f in later(b)],
                         u + at["end"] + 0.1, u + at["end"] + 0.9)]
        merge(*streams)

    def turned(layer):
        def thunks(b):
            def f():
                add("xt", layer=layer, xn=normed(b), m=take("M"))

            def g():
                last["lm"] = add("xl", layer=layer, b=b, m=take("M"), m_prev=steps_m(b)).m

            def steps_m(b):
                return [s.m for s in steps if s.kind == "xt" and s.xn.b == b][-1]
            return [f, g] if layer != 1 else [f]
        return thunks

    def route(layer, m):
        add("route", layer=layer, m=m, lm=last["lm"], exp_i=take("exp"))

    def moe_capacity():
        barrier()
        wload(1)
        route(0, take("M"))
        for b in range(NB):
            add("scatter", b=b)
        out, rec = [], {}

        def ext(e):
            def f():
                rec[e] = add("ext", i=e, m=take("M"))
            return f

        def exu(e):
            def f():
                rec[e, "u"] = add("exu", i=e, m=rec[e].m, n=take("T"))
            return f

        def exd(e):
            def f():
                s = add("exd", i=e, n=rec[e, "u"].n, s=take("S"))
                item_free[e] = s.s
                if e + 2 <= 8:
                    wload(e + 2)
            return f
        for e in range(8):
            out += [ext(e), exu(e)] + ([exd(e - 1)] if e else [])
        out.append(exd(7))
        keys = keys_ahead()
        merge((keys, 0.0, 1.0), (out, 0.12, 1.0))
        add("w3load", item="w_at2")
        for b in range(NB):
            add("gather", b=b)
        for b in range(NB):
            add("combine", b=b)
            stats(b)

    def sorted_experts():
        add("w3first", p=last["P3"])
        barrier()
        route(3, take("M"))
        for b in range(NB):
            add("scatter3", b=b)
        tiles = []

        def sx(t):
            tiles.append(Record(i=t, sg=[], g=[]))
            tiles[t].m_x = add("sx", i=t, m=take("M")).m

        def su(t, j):
            r = tiles[t]
            g, m_x = take("sg3"), r.m_x
            r.g.append(g)
            add("su", i=t, j=j, m_x=m_x, g=g, n=take("T"), sg=take("sg"), un=r)

        def sh(t, j):
            r = tiles[t]
            r.m = (r.m or []) + [add("sh", i=t, j=j, g=r.g[j], m=take("M"), m_prev=tiles[t - 2].s if t >= 2 else None).m]

        def sd(t):
            r = tiles[t]
            r.s = add("sd", i=t, un=r, s=take("M")).s
        add("sx_load", i=None)
        sx(0)
        for t in range(TILES3):
            su(t, 0)
            if t >= 1:
                sh(t - 1, 1)
            if t + 1 < TILES3:
                sx(t + 1)
            su(t, 1)
            if t >= 1:
                sd(t - 1)
            sh(t, 0)
        sh(TILES3 - 1, 1)
        sd(TILES3 - 1)
        for b in range(NB):
            add("gather3", b=b)
        for b in range(NB):
            add("combine3", b=b)

    def dense(layer):
        barrier()
        if layer == 2:
            wload(9)
            add("w3load", item="w_at3")
        if layer > 1:
            route(layer, None)
        blocks = ffn_blocks(layer)
        pending, hcount, h_free = None, 0, {}

        def down(work):
            blk, tg, h, last_T = work
            final = blk is blocks[-1]
            for tc in range(4):
                x_after = list(s_count)
                s = add("down", layer=layer, blk=blk, tg=tg, tc=tc, h=h, last_T=last_T, x_after=x_after, n=take("S"))
                if final:
                    stats(tg * 4 + tc, list(s_count))
            h_free[h] = s.n
            item_free[blk.item] = s.n
            if tg == 1:
                after = {(2, 9): 11, (2, 10): 12, (1, 8): 10}.get((layer, blk.item))
                last_of_item = blk is [x for x in blocks if x.item == blk.item][-1]
                if after is not None and last_of_item:
                    wload(after)

        xt_last = [s.m for s in steps if s.kind == "xt"][-1]
        for blk in blocks:
            for tg in range(2):
                h = hcount
                hcount += 1
                for ch, width in enumerate(blk.widths):
                    s = add("gu", layer=layer, blk=blk, tg=tg, ch=ch, width=width, h=h, m=xt_last,
                            h_free=h_free.get(h - 2), n=take("T"), sg=take("sg"))
                if pending:
                    down(pending)
                pending = (blk, tg, h, s.n)
        down(pending)

    wload(0)
    for b in range(NB):
        stats(b)
    for i, A in enumerate(ATT):
        attention(A, turned(A.layer))
        moe_capacity() if i == 0 else sorted_experts() if i == 3 else dense(i)
    return steps


def flamingo(nc, t, out):
    steps = plan()
    ext_m = {s.i: s.m for s in steps if s.kind == "ext"}
    hidden_turned = {s.g: s.m for s in steps if s.kind == "sh"}
    row_at, row_n = offsets(ROWS)
    col_at, col_n = offsets(COLS)
    cst_at, cst_n = offsets(CONST)

    with ExitStack() as ctx:
        def sb(name, shape, dt=F32):
            return ctx.enter_context(nc.sbuf_tensor(name, shape, dt))

        def pb(name, shape, dt=F32):
            return ctx.enter_context(nc.psum_tensor(name, shape, dt))

        def sem(name):
            return ctx.enter_context(nc.semaphore(name))

        def ring(name):
            return [sem(f"{name}{i}") for i in range(BANKS)]

        def pair(name):
            return [sem(f"{name}{i}") for i in range(2)]

        x = sb("x", [P, NB, D])
        xn = sb("xn", [P, NB, D])
        ctx_t = sb("ctx_t", [P, 2, NT])
        xn_t = sb("xn_t", [P, 2, NT])
        whole = sb("whole", [P, SLOTW + 17408 + NB * D])
        w0 = whole[:, 0:SLOTW]
        arena = whole[:, SLOTW:SLOTW + 17408]
        ctx_s = whole[:, SLOTW + 17408:].rearrange("p (b n) -> p b n", b=NB)
        QP = arena[:, 0:6144].bitcast(BF16).rearrange("p (r n) -> p r n", r=3)
        KP = arena[:, 6144:14336].bitcast(BF16)
        VA = arena[:, 14336:17408].rearrange("p (r w e) -> p r w e", r=3, e=EW)
        VQ = arena[:, 14336:16384].bitcast(BF16).rearrange("p (w e) -> p w e", e=EW)
        VQ_made = arena[:, 0:2048].bitcast(BF16).rearrange("p (w e) -> p w e", e=EW)
        Hb = arena[:, 0:8192].rearrange("p (r c n) -> p r c n", r=2, c=8)
        vf = arena[:, 0:2048].rearrange("p (m n) -> p m n", m=2)
        vr = arena[:, 2048:4096].rearrange("p (m n) -> p m n", m=2)
        vi = arena[:, 4096:5120].bitcast(BF16).rearrange("p (m n) -> p m n", m=2)
        Wslot = [w0, arena[:, 8192:8192 + SLOTW]]
        Pt = sb("Pt", [P, 3, 1024])
        nb_t = sb("nb_t", [P, 2, 512])
        nb16 = nb_t[:, :, :].rearrange("p r n -> p (r n)").bitcast(BF16).rearrange("p (r n) -> p r n", r=2)
        sq = sb("sq", [P, 2, 3, 512], BF16)
        sk = sb("sk", [P, 2, 3, 512], BF16)
        qf = sb("qf", [P, 2, 512])
        kf = sb("kf", [P, 2, 512])
        rem = sb("rem", [P, 512])
        Oe = sb("Oe", [P, 2, 256])
        On = sb("On", [P, 2, 512])
        OnT = sb("OnT", [P, 2, 256])
        w_at0 = sb("w_at0", [P, 4, 128])
        w_at2 = sb("w_at2", [P, 4, 2, 256])
        wr = sb("wr", [P, 2, 28])
        rows = sb("rows", [P, row_n])
        cols = sb("cols", [P, col_n])
        cst = sb("cst", [P, cst_n])
        ident16 = sb("ident16", [P, P], BF16)
        mask_i = sb("mask_i", [P, NB], I32)
        att = sb("att", [P, NB])
        att_b = sb("att_b", [P, NB])
        tg = sb("tg", [P, 16])
        colx = sb("colx", [P, 4])
        st6 = sb("st6", [P, 6])
        mv = sb("mv", [P, NB, 2])
        vare = sb("vare", [P, NB])
        rstd = sb("rstd", [P, NB])
        mv2 = sb("mv2", [P, 2])
        vare2 = sb("vare2", [P, 1])
        rstd2 = sb("rstd2", [P, 1])
        mxp = sb("mxp", [P, 2, 64])
        nm = sb("nm", [P, 2, 32])
        npt = sb("npt", [P, 2, 2 * 3 * 16], BF16)
        nmT = sb("nmT", [48, 2, 256], BF16)
        rden = sb("rden", [P, 2, 4])
        tmp = sb("tmp", [P, 512])
        tmp2 = sb("tmp2", [P, 512])
        y_t = sb("y_t", [P, 256])
        qs = sb("qs", [P, 3, 32])
        vs = sb("vs", [P, 3, 2])
        lg = sb("lg", [P, NB, 16])
        r8 = sb("r8", [P, 6, NB])
        te = sb("te", [P, 16], I32)
        idx = sb("idx", [P, 2, NB], I32)

        psB = pb("psB", [P, BANKS, 512])
        psT = pb("psT", [P, 2, 1024])
        psO = pb("psO", [P, 2, 256])

        ra, rb, rc, oh, cm = [Pt[:, 2, 128 * i:128 * (i + 1)].rearrange("p (b e) -> p b e", b=NB)
                              for i in range(5)]
        sg = Pt[:, 0:2, 0:512]
        xe = qf[:, :, 0:256]
        xeT = qf[:, :, 256:512].rearrange("p r (k n) -> p r k n", k=2)
        eo = Oe
        ge = arena[:, 5120:7168].rearrange("p (b n) -> p b n", b=NB)

        sx = xn[:, 0:4, :]
        so = xn[:, 4:8, :]
        htok = Pt[:, 0:2, 512:1024]
        hT = ctx_t
        ge3 = xn_t[:, :, :].rearrange("p k n -> p (k n)").rearrange("p (b n) -> p b n", b=NB)

        sxd = nc.dram_tensor("scr_sorted", [TILES3 * P, D], F32).ap()
        sod = nc.dram_tensor("scr_sorted_out", [TILES3 * P, D], F32).ap()
        dq = [nc.dram_tensor(f"scr_q{i}", [3, 2 * P, 256], BF16).ap() for i in range(2)]
        dk = [nc.dram_tensor(f"scr_k{i}", [3, 2 * P, 256], BF16).ap() for i in range(2)]
        dk3 = nc.dram_tensor("scr_k3", [3, 2 * P, NT], BF16).ap()
        dv3 = nc.dram_tensor("scr_v3", [P, NB * 16, EW], BF16).ap()
        xd = nc.dram_tensor("scr_dispatched", [2 * NT, D], F32).ap()
        eod = nc.dram_tensor("scr_expert_out", [NT, D], F32).ap()

        def row(name):
            return rows[:, row_at[name][0]:row_at[name][1]]

        def col(name, j=0, n=P):
            return cols[0:n, col_at[name][0] + j:col_at[name][0] + j + 1]

        def const(name):
            return cst[:, cst_at[name][0]:cst_at[name][1]]

        x_in = sem("x_in")
        const_in = sem("const_in")
        w_in = pair("w_in")
        w3_in = sem("w3_in")
        var_ready = sem("var_ready")
        rstd_ready = sem("rstd_ready")
        xn_ready = sem("xn_ready")
        bank_ready, bank_used = ring("bank_ready"), ring("bank_used")
        T_ready, T_used = pair("T_ready"), pair("T_used")
        O_used = pair("O_used")
        PV_done = sem("PV_done")
        parts_q = sem("parts_q")
        parts_k = sem("parts_k")
        V_copied = sem("V_copied")
        q_stored, k_stored = pair("q_stored"), pair("k_stored")
        q_packed, k_packed = pair("q_packed"), pair("k_packed")
        v3_stored = sem("v3_stored")
        v3_in = sem("v3_in")
        k3_in = sem("k3_in")
        k_ones = sem("k_ones")
        neg_split = sem("neg_split")
        neg_in = pair("neg_in")
        exp_done = sem("exp_done")
        clipped = sem("clipped")
        rounded = sem("rounded")
        quant_q = sem("quant_q")
        v_quant = sem("v_quant")
        delta_var = sem("delta_var")
        delta_rstd = sem("delta_rstd")
        silu_done = sem("silu_done")
        gates_done = sem("gates_done")
        route_a = sem("route_a")
        route_b = sem("route_b")
        route_pe = sem("route_pe")
        routed = sem("routed")
        zero_in = sem("zero_in")
        zeros_made = sem("zeros_made")
        scattered = sem("scattered")
        xe_in = pair("xe_in")
        eo_out = pair("eo_out")
        gathered = [sem(f"gathered{b}") for b in range(NB)]
        combined = sem("combined")
        sorted_in = [sem(f"sorted_in{i}") for i in range(4)]
        sorted_out = [sem(f"sorted_out{i}") for i in range(4)]
        scattered3 = sem("scattered3")
        gathered3 = [sem(f"gathered3_{b}") for b in range(NB)]
        routed3 = sem("routed3")
        experts_in = sem("experts_in")
        hidden3 = sem("hidden3")
        combined3 = sem("combined3")
        out_done = sem("out_done")
        memset_done = sem("memset_done")
        dve_chain = sem("dve_chain")
        pool_chain = sem("pool_chain")

        N_CONST = 12

        def turn(eng, ready, n):
            eng.wait_ge(ready[n % len(ready)], n // len(ready) + 1)

        def free(eng, used, n):
            if n >= len(used):
                eng.wait_ge(used[n % len(used)], n // len(used))

        def m_slot(n):
            return psB[:, n % BANKS, 0:256]

        def evacuated(eng, n):
            turn(eng, bank_used, n)

        def scratch(tiles, A, g):
            if A.halves == 2:
                return tiles[g % 2]
            return tiles[g % 2].rearrange("c p n -> (c p) n")[0:3 * P, :].rearrange("(c p) n -> c p n", p=P)

        def kslot(A, u):
            return KP[:, :] if A.layer == 3 else KP[:, 4096 * (u.g % 3):4096 * (u.g % 3 + 1)]

        def wait_packs(pe, s):
            g = s.un.g
            pe.wait_ge(q_packed[g % 2], s.un.packed)
            if s.A.layer < 3:
                pe.wait_ge(k_packed[g % 2], s.un.packed)
            else:
                pe.wait_ge(k3_in, 48)

        block = ctx.enter_context(nc.Block())

        @block.sync
        def _(sp):
            sp.dma_start(x[:, :, :], t["x"].rearrange("b p d -> p b d")).then_inc(x_in, 16)
            sp.dma_start(rows[:, :], t["rows"].partition_broadcast(P)).then_inc(const_in, 16)
            sp.dma_start(cols[:, :], t["cols"]).then_inc(const_in, 16)
            sp.dma_start(cst[:, :], t["cst"]).then_inc(const_in, 16)
            sp.dma_start(w_at0[:, :, :], t["w_at0"]).then_inc(const_in, 16)
            sp.dma_start(ctx_s[:, :, :], t["ctx"].rearrange("b p d -> p b d")).then_inc(const_in, 16)
            sp.dma_start(ident16[:, :], t["ident16"]).then_inc(const_in, 16)
            sp.dma_start(mask_i[:, :], t["mask"]).then_inc(const_in, 16)
            sp.dma_start(wr[:, :, :], t["wr"]).then_inc(const_in, 16)
            for kd in range(2):
                sp.dma_start(ctx_t[:, kd, :], t["ctx_t"][:, kd, :]).then_inc(const_in, 16)
            sp.dma_start(w_at2[:, :, :, :], t["w_at3"]).then_inc(w3_in, 16)
            sp.wait_ge(zeros_made, 1)
            for r in range(0, NT, P):
                sp.dma_start(xd[r:r + P, :], On[:, 0, 0:256]).then_inc(zero_in, 16)
            for r in range(0, TILES3 * P, P):
                sp.dma_start(sxd[r:r + P, :], On[:, 0, 0:256]).then_inc(zero_in, 16)
            sp.wait_ge(memset_done, 4)
            for s in steps:
                if s.kind == "barrier":
                    sp.wait_ge(rstd_ready, s.stats)
                elif s.kind == "attn_begin":
                    A = s.A
                    if A.layer == 3:
                        pack(sp, A, KP[:, :], dk3, NT, k3_in, is_q=False)
                        sp.wait_ge(v3_stored, 16)
                        sp.dma_start(VQ[:, :, :], dv3).then_inc(v3_in, 16)
                    if A.has_max:
                        for r in range(4):
                            sp.dma_start(KP[96:99, 4096 * r:4096 * (r + 1)], t["ones3"]).then_inc(k_ones, 16)
                elif s.kind == "vstore":
                    turn(sp, bank_used, s.m)
                    sp.dma_start(dv3, VQ_made[:, :, :]).then_inc(v3_stored, 16)
                elif s.kind == "w3load":
                    sp.dma_start(w_at2[:, :, :, :], t[s.item]).then_inc(w3_in, 16)
                elif s.kind == "wload":
                    i, slot = s.item, s.item % 2
                    if s.free is not None:
                        turn(sp, bank_ready, s.free)
                    w = t[f"w{i}"]
                    sp.dma_start(Wslot[slot][:, 0:w.shape[1]], w).then_inc(w_in[slot], 16)
                elif s.kind == "store":
                    A, u = s.A, s.un
                    w = A.halves * A.T // 2

                    def store(dst, src, sem):
                        for m in range(2):
                            rows_ = slice(m * P, (m + 1) * P) if A.halves == 2 else slice(0, P)
                            at = 0 if A.halves == 2 else m * w
                            sp.dma_start(dst[:, rows_, at:at + w].rearrange("c p n -> p c n"),
                                         src[:, :, m * w:(m + 1) * w]).then_inc(sem, 16)
                    if s.kind_of == "qk":
                        sp.wait_ge(parts_q, u.g + 1)
                        if u.g >= 2:
                            sp.wait_ge(q_packed[u.g % 2], u.packed_before)
                        store(scratch(dq, A, u.g), sq[:, u.g % 2], q_stored[u.g % 2])
                    if u.k is not None:
                        sp.wait_ge(parts_k, u.k + 1)
                        if s.kind_of == "k":
                            store(dk3[:, :, u.u * 256:(u.u + 1) * 256], sk[:, u.k % 2], k_stored[u.k % 2])
                        else:
                            if u.g >= 2:
                                sp.wait_ge(k_packed[u.g % 2], u.packed_before)
                            store(scratch(dk, A, u.g), sk[:, u.k % 2], k_stored[u.k % 2])
                elif s.kind == "packs":
                    A, u = s.A, s.un
                    if s.done_before >= 0:
                        sp.wait_ge(PV_done, s.done_before + 1)
                    sp.wait_ge(q_stored[u.g % 2], 32 * (u.g // 2 + 1))
                    pack(sp, A, QP[:, u.g % 3, :], scratch(dq, A, u.g), A.T, q_packed[u.g % 2], is_q=True)
                    if u.k is not None:
                        sp.wait_ge(k_stored[u.k % 2], 32 * (u.k // 2 + 1))
                        pack(sp, A, KP[:, 4096 * (u.g % 3):4096 * (u.g % 3 + 1)], scratch(dk, A, u.g), A.T,
                             k_packed[u.g % 2], is_q=False)
                elif s.kind == "negmax":
                    A = s.A
                    turn(sp, bank_used, s.m)
                    for p3 in range(3):
                        r = 96 + p3
                        sp.dma_start(QP[r:r + 1, s.un.g % 3, 0:A.H * A.T],
                                     nmT[p3 * A.H:(p3 + 1) * A.H, s.i % 2, 0:A.T]).then_inc(neg_in[s.i % 2], 16)
                elif s.kind == "ext":
                    e = s.i
                    if e == 0:
                        sp.wait_ge(scattered, 16 * NB)
                    for k in [0, 1] if e == 0 else ([e + 1] if e + 1 < 8 else []):
                        if k >= 2:
                            turn(sp, bank_ready, ext_m[k - 2])
                        sp.dma_start(xe[:, k % 2, 0:256], xd[k * P:(k + 1) * P, :]).then_inc(xe_in[k % 2], 16)
                elif s.kind == "w3first":
                    sp.wait_ge(w_in[0], 16 * 7)
                    sp.sem_inc(experts_in, 16)
                    sp.wait_ge(PV_done, s.p + 1)
                    sp.dma_start(whole[:, SLOTW:2 * SLOTW], t["w13"]).then_inc(experts_in, 16)
                elif s.kind == "sx_load":
                    sp.wait_ge(experts_in, 32)
                    sp.dma_start(whole[:, 2 * SLOTW:3 * SLOTW], t["w14"]).then_inc(experts_in, 16)
                    sp.wait_ge(experts_in, 48)
                    sp.dma_start(whole[:, 3 * SLOTW:4 * SLOTW], t["w15"]).then_inc(experts_in, 16)
                elif s.kind == "combine3":
                    sp.wait_ge(combined3, s.b + 1)
                    sp.dma_start(out[s.b], x[:, s.b, :]).then_inc(out_done, 16)
                elif s.kind == "exd":
                    e = s.i
                    turn(sp, bank_used, s.s)
                    sp.dma_start(eod[e * P:(e + 1) * P, :], eo[:, e % 2, :]).then_inc(eo_out[e % 2], 16)
            sp.wait_ge(out_done, 16 * NB)

        @block.tensor
        def _(pe):
            ident = const("ident")

            def m_begin(n):
                free(pe, bank_used, n)
                return m_slot(n)

            def project(dst, lhs, rhs, halves):
                for kd in range(halves):
                    ins = pe.matmul(dst, lhsT=lhs(kd), rhs=rhs(kd), start=(kd == 0), stop=(kd == halves - 1))
                return ins

            def turn_x(n, xs):
                dst = m_begin(n)
                pe.wait_ge(xn_ready, xs.i + 1)
                for kd in range(2):
                    ins = pe.transpose(dst[:, kd * P:(kd + 1) * P], xn[:, xs.b, kd * P:(kd + 1) * P], ident)
                ins.then_inc(bank_ready[n % BANKS], 1)

            w_seen = set()

            def weights(item):
                if item not in w_seen:
                    w_seen.add(item)
                    pe.wait_ge(w_in[item % 2], 16 * (item // 2 + 1))

            pe.wait_ge(const_in, 16 * 10)
            for s in steps:
                if s.kind == "barrier":
                    pe.wait_ge(rstd_ready, s.stats)
                elif s.kind == "attn_begin":
                    if s.A.layer == 2:
                        pe.wait_ge(w3_in, 32)
                    if s.A.layer == 3:
                        pe.wait_ge(w3_in, 48)
                        pe.wait_ge(v3_in, 16)
                    if s.A.has_max:
                        pe.wait_ge(k_ones, 64 * {0: 1, 1: 2, 3: 3}[s.A.layer])
                elif s.kind == "kp":
                    dst = m_begin(s.m)
                    if s.u == 0 and s.j == 0:
                        pe.wait_ge(w3_in, 16)
                    tok = (2 * s.u + s.j) * P
                    project(dst, lambda kd: ctx_t[:, kd, tok:tok + P], lambda kd: w_at2[:, 1, kd, :], 2
                            ).then_inc(bank_ready[s.m % BANKS], 1)
                elif s.kind in ("kt", "fqt"):
                    dst = m_begin(s.m)
                    pe.wait_ge(quant_q, s.i + 1)
                    for j in range(2):
                        ins = pe.transpose(dst[:, j * P:(j + 1) * P], tmp2[:, j * 256 + s.c * P:j * 256 + (s.c + 1) * P], ident)
                    ins.then_inc(bank_ready[s.m % BANKS], 1)
                elif s.kind == "vp":
                    dst = m_begin(s.m)
                    tok = 2 * s.u * P
                    project(dst, lambda kd: w_at2[:, 2, kd, s.c * P:(s.c + 1) * P],
                            lambda kd: ctx_t[:, kd, tok:tok + 256], 2).then_inc(bank_ready[s.m % BANKS], 1)
                elif s.kind == "vturn":
                    dst = m_begin(s.m).bitcast(BF16)
                    pe.wait_ge(v_quant, 2)
                    for m in range(2):
                        ins = pe.transpose(dst[:, m * P:(m + 1) * P], vi[:, m, s.c * P:(s.c + 1) * P], ident16[:, :])
                    ins.then_inc(bank_ready[s.m % BANKS], 1)
                elif s.kind in ("fx", "xt"):
                    turn_x(s.m, s.xn)
                elif s.kind in ("fq", "fk") and s.A.layer == 0:
                    dst = m_begin(s.m)
                    if s.kind == "fq":
                        pe.wait_ge(xn_ready, s.un.xn.i + 1)
                    k, src = (0, xn) if s.kind == "fq" else (1, ctx_s)
                    pe.matmul(dst, lhsT=w_at0[:, k, :], rhs=src[:, s.un.u, :], start=True, stop=True
                              ).then_inc(bank_ready[s.m % BANKS], 1)
                elif s.kind == "fv" and s.A.layer == 0:
                    dst = m_begin(s.m)
                    for c in range(2):
                        ins = pe.matmul(dst[:, c * P:(c + 1) * P], lhsT=ctx_s[:, s.un.u, c * P:(c + 1) * P],
                                        rhs=w_at0[:, 2, :], start=True, stop=True)
                    ins.then_inc(bank_ready[s.m % BANKS], 1)
                elif s.kind in ("fq", "fk"):
                    dst = m_begin(s.m)
                    k, src = (0, xn_t) if s.kind == "fq" else (1, ctx_t)
                    if k == 0:
                        evacuated(pe, s.un.m_x)
                    tok = s.un.u * P
                    for m in range(2):
                        ins = project(dst[:, m * P:(m + 1) * P], lambda kd: w_at2[:, k, kd, m * P:(m + 1) * P],
                                      lambda kd: src[:, kd, tok:tok + P], 2)
                    ins.then_inc(bank_ready[s.m % BANKS], 1)
                elif s.kind == "fv":
                    dst = m_begin(s.m)
                    tok = s.un.u * P
                    project(dst, lambda kd: ctx_t[:, kd, tok:tok + P], lambda kd: w_at2[:, 2, kd, :], 2
                            ).then_inc(bank_ready[s.m % BANKS], 1)
                elif s.kind == "fq3":
                    dst = m_begin(s.m)
                    evacuated(pe, s.m_prev)
                    tok = (2 * s.un.u + s.j) * P
                    project(dst, lambda kd: xn_t[:, kd, tok:tok + P], lambda kd: w_at2[:, 0, kd, :], 2
                            ).then_inc(bank_ready[s.m % BANKS], 1)
                elif s.kind == "smax":
                    A, u, K = s.A, s.un, 96
                    if s.first:
                        wait_packs(pe, s)
                    free(pe, bank_used, s.n)
                    dst = psB[:, s.n % BANKS, :]
                    q_at, k_at = QP[0:K, u.g % 3, :], kslot(A, u)[0:K, :]
                    if A.layer == 3:
                        h, half = s.j // 2, s.j % 2
                        ins = pe.matmul(dst, lhsT=q_at[:, h * A.T + s.tc * P:h * A.T + (s.tc + 1) * P],
                                        rhs=k_at[:, h * NT + half * 512:h * NT + (half + 1) * 512],
                                        start=True, stop=True)
                    else:
                        for i in range(2):
                            h = 2 * s.j + i
                            ins = pe.matmul(dst[:, i * 256:(i + 1) * 256],
                                            lhsT=q_at[:, h * A.T + s.tc * P:h * A.T + (s.tc + 1) * P],
                                            rhs=k_at[:, h * A.T:(h + 1) * A.T], start=True, stop=True)
                    ins.then_inc(bank_ready[s.n % BANKS], 1)
                elif s.kind == "negmax":
                    A = s.A
                    dst = m_begin(s.m).bitcast(BF16)
                    pe.wait_ge(neg_split, s.i + 1)
                    w = 3 * A.H
                    for tc in range(A.TC):
                        ins = pe.transpose(dst[0:w, tc * P:(tc + 1) * P], npt[:, s.i % 2, tc * w:(tc + 1) * w],
                                           ident16[:, :])
                    ins.then_inc(bank_ready[s.m % BANKS], 1)
                elif s.kind == "st":
                    A, u = s.A, s.un
                    K = 99 if A.has_max else 96
                    if s.first:
                        if A.has_max:
                            pe.wait_ge(neg_in[u.neg % 2], 48 * (u.neg // 2 + 1))
                        else:
                            wait_packs(pe, s)
                    free(pe, T_used, s.n)
                    q_at, k_at = QP[0:K, u.g % 3, :], kslot(A, u)[0:K, :]
                    kw = NT if A.layer == 3 else A.T if A.layer < 2 else P
                    for i in range(4):
                        h = 4 * s.g + i
                        ins = pe.matmul(psT[:, s.n % 2, i * A.T:(i + 1) * A.T],
                                        lhsT=k_at[:, h * kw + s.c * P:h * kw + (s.c + 1) * P],
                                        rhs=q_at[:, h * A.T:(h + 1) * A.T], start=True, stop=True)
                    ins.then_inc(T_ready[s.n % 2], 1)
                elif s.kind == "pv":
                    A, u = s.A, s.un
                    if A.layer == 2:
                        pe.wait_ge(exp_done, s.clip + 1)
                    else:
                        turn(pe, T_used, s.n)
                    if A.layer == 3:
                        pe.wait_ge(rounded, s.clip3 + 1)
                    if s.g == 0 and s.c == 0:
                        if A.layer == 0:
                            evacuated(pe, u.m_v)
                        elif A.layer == 1:
                            pe.wait_ge(V_copied, u.u + 1)
                        elif A.layer == 2:
                            evacuated(pe, u.m_v)
                    if s.c == 0 and s.o >= 1:
                        turn(pe, O_used, s.o - 1)
                    for i in range(4):
                        h = 4 * s.g + i
                        dst = psO[32 * i:32 * (i + 1), s.o % 2, 0:A.T]
                        pr = Pt[:, s.p % 3, i * A.T:(i + 1) * A.T]
                        first, last = s.c == 0, s.c == A.NC - 1
                        if A.layer < 3:
                            ins = pe.matmul(dst, lhsT=VA[:, u.g % 3, s.c * A.H + h, :], rhs=pr, start=first, stop=last)
                        else:
                            pe.matmul(dst, lhsT=VQ[:, s.c * A.H + h, :], rhs=nb16[:, s.p % 2, i * A.T:(i + 1) * A.T],
                                      start=first, stop=False)
                    if A.layer == 3:
                        for i in range(4):
                            dst = psO[32 * i:32 * (i + 1), s.o % 2, 0:A.T]
                            pr = Pt[:, s.p % 3, i * A.T:(i + 1) * A.T]
                            ins = pe.matmul(dst, lhsT=const("sumsel"), rhs=pr, start=False, stop=last)
                    ins.then_inc(PV_done, 1)
                elif s.kind == "onorm":
                    A = s.A
                    turn(pe, O_used, s.o)
                    dst = m_begin(s.m)
                    for tc in range(A.TC):
                        ins = pe.transpose(dst[:, tc * P:(tc + 1) * P], Oe[:, s.o % 2, tc * P:(tc + 1) * P], ident)
                    ins.then_inc(bank_ready[s.m % BANKS], 1)
                elif s.kind == "ot":
                    A, u = s.A, s.un
                    dst = m_begin(s.m)
                    evacuated(pe, s.m_last_norm)
                    HD = A.H * A.d
                    for j in range(2):
                        at = j * P if A.layer == 2 else j * HD + s.c * P
                        ins = pe.transpose(dst[:, j * P:(j + 1) * P], On[:, u.g % 2, at:at + P], ident)
                    ins.then_inc(bank_ready[s.m % BANKS], 1)
                elif s.kind == "oy":
                    A = s.A
                    dst = m_begin(s.m)
                    for m in s.un.m_t:
                        evacuated(pe, m)
                    if A.layer == 0:
                        ins = pe.matmul(dst, lhsT=w_at0[:, 3, :], rhs=OnT[:, 0, :], start=True, stop=True)
                    elif A.layer == 2:
                        ins = project(dst, lambda m: OnT[:, 0, m * P:(m + 1) * P], lambda m: w_at2[:, 3, m, :], 2)
                    else:
                        ins = project(dst, lambda m: OnT[:, m, s.j * P:(s.j + 1) * P], lambda m: w_at2[:, 3, m, :], 2)
                    ins.then_inc(bank_ready[s.m % BANKS], 1)
                elif s.kind == "xl":
                    dst = m_begin(s.m)
                    evacuated(pe, s.m_prev)
                    a, n = {0: (0, 8), 2: (8, 16), 3: (24, 4)}[s.layer]
                    tok = s.b * P
                    project(dst[:, 0:n], lambda kd: xn_t[:, kd, tok:tok + P], lambda kd: wr[:, kd, a:a + n], 2
                            ).then_inc(bank_ready[s.m % BANKS], 1)
                elif s.kind == "route" and s.layer == 0:
                    dst = m_begin(s.m)
                    pe.wait_ge(route_pe, 1)
                    pe.matmul(dst[:, 0:64], lhsT=const("before"), rhs=oh[:, :, 0:8], start=True, stop=False)
                    pe.matmul(dst[:, 0:64], lhsT=const("ones"), rhs=rc[:, :, 0:8], start=False, stop=True
                              ).then_inc(bank_ready[s.m % BANKS], 1)
                elif s.kind == "route" and s.layer == 3:
                    dst = m_begin(s.m)
                    pe.wait_ge(route_pe, 2)
                    pe.matmul(dst[:, 0:32], lhsT=const("before"), rhs=oh[:, :, 0:4], start=True, stop=False)
                    pe.matmul(dst[:, 0:32], lhsT=const("ones"), rhs=rc[:, :, 0:4], start=False, stop=True)
                    pe.matmul(dst[:, 32:36], lhsT=const("ones"), rhs=rc[:, 0, 8:12], start=True, stop=True
                              ).then_inc(bank_ready[s.m % BANKS], 1)
                elif s.kind == "sx":
                    dst = m_begin(s.m)
                    pe.wait_ge(sorted_in[s.i % 4], 16 * (s.i // 4 + 1))
                    for kd in range(2):
                        ins = pe.transpose(dst[:, kd * P:(kd + 1) * P], sx[:, s.i % 4, kd * P:(kd + 1) * P], ident)
                    ins.then_inc(bank_ready[s.m % BANKS], 1)
                elif s.kind == "su":
                    if s.j == 0:
                        if s.i == 0:
                            pe.wait_ge(routed3, 1)
                        s.un.k = pe.value_load(te[0:1, s.i:s.i + 1], min_val=0, max_val=3)
                        pe.wait_ge(experts_in, s.un.k * 16 + 16)
                        evacuated(pe, s.m_x)
                    free(pe, T_used, s.n)
                    for k in range(2):
                        for kd in range(2):
                            at = k * 2048 + kd * 1024 + s.j * 512
                            ins = pe.matmul(psT[:, s.n % 2, k * 512:(k + 1) * 512], lhsT=xeT[:, s.i % 2, kd, :],
                                            rhs=whole[:, bass.ds(s.un.k * SLOTW + at, 512)], start=(kd == 0), stop=(kd == 1))
                    ins.then_inc(T_ready[s.n % 2], 1)
                elif s.kind == "sh":
                    free(pe, bank_used, s.m)
                    pe.wait_ge(hidden3, s.g + 1)
                    for c in range(4):
                        ins = pe.transpose(psB[:, s.m % BANKS, c * P:(c + 1) * P], htok[:, s.g % 2, c * P:(c + 1) * P], ident)
                    ins.then_inc(bank_ready[s.m % BANKS], 1)
                elif s.kind == "sd":
                    free(pe, bank_used, s.s)
                    for m in s.un.m:
                        evacuated(pe, m)
                    for c in range(8):
                        ins = pe.matmul(m_slot(s.s), lhsT=hT[:, s.i % 2, c * P:(c + 1) * P],
                                        rhs=whole[:, bass.ds(s.un.k * SLOTW + 4096 + c * 256, 256)],
                                        start=(c == 0), stop=(c == 7))
                    ins.then_inc(bank_ready[s.s % BANKS], 1)
                elif s.kind == "ext":
                    e = s.i
                    dst = m_begin(s.m)
                    pe.wait_ge(xe_in[e % 2], 16 * (e // 2 + 1))
                    for kd in range(2):
                        ins = pe.transpose(dst[:, kd * P:(kd + 1) * P], xe[:, e % 2, kd * P:(kd + 1) * P], ident)
                    ins.then_inc(bank_ready[s.m % BANKS], 1)
                elif s.kind == "exu":
                    e, W = s.i, Wslot[s.i % 2]
                    weights(e)
                    free(pe, T_used, s.n)
                    evacuated(pe, s.m)
                    for ch in range(8):
                        ins = project(psT[:, s.n % 2, ch * P:(ch + 1) * P],
                                      lambda kd: W[:, kd * 1024 + ch * P:kd * 1024 + (ch + 1) * P],
                                      lambda kd: xeT[:, e % 2, kd, :], 2)
                    ins.then_inc(T_ready[s.n % 2], 1)
                elif s.kind == "exd":
                    e, W = s.i, Wslot[s.i % 2]
                    free(pe, bank_used, s.s)
                    turn(pe, T_used, s.n)
                    for ch in range(8):
                        ins = pe.matmul(psB[:, s.s % BANKS, 0:256], lhsT=Pt[:, e % 2, ch * P:(ch + 1) * P],
                                        rhs=W[:, 2048 + ch * 256:2048 + (ch + 1) * 256], start=(ch == 0), stop=(ch == 7))
                    ins.then_inc(bank_ready[s.s % BANKS], 1)
                elif s.kind == "gu":
                    W, F, ch, w = Wslot[s.blk.item % 2], s.blk.F, s.ch, s.width
                    weights(s.blk.item)
                    if s.ch == 0:
                        evacuated(pe, s.m)
                    free(pe, T_used, s.n)
                    for k in range(2):
                        at = s.blk.off + k * 2 * F + ch * P
                        ins = project(psT[0:w, s.n % 2, k * 512:(k + 1) * 512],
                                      lambda kd: W[:, at + kd * F:at + kd * F + w],
                                      lambda kd: xn_t[:, kd, s.tg * 512:(s.tg + 1) * 512], 2)
                    ins.then_inc(T_ready[s.n % 2], 1)
                elif s.kind == "down":
                    W, off = Wslot[s.blk.item % 2], s.blk.off + 4 * s.blk.F
                    free(pe, bank_used, s.n)
                    if s.tc == 0:
                        turn(pe, T_used, s.last_T)
                        if s.last_T >= 1:
                            turn(pe, T_used, s.last_T - 1)
                    last = len(s.blk.widths) - 1
                    for ch, w in enumerate(s.blk.widths):
                        ins = pe.matmul(psB[:, s.n % BANKS, 0:256], lhsT=Hb[0:w, s.h % 2, ch, s.tc * P:(s.tc + 1) * P],
                                        rhs=W[0:w, off + ch * 256:off + (ch + 1) * 256], start=(ch == 0), stop=(ch == last))
                    ins.then_inc(bank_ready[s.n % BANKS], 1)

        @block.scalar
        def _(act):
            act.wait_ge(const_in, 16 * 10)
            act.activation(tg[:, 0:8], rows[:, 0:8], ACT.Tanh).then_inc(gates_done, 1)
            act.wait_ge(gates_done, 4)
            for s in steps:
                if s.kind == "barrier":
                    act.wait_ge(rstd_ready, s.stats)
                elif s.kind == "kt":
                    if s.un.k >= 2:
                        act.wait_ge(parts_k, s.un.k - 1)
                    turn(act, bank_ready, s.m)
                    act.activation(kf[:, s.un.k % 2, s.c * 256:(s.c + 1) * 256], m_slot(s.m), ACT.Copy
                                   ).then_inc(bank_used[s.m % BANKS], 1)
                elif s.kind == "vp":
                    turn(act, bank_ready, s.m)
                    act.activation(vf[:, s.c, s.u * 256:(s.u + 1) * 256], m_slot(s.m), ACT.Identity,
                                   bias=col("bv3", s.c)).then_inc(bank_used[s.m % BANKS], 1)
                elif s.kind in ("fx", "xt"):
                    b = s.xn.b
                    turn(act, bank_ready, s.m)
                    act.activation(xn_t[:, :, b * P:(b + 1) * P], m_slot(s.m).rearrange("p (k n) -> p k n", k=2),
                                   ACT.Copy).then_inc(bank_used[s.m % BANKS], 1)
                elif s.kind in ("fq", "fk"):
                    A, is_q = s.A, s.kind == "fq"
                    i = s.un.g if is_q else s.un.k
                    if i >= 2:
                        act.wait_ge(parts_q if is_q else parts_k, i - 1)
                    dst = (qf if is_q else kf)[:, i % 2, :]
                    scale = float(A.d) ** -0.5 if is_q else 1.0
                    turn(act, bank_ready, s.m)
                    if A.layer == 0:
                        ins = act.activation(dst[:, 0:256], m_slot(s.m), ACT.Identity, scale=scale,
                                             bias=colx[:, 0:1] if is_q else col("bk0"))
                    else:
                        for m in range(2):
                            ins = act.activation(dst[:, m * P:(m + 1) * P], m_slot(s.m)[:, m * P:(m + 1) * P],
                                                 ACT.Identity, scale=scale,
                                                 bias=colx[:, 1 + m:2 + m] if is_q else col("bk2", m))
                    ins.then_inc(bank_used[s.m % BANKS], 1)
                elif s.kind == "fqt":
                    if s.un.g >= 2:
                        act.wait_ge(parts_q, s.un.g - 1)
                    turn(act, bank_ready, s.m)
                    act.activation(qf[:, s.un.g % 2, s.c * 256:(s.c + 1) * 256], m_slot(s.m), ACT.Copy
                                   ).then_inc(bank_used[s.m % BANKS], 1)
                elif s.kind == "negmax":
                    A = s.A
                    turn(act, bank_ready, s.m)
                    if s.i >= 2:
                        act.wait_ge(neg_in[s.i % 2], 48 * (s.i // 2))
                    act.activation(nmT[0:3 * A.H, s.i % 2, 0:A.T], m_slot(s.m).bitcast(BF16)[0:3 * A.H, 0:A.T],
                                   ACT.Copy).then_inc(bank_used[s.m % BANKS], 1)
                elif s.kind == "st":
                    A = s.A
                    if s.p >= 3:
                        act.wait_ge(PV_done, s.p - 2)
                    if A.layer == 2:
                        b = s.un.u
                        act.wait_ge(clipped, s.clip + 1)
                        act.activation(Pt[:, s.p % 3, 0:512], nb_t[:, s.clip % 2, :], ACT.Exp,
                                       bias=att_b[:, b:b + 1], scale=att[:, b:b + 1]).then_inc(exp_done, 1)
                    else:
                        turn(act, T_ready, s.n)
                        act.activation(Pt[:, s.p % 3, :], psT[:, s.n % 2, :], ACT.Exp).then_inc(T_used[s.n % 2], 1)
                elif s.kind == "oev":
                    A = s.A
                    act.wait_ge(PV_done, s.p + 1)
                    if s.m_prev2 is not None:
                        turn(act, bank_ready, s.m_prev2)
                    act.activation(Oe[:, s.o % 2, 0:A.T], psO[:, s.o % 2, 0:A.T], ACT.Copy).then_inc(O_used[s.o % 2], 1)
                elif s.kind == "ot" and s.A.layer != 1:
                    turn(act, bank_ready, s.m)
                    if s.m_prev is not None:
                        turn(act, bank_ready, s.m_prev)
                    scale = vs[:, 0, s.c:s.c + 1] if s.A.layer == 3 else 1.0
                    act.activation(OnT[:, s.c, :], m_slot(s.m), ACT.Copy, scale=scale).then_inc(bank_used[s.m % BANKS], 1)
                elif s.kind == "route":
                    act.wait_ge(route_a, s.exp_i + 1)
                    n = {0: 8, 2: 16, 3: 4}[s.layer]
                    act.activation(ra[:, :, 0:n], ra[:, :, 0:n], ACT.Exp, scale=-1.0 if s.layer == 2 else 1.0
                                   ).then_inc(route_b, 1)
                elif s.kind == "ext":
                    e = s.i
                    turn(act, bank_ready, s.m)
                    act.activation(xeT[:, e % 2, :, :], m_slot(s.m).rearrange("p (k n) -> p k n", k=2), ACT.Copy
                                   ).then_inc(bank_used[s.m % BANKS], 1)
                elif s.kind == "sx_load":
                    act.wait_ge(scattered3, 16 * NB)
                    for i in range(4):
                        act.dma_start(sx[:, i, :], sxd[i * P:(i + 1) * P, :]).then_inc(sorted_in[i], 16)
                elif s.kind == "sx":
                    turn(act, bank_ready, s.m)
                    act.activation(xeT[:, s.i % 2, :, :], m_slot(s.m).rearrange("p (k n) -> p k n", k=2), ACT.Copy
                                   ).then_inc(bank_used[s.m % BANKS], 1)
                    if s.i + 4 < TILES3:
                        act.dma_start(sx[:, s.i % 4, :], sxd[(s.i + 4) * P:(s.i + 5) * P, :]).then_inc(sorted_in[s.i % 4], 16)
                elif s.kind == "su":
                    turn(act, T_ready, s.n)
                    act.activation(sg[:, s.sg % 2, :], psT[:, s.n % 2, 0:512], ACT.Silu).then_inc(silu_done, 1)
                elif s.kind == "sh":
                    turn(act, bank_ready, s.m)
                    if s.m_prev is not None:
                        turn(act, bank_ready, s.m_prev)
                    act.activation(hT[:, s.i % 2, s.j * 512:(s.j + 1) * 512], psB[:, s.m % BANKS, :], ACT.Copy
                                   ).then_inc(bank_used[s.m % BANKS], 1)
                elif s.kind == "sd":
                    turn(act, bank_used, s.s)
                    act.dma_start(sod[s.i * P:(s.i + 1) * P, :], so[:, s.i % 4, :]).then_inc(sorted_out[s.i % 4], 16)
                elif s.kind == "exu":
                    turn(act, T_ready, s.n)
                    act.activation(Pt[:, s.i % 2, :], psT[:, s.n % 2, :], ACT.Gelu_apprx_tanh
                                   ).then_inc(T_used[s.n % 2], 1)
                elif s.kind == "gu":
                    w = s.width
                    turn(act, T_ready, s.n)
                    sc = col("gs1", s.ch, w) if s.layer == 1 else 1.0
                    act.activation(sg[0:w, s.sg % 2, :], psT[0:w, s.n % 2, 0:512], ACT.Silu, scale=sc
                                   ).then_inc(silu_done, 1)

        @block.vector
        def _(dve):
            chained = [0]

            def link(ins):
                chained[0] += 1
                ins.then_inc(dve_chain, 1)
                dve.wait_ge(dve_chain, chained[0])

            def normalise(xs):
                dve.wait_ge(rstd_ready, xs.stat + 1)
                dve.tensor_scalar(xn[:, xs.b, :], x[:, xs.b, :], mv[:, xs.b, 0:1], rstd[:, xs.b:xs.b + 1],
                                  ALU.subtract, ALU.mult).then_inc(xn_ready, 1)

            def bc(ap, shape):
                return ap.to_broadcast(shape)

            def quantise(src, dst, H, n):
                s4 = src.rearrange("p (j d h) -> p j h d", j=n, h=H)
                scale = qs[:, 0, 0:n * H].rearrange("p (j h) -> p j h", j=n)
                link(dve.tensor_reduce(scale, s4, AX.X, ALU.max, apply_absolute_value=True))
                link(dve.tensor_scalar(qs[:, 1, 0:n * H], qs[:, 0, 0:n * H], 1.0 / 127.0, 1e-8, ALU.mult, ALU.max))
                link(dve.reciprocal(qs[:, 2, 0:n * H], qs[:, 1, 0:n * H]))
                for j in range(n):
                    v = src[:, j * 256:(j + 1) * 256].rearrange("p (d h) -> p d h", h=H)
                    o = dst[:, j * 256:(j + 1) * 256].rearrange("p (d h) -> p d h", h=H)
                    r = qs[:, 2, j * H:(j + 1) * H].rearrange("p (o h) -> p o h", o=1)
                    ins = dve.tensor_tensor(o, v, r.to_broadcast([P, 16, H]), ALU.mult)
                link(ins)
                link(dve.tensor_scalar(dst, dst, MAGIC, MAGIC, ALU.add, ALU.subtract))
                for j in range(n):
                    o = dst[:, j * 256:(j + 1) * 256].rearrange("p (d h) -> p d h", h=H)
                    r = qs[:, 1, j * H:(j + 1) * H].rearrange("p (o h) -> p o h", o=1)
                    ins = dve.tensor_tensor(o, o, r.to_broadcast([P, 16, H]), ALU.mult)
                ins.then_inc(quant_q, 1)

            def first_max(src, E, onehot):
                link(dve.tensor_reduce(r8[:, 0, :], src, AX.X, ALU.max))
                mx = r8[:, 0, :].unsqueeze(2).to_broadcast([P, NB, E])
                link(dve.tensor_tensor(rb[:, :, 0:E], src, mx, ALU.is_equal))
                desc = const("desc")[:, 0:E].unsqueeze(1).to_broadcast([P, NB, E])
                link(dve.tensor_tensor(rb[:, :, 0:E], rb[:, :, 0:E], desc, ALU.mult))
                link(dve.tensor_reduce(r8[:, 1, :], rb[:, :, 0:E], AX.X, ALU.max))
                m2 = r8[:, 1, :].unsqueeze(2).to_broadcast([P, NB, E])
                link(dve.tensor_tensor(onehot, rb[:, :, 0:E], m2, ALU.is_equal))

            link(dve.memset(On[:, :, :], 0.0))
            dve.memset(rem[:, 0:1], 0.0).then_inc(zeros_made, 1)
            link(dve.memset(VA[:, :, :, :], 0.0))
            link(dve.memset(VA[:, :, :, SUMCOL:SUMCOL + 1], 1.0))
            dve.memset(arena[32:64, 0:6144], 0.0).then_inc(memset_done, 1)
            dve.memset(arena[64:96, 0:6144], 0.0).then_inc(memset_done, 1)
            dve.wait_ge(const_in, 16 * 10)
            dve.tensor_scalar(colx[:, 0:1], col("bq0"), float(ATT[0].d) ** -0.5, None, ALU.mult).then_inc(gates_done, 1)
            dve.tensor_scalar(colx[:, 1:3], cols[:, col_at["bq2"][0]:col_at["bq2"][1]], float(ATT[2].d) ** -0.5, None,
                              ALU.mult).then_inc(gates_done, 1)
            dve.tensor_scalar(att[:, :], mask_i[:, :], 0.5, None, ALU.is_gt).then_inc(gates_done, 1)
            dve.wait_ge(gates_done, 4)
            link(dve.tensor_scalar(att_b[:, :], att[:, :], 50.0, -50.0, ALU.mult, ALU.add))
            link(dve.tensor_scalar(tg[:, 8:9], row("gamma"), tg[:, 1:2], None, ALU.mult))
            link(dve.tensor_scalar(tg[:, 9:10], row("rscale"), 0.0, 0.3, ALU.max, ALU.min))
            link(dve.tensor_scalar(tg[:, 10:11], tg[:, 6:7], 0.1, None, ALU.mult))
            dve.wait_ge(x_in, 16)
            for s in steps:
                if s.kind == "barrier":
                    dve.wait_ge(rstd_ready, s.stats)
                elif s.kind == "stats":
                    b = s.b
                    if s.after is not None:
                        for i in range(BANKS):
                            if s.after[i]:
                                dve.wait_ge(bank_used[i], s.after[i])
                    link(dve.bn_stats(st6[:, :], x[:, b, :]))
                    link(dve.bn_aggr(mv[:, b, :], st6[:, :]))
                    dve.tensor_scalar(vare[:, b:b + 1], mv[:, b, 1:2], EPS, None, ALU.add).then_inc(var_ready, 1)
                elif s.kind == "kp":
                    turn(dve, bank_ready, s.m)
                    dve.tensor_tensor(tmp[:, s.j * 256:(s.j + 1) * 256], m_slot(s.m), row("bk3"), ALU.add
                                      ).then_inc(bank_used[s.m % BANKS], 1)
                elif s.kind == "fq3":
                    turn(dve, bank_ready, s.m)
                    dve.tensor_tensor(tmp[:, s.j * 256:(s.j + 1) * 256], m_slot(s.m), row("bq3"), ALU.add
                                      ).then_inc(bank_used[s.m % BANKS], 1)
                elif s.kind == "quant":
                    if s.prev_m is not None:
                        turn(dve, bank_ready, s.prev_m)
                    for m in s.un.m_v:
                        evacuated(dve, m)
                    if s.s:
                        link(dve.tensor_scalar(tmp[:, 0:512], tmp[:, 0:512], 0.25, None, ALU.mult))
                    quantise(tmp[:, 0:512], tmp2[:, 0:512], 16, 2)
                elif s.kind == "vscale":
                    evacuated(dve, s.last_m)
                    link(dve.tensor_reduce(vs[:, 2, :], vf[:, :, :], AX.X, ALU.max, apply_absolute_value=True))
                    link(dve.tensor_scalar(vs[:, 0, :], vs[:, 2, :], 1.0 / 127.0, 1e-8, ALU.mult, ALU.max))
                    link(dve.reciprocal(vs[:, 1, :], vs[:, 0, :]))
                    for m in range(2):
                        ins = dve.tensor_scalar(vr[:, m, :], vf[:, m, :], vs[:, 1, m:m + 1], MAGIC, ALU.mult, ALU.add)
                    link(ins)
                    dve.tensor_scalar(vi[:, :, :], vr[:, :, :], MAGIC, None, ALU.subtract).then_inc(v_quant, 1)
                    dve.memset(VQ_made[:, :, :], 0.0).then_inc(v_quant, 1)
                    dve.wait_ge(v_quant, 2)
                elif s.kind == "vturn":
                    turn(dve, bank_ready, s.m)
                    src = m_slot(s.m).bitcast(BF16)[:, 0:256].rearrange("p (h d) -> p h d", d=16)
                    dve.tensor_copy(VQ_made[:, s.c * 16:(s.c + 1) * 16, 0:16], src).then_inc(bank_used[s.m % BANKS], 1)
                elif s.kind in ("fn", "fx", "xt"):
                    normalise(s.xn)
                elif s.kind == "fv":
                    A, n = s.A, s.m
                    turn(dve, bank_ready, n)
                    if s.done_before >= 0:
                        dve.wait_ge(PV_done, s.done_before + 1)
                    if A.layer == 0:
                        for c in range(2):
                            ins = dve.tensor_tensor(VA[:, s.un.g % 3, c * 16:(c + 1) * 16, 0:8],
                                                    m_slot(n)[:, c * P:(c + 1) * P].rearrange("p (h d) -> p h d", d=8),
                                                    row("bv0").rearrange("p (h d) -> p h d", d=8), ALU.add)
                    else:
                        ins = dve.tensor_tensor(VA[:, s.un.g % 3, 0:16, 0:16],
                                                m_slot(n).rearrange("p (h d) -> p h d", d=16),
                                                row("bv2").rearrange("p (h d) -> p h d", d=16), ALU.add)
                    ins.then_inc(bank_used[n % BANKS], 1)
                elif s.kind == "smax":
                    A = s.A
                    turn(dve, bank_ready, s.n)
                    if A.layer == 3:
                        at = s.tc * 32 + s.j
                        dve.tensor_reduce(mxp[:, s.un.g % 2, at:at + 1], psB[:, s.n % BANKS, :], AX.X, ALU.max
                                          ).then_inc(bank_used[s.n % BANKS], 1)
                    else:
                        at = s.tc * A.H + 2 * s.j
                        dve.tensor_reduce(mxp[:, s.un.g % 2, at:at + 2],
                                          psB[:, s.n % BANKS, :].rearrange("p (h n) -> p h n", h=2), AX.X, ALU.max
                                          ).then_inc(bank_used[s.n % BANKS], 1)
                elif s.kind == "negsplit":
                    A, w = s.A, s.A.TC * s.A.H
                    turn(dve, bank_used, s.un.last_S)
                    mx = mxp[:, s.un.g % 2, 0:w]
                    if A.layer == 3:
                        link(dve.tensor_reduce(nm[:, 1, 0:w], mxp[:, s.un.g % 2, :].rearrange("p (h n) -> p h n", n=2),
                                               AX.X, ALU.max))
                        mx = nm[:, 1, 0:w]
                    link(dve.tensor_scalar(nm[:, 0, 0:w], mx, -1.0, LN255 if A.layer == 3 else 0.0, ALU.mult, ALU.add))
                    if s.m_prev2 is not None:
                        turn(dve, bank_ready, s.m_prev2)
                    part = npt[:, s.i % 2, 0:3 * w].rearrange("p (t c h) -> p c t h", t=A.TC, c=3)
                    src = nm[:, 0, 0:w].rearrange("p (t h) -> p t h", t=A.TC)
                    left = nm[:, 1, 0:w].rearrange("p (t h) -> p t h", t=A.TC)
                    link(dve.tensor_copy(part[:, 0], src))
                    link(dve.tensor_tensor(left, src, part[:, 0], ALU.subtract))
                    link(dve.tensor_copy(part[:, 1], left))
                    dve.tensor_tensor(part[:, 2], left, part[:, 1], ALU.subtract).then_inc(neg_split, 1)
                elif s.kind == "st" and s.A.layer == 2:
                    turn(dve, T_ready, s.n)
                    if s.clip >= 2:
                        dve.wait_ge(exp_done, s.clip - 1)
                    dve.tensor_scalar(nb_t[:, s.clip % 2, :], psT[:, s.n % 2, 0:512], 50.0, -50.0, ALU.min, ALU.max
                                      ).then_inc(T_used[s.n % 2], 1)
                    turn(dve, T_used, s.n)
                    dve.sem_inc(clipped, 1)
                elif s.kind == "round":
                    turn(dve, T_used, s.n)
                    if s.p >= 2:
                        dve.wait_ge(PV_done, s.p - 1)
                    dve.tensor_scalar(nb16[:, s.p % 2, :], Pt[:, s.p % 3, :], MAGIC, MAGIC, ALU.add, ALU.subtract
                                      ).then_inc(rounded, 1)
                elif s.kind == "onorm":
                    A = s.A
                    turn(dve, bank_ready, s.m)
                    if s.m_prev is not None:
                        evacuated(dve, s.m_prev)
                    src = m_slot(s.m)[:, 0:A.T].rearrange("p (t h e) -> p t h e", t=A.TC, h=4)
                    link(dve.reciprocal(rden[:, 0:A.TC, :].unsqueeze(3), src[:, :, :, SUMCOL:SUMCOL + 1]))
                    for tc in range(A.TC):
                        HD = A.H * A.d
                        dst = On[:, s.un.g % 2, tc * HD + s.g * 4 * A.d:tc * HD + (s.g + 1) * 4 * A.d]
                        ins = dve.tensor_tensor(dst.rearrange("p (h d) -> p h d", h=4), src[:, tc, :, 0:A.d],
                                                rden[:, tc, :].unsqueeze(2).to_broadcast([P, 4, A.d]), ALU.mult)
                    ins.then_inc(bank_used[s.m % BANKS], 1)
                elif s.kind == "ot" and s.A.layer == 1:
                    u = s.un.u
                    turn(dve, bank_ready, s.m)
                    dve.scalar_tensor_tensor(out=x[:, u, :], in0=m_slot(s.m), scalar=tg[:, 8:9],
                                             in1=x[:, u, :], op0=ALU.mult, op1=ALU.add).then_inc(bank_used[s.m % BANKS], 1)
                    evacuated(dve, s.m)
                elif s.kind == "oy":
                    A, u = s.A, s.un.u
                    turn(dve, bank_ready, s.m)
                    if A.layer == 0:
                        dve.tensor_scalar(y_t[:, :], m_slot(s.m), col("bo0"), tg[:, 0:1], ALU.add, ALU.mult
                                          ).then_inc(bank_used[s.m % BANKS], 1)
                        evacuated(dve, s.m)
                        link(dve.tensor_tensor(x[:, u, :], x[:, u, :], y_t[:, :], ALU.add))
                    elif A.layer == 2:
                        dve.tensor_tensor(y_t[:, :], m_slot(s.m), row("bo2"), ALU.add).then_inc(bank_used[s.m % BANKS], 1)
                        evacuated(dve, s.m)
                        link(dve.tensor_scalar(y_t[:, :], y_t[:, :], tg[:, 9:10], None, ALU.mult))
                        link(dve.bn_stats(st6[:, :], y_t[:, :]))
                        link(dve.bn_aggr(mv2[:, :], st6[:, :]))
                        dve.tensor_scalar(vare2[:, :], mv2[:, 1:2], EPS, None, ALU.add).then_inc(delta_var, 1)
                    else:
                        b = 2 * u + s.j
                        dve.tensor_tensor(y_t[:, :], m_slot(s.m), row("bp3"), ALU.add).then_inc(bank_used[s.m % BANKS], 1)
                        evacuated(dve, s.m)
                        link(dve.scalar_tensor_tensor(out=x[:, b, :], in0=y_t[:, :], scalar=tg[:, 3:4],
                                                      in1=x[:, b, :], op0=ALU.mult, op1=ALU.add))
                elif s.kind == "oz":
                    u = s.un.u
                    dve.wait_ge(delta_rstd, u + 1)
                    link(dve.tensor_scalar(tmp2[:, 0:256], y_t[:, :], mv2[:, 0:1], rstd2[:, :], ALU.subtract, ALU.mult))
                    link(dve.tensor_tensor(tmp[:, 0:256], tmp2[:, 0:256], row("lng"), ALU.mult))
                    link(dve.tensor_tensor(tmp2[:, 0:256], tmp[:, 0:256], row("lnb"), ALU.add))
                    link(dve.scalar_tensor_tensor(out=x[:, u, :], in0=tmp2[:, 0:256], scalar=tg[:, 2:3],
                                                  in1=x[:, u, :], op0=ALU.mult, op1=ALU.add))
                elif s.kind == "xl":
                    n = {0: 8, 2: 16, 3: 4}[s.layer]
                    turn(dve, bank_ready, s.m)
                    dve.tensor_copy(lg[:, s.b, 0:n], m_slot(s.m)[:, 0:n]).then_inc(bank_used[s.m % BANKS], 1)
                elif s.kind == "route":
                    evacuated(dve, s.lm)
                    n = {0: 8, 2: 16, 3: 4}[s.layer]
                    L = lg[:, :, 0:n]
                    if s.layer == 3:
                        link(dve.tensor_tensor(L, L, row("br3").unsqueeze(1).to_broadcast([P, NB, n]), ALU.add))
                    if s.layer in (0, 3):
                        first_max(L, n, oh[:, :, 0:n])
                        mx = r8[:, 0, :].unsqueeze(2).to_broadcast([P, NB, n])
                        dve.tensor_tensor(ra[:, :, 0:n], L, mx, ALU.subtract).then_inc(route_a, 1)
                        dve.wait_ge(route_b, s.exp_i + 1)
                        link(dve.tensor_reduce(r8[:, 2, :], ra[:, :, 0:n], AX.X, ALU.add))
                        link(dve.reciprocal(r8[:, 3, :], r8[:, 2, :]))
                        link(dve.tensor_scalar(r8[:, 3, :], r8[:, 3, :], tg[:, 4 + s.layer:5 + s.layer], None, ALU.mult))
                    if s.layer == 3:
                        link(dve.memset(rc[:, 0, 0:4], 0.0))
                        for b in range(1, NB):
                            link(dve.tensor_tensor(rc[:, b, 0:4], rc[:, b - 1, 0:4], oh[:, b - 1, 0:4], ALU.add))
                        link(dve.tensor_tensor(rc[:, 0, 8:12], rc[:, NB - 1, 0:4], oh[:, NB - 1, 0:4], ALU.add))
                        dve.sem_inc(route_pe, 1)
                        turn(dve, bank_ready, s.m)
                        link(dve.tensor_tensor(rb[:, :, 0:4], m_slot(s.m)[:, 0:32].rearrange("p (b e) -> p b e", b=NB),
                                               oh[:, :, 0:4], ALU.mult))
                        dve.tensor_scalar(r8[:, 5, 0:4], m_slot(s.m)[:, 32:36], 1.0 / P, 0.5 - 0.5 / P, ALU.mult, ALU.add
                                          ).then_inc(bank_used[s.m % BANKS], 1)
                        turn(dve, bank_used, s.m)
                        link(dve.tensor_scalar(r8[:, 5, 0:4], r8[:, 5, 0:4], MAGIC, MAGIC, ALU.add, ALU.subtract))
                        link(dve.tensor_reduce(r8[:, 4, :], rb[:, :, 0:4], AX.X, ALU.add))
                        link(dve.memset(ra[:, 0, 0:4], 0.0))
                        for e in range(1, 4):
                            link(dve.tensor_tensor(ra[:, 0, e:e + 1], ra[:, 0, e - 1:e], r8[:, 5, e - 1:e], ALU.add))
                        link(dve.tensor_scalar(ra[:, 1, :], const("tiles"), ra[:, 0, 1:2], None, ALU.is_ge))
                        for e in range(2, 4):
                            link(dve.scalar_tensor_tensor(out=ra[:, 1, :], in0=const("tiles"), scalar=ra[:, 0, e:e + 1],
                                                          in1=ra[:, 1, :], op0=ALU.is_ge, op1=ALU.add))
                        link(dve.tensor_copy(te[:, :], ra[:, 1, :]))
                        link(dve.tensor_tensor(rb[:, :, 0:4], oh[:, :, 0:4],
                                               ra[:, 0, 0:4].unsqueeze(1).to_broadcast([P, NB, 4]), ALU.mult))
                        link(dve.tensor_reduce(r8[:, 5, :], rb[:, :, 0:4], AX.X, ALU.add))
                        link(dve.tensor_scalar(r8[:, 5, :], r8[:, 5, :], float(P), None, ALU.mult))
                        link(dve.tensor_tensor(r8[:, 5, :], r8[:, 5, :], r8[:, 4, :], ALU.add))
                        dve.tensor_copy(idx[:, 0, :], r8[:, 5, :]).then_inc(routed3, 1)
                    elif s.layer == 0:
                        link(dve.memset(rc[:, 0, 0:8], 0.0))
                        for b in range(1, NB):
                            link(dve.tensor_tensor(rc[:, b, 0:8], rc[:, b - 1, 0:8], oh[:, b - 1, 0:8], ALU.add))
                        dve.sem_inc(route_pe, 1)
                        turn(dve, bank_ready, s.m)
                        dve.tensor_tensor(rb[:, :, 0:8], m_slot(s.m)[:, 0:64].rearrange("p (b e) -> p b e", b=NB),
                                          oh[:, :, 0:8], ALU.mult).then_inc(bank_used[s.m % BANKS], 1)
                        turn(dve, bank_used, s.m)
                        link(dve.tensor_reduce(r8[:, 4, :], rb[:, :, 0:8], AX.X, ALU.add))
                        link(dve.tensor_tensor(rb[:, :, 0:8], oh[:, :, 0:8],
                                               const("base").unsqueeze(1).to_broadcast([P, NB, 8]), ALU.mult))
                        link(dve.tensor_reduce(r8[:, 5, :], rb[:, :, 0:8], AX.X, ALU.add))
                        link(dve.tensor_tensor(r8[:, 5, :], r8[:, 5, :], r8[:, 4, :], ALU.add))
                        link(dve.tensor_scalar(r8[:, 4, :], r8[:, 4, :], float(P), None, ALU.is_lt))
                        link(dve.tensor_tensor(r8[:, 5, :], r8[:, 5, :], r8[:, 4, :], ALU.mult))
                        link(dve.tensor_copy(idx[:, 1, :], r8[:, 5, :]))
                        link(dve.tensor_scalar(r8[:, 1, :], r8[:, 4, :], -1.0, 1.0, ALU.mult, ALU.add))
                        link(dve.tensor_tensor(r8[:, 1, :], r8[:, 1, :], const("trash"), ALU.mult))
                        link(dve.tensor_tensor(r8[:, 5, :], r8[:, 5, :], r8[:, 1, :], ALU.add))
                        link(dve.tensor_tensor(r8[:, 3, :], r8[:, 3, :], r8[:, 4, :], ALU.mult))
                        dve.tensor_copy(idx[:, 0, :], r8[:, 5, :]).then_inc(routed, 1)
                    else:
                        link(dve.tensor_scalar(ra[:, :, :], L, -87.0, None, ALU.max))
                        dve.sem_inc(route_a, 1)
                        dve.wait_ge(route_b, s.exp_i + 1)
                        link(dve.tensor_scalar(rc[:, :, :], ra[:, :, :], 1.0, None, ALU.add))
                        link(dve.reciprocal(ra[:, :, :], rc[:, :, :]))
                        gb = row("gb2").unsqueeze(1).to_broadcast([P, NB, 16])
                        link(dve.tensor_tensor(rc[:, :, :], ra[:, :, :], gb, ALU.add))
                        first_max(rc[:, :, :], 16, oh[:, :, :])
                        link(dve.tensor_scalar(lg[:, :, :], oh[:, :, :], -1e30, None, ALU.mult))
                        link(dve.tensor_tensor(rc[:, :, :], rc[:, :, :], lg[:, :, :], ALU.add))
                        first_max(rc[:, :, :], 16, lg[:, :, :])
                        link(dve.tensor_tensor(oh[:, :, :], oh[:, :, :], lg[:, :, :], ALU.add))
                        link(dve.tensor_tensor(oh[:, :, :], oh[:, :, :], ra[:, :, :], ALU.mult))
                        link(dve.tensor_reduce(r8[:, 2, :], oh[:, :, :], AX.X, ALU.add))
                        link(dve.tensor_scalar(r8[:, 2, :], r8[:, 2, :], 1e-9, None, ALU.add))
                        link(dve.reciprocal(r8[:, 3, :], r8[:, 2, :]))
                        link(dve.tensor_scalar(r8[:, 3, :], r8[:, 3, :], tg[:, 6:7], None, ALU.mult))
                        link(dve.tensor_tensor(cm[:, :, :], oh[:, :, :], r8[:, 3, :].unsqueeze(2).to_broadcast([P, NB, 16]),
                                               ALU.mult))
                elif s.kind == "exd":
                    e = s.i
                    turn(dve, bank_ready, s.s)
                    if e >= 2:
                        dve.wait_ge(eo_out[e % 2], 16 * (e // 2))
                    dve.tensor_copy(eo[:, e % 2, :], psB[:, s.s % BANKS, 0:256]).then_inc(bank_used[s.s % BANKS], 1)
                elif s.kind == "su":
                    turn(dve, T_ready, s.n)
                    dve.wait_ge(silu_done, s.sg + 1)
                    if s.g >= 2:
                        turn(dve, bank_ready, hidden_turned[s.g - 2])
                    dve.tensor_tensor(htok[:, s.g % 2, :], psT[:, s.n % 2, 512:1024], sg[:, s.sg % 2, :], ALU.mult
                                      ).then_inc(T_used[s.n % 2], 1)
                    turn(dve, T_used, s.n)
                    dve.sem_inc(hidden3, 1)
                elif s.kind == "sd":
                    turn(dve, bank_ready, s.s)
                    if s.i >= 4:
                        dve.wait_ge(sorted_out[s.i % 4], 16 * (s.i // 4))
                    dve.tensor_copy(so[:, s.i % 4, :], m_slot(s.s)).then_inc(bank_used[s.s % BANKS], 1)
                elif s.kind == "combine3":
                    b = s.b
                    dve.wait_ge(gathered3[b], 16)
                    dve.scalar_tensor_tensor(out=x[:, b, :], in0=ge3[:, b, :], scalar=r8[:, 3, b:b + 1],
                                             in1=x[:, b, :], op0=ALU.mult, op1=ALU.add).then_inc(combined3, 1)
                elif s.kind == "combine":
                    b = s.b
                    dve.wait_ge(gathered[b], 16)
                    dve.scalar_tensor_tensor(out=x[:, b, :], in0=ge[:, b, :], scalar=r8[:, 3, b:b + 1],
                                             in1=x[:, b, :], op0=ALU.mult, op1=ALU.add).then_inc(combined, 1)
                    dve.wait_ge(combined, b + 1)
                elif s.kind == "gu":
                    w = s.width
                    if s.ch == 0 and s.h_free is not None:
                        turn(dve, bank_ready, s.h_free)
                    dve.wait_ge(silu_done, s.sg + 1)
                    up = psT[0:w, s.n % 2, 512:1024]
                    dst = Hb[0:w, s.h % 2, s.ch, :]
                    if s.layer == 1:
                        ins = dve.scalar_tensor_tensor(out=dst, in0=up, scalar=col("us1", s.ch, w),
                                                       in1=sg[0:w, s.sg % 2, :], op0=ALU.mult, op1=ALU.mult)
                    else:
                        ins = dve.tensor_tensor(dst, up, sg[0:w, s.sg % 2, :], ALU.mult)
                    ins.then_inc(T_used[s.n % 2], 1)
                elif s.kind == "down":
                    b = s.tg * 4 + s.tc
                    turn(dve, bank_ready, s.n)
                    for i in range(BANKS):
                        if s.x_after[i]:
                            dve.wait_ge(bank_used[i], s.x_after[i])
                    src = psB[:, s.n % BANKS, 0:256]
                    if s.layer == 1:
                        link(dve.tensor_tensor(tmp[:, 0:256], src, row("ds1"), ALU.mult))
                        src, w = tmp[:, 0:256], tg[:, 5:6]
                    elif s.blk.mask is None:
                        w = tg[:, 10:11]
                    else:
                        w = cm[:, b, s.blk.mask:s.blk.mask + 1]
                    dve.scalar_tensor_tensor(out=x[:, b, :], in0=src, scalar=w, in1=x[:, b, :],
                                             op0=ALU.mult, op1=ALU.add).then_inc(bank_used[s.n % BANKS], 1)

        @block.gpsimd
        def _(pool):
            chained = [0]

            def link(ins):
                chained[0] += 1
                ins.then_inc(pool_chain, 1)
                pool.wait_ge(pool_chain, chained[0])

            def split(src, dst, w, order, done):
                high, middle, low = [dst[:, i, 0:w] for i in order]
                link(pool.tensor_scalar(high, src, 1.0, 0.0, ALU.mult, ALU.add))
                link(pool.tensor_tensor(rem[:, 0:w], src, high, ALU.subtract))
                link(pool.tensor_scalar(middle, rem[:, 0:w], 1.0, 0.0, ALU.mult, ALU.add))
                pool.tensor_tensor(low, rem[:, 0:w], middle, ALU.subtract).then_inc(done, 1)

            link(pool.memset(arena[32:64, 6144:12288], 0.0))
            link(pool.memset(arena[64:96, 6144:12288], 0.0))
            pool.sem_inc(memset_done, 2)
            pool.wait_ge(const_in, 16 * 10)
            pool.wait_ge(zeros_made, 1)
            for s in steps:
                if s.kind == "barrier":
                    pool.wait_ge(rstd_ready, s.stats)
                elif s.kind == "stats":
                    pool.wait_ge(var_ready, s.i + 1)
                    pool.tensor_tensor(rstd[:, s.b:s.b + 1], vare[:, s.b:s.b + 1], const("mhalf"), ALU.pow
                                       ).then_inc(rstd_ready, 1)
                elif s.kind == "split":
                    A, u = s.A, s.un
                    w = A.halves * A.T
                    if s.kind_of == "qk":
                        if u.g >= 1:
                            pool.wait_ge(parts_q, u.g)
                        if A.layer == 1:
                            pool.wait_ge(xn_ready, u.xn.i + 1)
                            link(pool.tensor_scalar(qf[:, u.g % 2, 0:256], xn[:, u.u, :], 0.25, 0.0, ALU.mult, ALU.add))
                        else:
                            evacuated(pool, u.m[0])
                            evacuated(pool, u.m[1])
                        if u.g >= 2:
                            pool.wait_ge(q_stored[u.g % 2], 32 * (u.g // 2))
                        split(qf[:, u.g % 2, 0:w], sq[:, u.g % 2], w, (2, 1, 0), parts_q)
                        pool.wait_ge(parts_q, u.g + 1)
                    if u.k is not None:
                        if A.layer != 1:
                            evacuated(pool, u.m[1])
                        if s.kind_of == "k":
                            evacuated(pool, u.m[0])
                        if u.k >= 2:
                            pool.wait_ge(k_stored[u.k % 2], 32 * (u.k // 2))
                        src = ctx_s[:, u.u, :] if A.layer == 1 else kf[:, u.k % 2, 0:w]
                        split(src, sk[:, u.k % 2], w, (0, 1, 2), parts_k)
                        pool.wait_ge(parts_k, u.k + 1)
                elif s.kind == "packs" and s.A.layer == 1:
                    u = s.un
                    if s.done_before >= 0:
                        pool.wait_ge(PV_done, s.done_before + 1)
                    for c in range(2):
                        ins = pool.tensor_copy(VA[:, u.g % 3, c * 8:(c + 1) * 8, 0:16],
                                               ctx_t[:, c, u.u * P:(u.u + 1) * P].rearrange("p (h d) -> p h d", d=16))
                    ins.then_inc(V_copied, 1)
                elif s.kind == "oy" and s.A.layer == 2:
                    pool.wait_ge(delta_var, s.un.u + 1)
                    pool.tensor_tensor(rstd2[:, :], vare2[:, :], const("mhalf"), ALU.pow).then_inc(delta_rstd, 1)
                elif s.kind == "scatter":
                    if s.b == 0:
                        pool.wait_ge(routed, 1)
                        pool.wait_ge(zero_in, 16 * (NB + TILES3))
                    pool.indirect_dma_start(xd, bass.IndirectOffsetOnAxis(ap=idx[:, 0, s.b:s.b + 1].bitcast(U32), axis=0),
                                            xn[:, s.b, :], None).then_inc(scattered, 16)
                elif s.kind == "scatter3":
                    if s.b == 0:
                        pool.wait_ge(routed3, 1)
                    pool.indirect_dma_start(sxd, bass.IndirectOffsetOnAxis(ap=idx[:, 0, s.b:s.b + 1].bitcast(U32), axis=0),
                                            xn[:, s.b, :], None).then_inc(scattered3, 16)
                elif s.kind == "gather3":
                    if s.b == 0:
                        for i in range(4):
                            pool.wait_ge(sorted_out[i], 16 * ((TILES3 - 1 - i) // 4 + 1))
                    pool.indirect_dma_start(ge3[:, s.b, :], None, sod,
                                            bass.IndirectOffsetOnAxis(ap=idx[:, 0, s.b:s.b + 1].bitcast(U32), axis=0)
                                            ).then_inc(gathered3[s.b], 16)
                elif s.kind == "gather":
                    if s.b == 0:
                        for i in range(2):
                            pool.wait_ge(eo_out[i], 16 * 4)
                    pool.indirect_dma_start(ge[:, s.b, :], None, eod,
                                            bass.IndirectOffsetOnAxis(ap=idx[:, 1, s.b:s.b + 1].bitcast(U32), axis=0)
                                            ).then_inc(gathered[s.b], 16)


def pack(sp, A, dst, src, width, sem, is_q):
    at = 0
    for first in range(3):
        n = 3 - first
        c0 = first if is_q else 0
        rows = dst[at * A.d:(at + n) * A.d, 0:A.H * width].rearrange("r (h n) -> r h n", h=A.H)
        at += n
        if A.layer == 1:
            for c in range(n):
                sp.dma_start(rows[c * A.d:(c + 1) * A.d], src[c0 + c, :, 0:width].rearrange("(h d) n -> d h n", d=A.d)
                             ).then_inc(sem, 16)
        else:
            sp.dma_start(rows, src[c0:c0 + n, :, 0:width].rearrange("c (d h) n -> (c d) h n", d=A.d)).then_inc(sem, 16)


def kernel(**inputs):
    import numpy as np
    import concourse.bacc as bacc
    from concourse.bass_utils import run_bass_kernel_spmd as run

    a = {k: np.asarray(v) for k, v in inputs.items()}

    def halves(w):
        k, n = w.shape
        c = -(-k // P)
        full = np.zeros((c * P, n), w.dtype)
        full[:k] = w
        return full.reshape(c, P, n).transpose(1, 0, 2)

    def flat(*ws):
        return np.ascontiguousarray(np.concatenate([halves(w).reshape(P, -1) for w in ws], axis=1))

    def d_major(w, heads):
        n = w.shape[-1] // heads
        return w.reshape(*w.shape[:-1], heads, n).swapaxes(-1, -2).reshape(w.shape)

    arrays = {"x": a["x"], "ctx": a["ctx_2048"]}
    arrays["ctx_t"] = halves(a["ctx_2048"].reshape(NT, D).T)
    arrays["mask"] = a["mask_BxS2_ik0"].T
    vals = {"g_xattn": a["g_xattn"], "g_ffn": a["g_ffn"], "gamma": a["L1_xattn_gamma"].reshape(1),
            "rscale": a["L2_xattn_residual_scale"].reshape(1), "bv0": a["L0_xattn_bv"], "bv2": a["L2_xattn_bv"],
            "bo2": a["L2_xattn_bo"], "lng": a["L2_xattn_ln_gamma"], "lnb": a["L2_xattn_ln_beta"],
            "bq3": d_major(a["L3_xattn_bq"], 16), "bk3": d_major(a["L3_xattn_bkv"][:256], 16),
            "bp3": a["L3_xattn_bp"], "ds1": a["L1_ffn_down_s"], "br3": a["L3_ffn_br"], "gb2": a["L2_ffn_gate_bias"]}
    arrays["rows"] = np.concatenate([vals[n].reshape(-1) for n, _ in ROWS])
    cvals = {"bq0": d_major(a["L0_xattn_bq"], 16), "bk0": d_major(a["L0_xattn_bk"], 16), "bo0": a["L0_xattn_bo"],
             "bq2": d_major(a["L2_xattn_bq"], 16), "bk2": d_major(a["L2_xattn_bk"], 16),
             "bv3": a["L3_xattn_bkv"][256:], "gs1": a["L1_ffn_gate_s"], "us1": a["L1_ffn_up_s"]}
    arrays["cols"] = np.concatenate([halves(cvals[n].reshape(-1, 1)).reshape(P, -1) for n, _ in COLS], axis=1)
    part = np.arange(P, dtype=np.float32)
    sumsel = np.zeros((P, EW), np.float32)
    sumsel[:, SUMCOL] = 1.0
    arrays["cst"] = np.concatenate([
        np.eye(P, dtype=np.float32), np.triu(np.ones((P, P), np.float32), 1), np.ones((P, P), np.float32),
        np.tile(16.0 - np.arange(16, dtype=np.float32), (P, 1)), np.tile(128.0 * np.arange(8, dtype=np.float32), (P, 1)),
        TRASH + part[:, None] + P * np.arange(NB, dtype=np.float32), np.full((P, 1), -0.5, np.float32), sumsel,
        np.tile(np.arange(16, dtype=np.float32), (P, 1))], axis=1)
    b16 = mybir.dt.np(BF16)
    arrays["ident16"] = np.eye(P).astype(b16)
    arrays["ones3"] = np.ones((3, 4096), b16)
    arrays["w_at0"] = np.stack([d_major(a["L0_xattn_Wq"].T, 16), d_major(a["L0_xattn_Wk"].T, 16),
                                a["L0_xattn_Wv"].T, a["L0_xattn_Wo"].T], axis=1)
    arrays["w_at2"] = np.stack([halves(w) for w in (d_major(a["L2_xattn_Wq"].T, 16), d_major(a["L2_xattn_Wk"].T, 16),
                                                    a["L2_xattn_Wv"].T, a["L2_xattn_Wo"].T)], axis=1)
    wkv = a["L3_xattn_Wkv"]
    arrays["w_at3"] = np.stack([halves(w) for w in (d_major(a["L3_xattn_Wq"], 16), d_major(wkv[:, :256], 16),
                                                    wkv[:, 256:], a["L3_xattn_Wp"])], axis=1)
    arrays["wr"] = np.concatenate([halves(a["L0_ffn_w_gate"]), halves(a["L2_ffn_centroids"].T), halves(a["L3_ffn_Wr"])],
                                  axis=2)
    for e in range(8):
        arrays[f"w{e}"] = flat(a["L0_ffn_w1"][e], a["L0_ffn_w2"][e])
    arrays["w8"] = flat(a["L1_ffn_gate_w"].T, a["L1_ffn_up_w"].T, a["L1_ffn_down_w"].T)
    arrays["w9"] = flat(a["L2_ffn_wg_s"], a["L2_ffn_wu_s"], a["L2_ffn_wd_s"])
    for g in range(2):
        arrays[f"w{10 + g}"] = np.concatenate([flat(a["L2_ffn_wg"][e], a["L2_ffn_wu"][e], a["L2_ffn_wd"][e])
                                               for e in range(8 * g, 8 * g + 8)], axis=1)
    for e in range(4):
        arrays[f"w{12 + e}"] = flat(a["L3_ffn_Wg"][e], a["L3_ffn_Wu"][e], a["L3_ffn_Wd"][e])

    nc = bacc.Bacc("TRN2", target_bir_lowering=False, num_devices=1)
    feeds, views = {}, {}
    for name, v in arrays.items():
        v = np.ascontiguousarray(v)
        feeds[f"in_{name}"] = v
        views[name] = nc.dram_tensor(f"in_{name}", v.shape, mybir.dt.from_np(v.dtype), kind="ExternalInput").ap()
    out = nc.dram_tensor("out_x", [NB, S, D], F32, kind="ExternalOutput").ap()
    flamingo(nc, views, out)
    r = run(nc, [feeds], core_ids=[0])
    return r.results[0]["out_x"]
```

```python
from contextlib import ExitStack

import concourse.bass as bass
from concourse import mybir

F32 = mybir.dt.float32
BF16 = mybir.dt.bfloat16
I32 = mybir.dt.int32
U32 = mybir.dt.uint32
ALU = mybir.AluOpType
ACT = mybir.ActivationFunctionType
AX = mybir.AxisListType


class Layer:

    def __init__(self, layer=None, H=None, d=None, U=None, nb=None, TC=None, T=None, NC=None,
                 has_max=None, G=None, halves=None, parts=None):
        self.layer, self.H, self.d, self.U, self.nb, self.TC, self.T, self.NC = layer, H, d, U, nb, TC, T, NC
        self.has_max, self.G, self.halves = has_max, G, halves
        self.parts = parts


class Blk:

    def __init__(self, widths=None, item=None, off=None, F=None):
        self.widths, self.item, self.off, self.F = widths, item, off, F


class Norm:

    def __init__(self, b=None, stat=None, i=None):
        self.b, self.stat, self.i = b, stat, i


class Record:

    def __init__(self, kind=None, kind_of=None, A=None, u=None, b=None, i=None, g=None, c=None,
                 j=None, tc=None, h=None, k=None, m=None, n=None, o=None, p=None, s=None, q=None,
                 sg=None, clip=None, un=None, item=None, free=None, stats=None, last_P=None,
                 last_S=None, neg=None, layer=None, xn=None, lm=None, first=None, blk=None, tg=None,
                 ch=None, width=None, h_free=None, last_T=None, last_m=None, done_before=None,
                 m_prev=None, m_prev2=None, m_last_norm=None, prev_m=None, clip3=None, exp_i=None,
                 after=None, x_after=None, m_x=None, m_v=None, m_t=None, o_of=None, packed=None,
                 packed_before=None, b0=None):
        self.kind, self.kind_of, self.A, self.u, self.b, self.i, self.g, self.c = kind, kind_of, A, u, b, i, g, c
        self.j, self.tc, self.h, self.k, self.m, self.n, self.o, self.p = j, tc, h, k, m, n, o, p
        self.s, self.q, self.sg, self.clip, self.un, self.item, self.free, self.stats = s, q, sg, clip, un, item, free, stats
        self.last_P, self.last_S, self.neg, self.layer, self.xn, self.lm, self.first, self.blk = last_P, last_S, neg, layer, xn, lm, first, blk
        self.tg, self.ch, self.width, self.h_free, self.last_T, self.last_m, self.done_before, self.m_prev = tg, ch, width, h_free, last_T, last_m, done_before, m_prev
        self.m_prev2, self.m_last_norm, self.prev_m, self.clip3, self.exp_i, self.after, self.x_after, self.m_x = m_prev2, m_last_norm, prev_m, clip3, exp_i, after, x_after, m_x
        self.m_v, self.m_t, self.o_of, self.packed, self.packed_before = m_v, m_t, o_of, packed, packed_before
        self.b0 = b0


P = 128
NB = 8
D = 256
S = 128
NT = NB * S
EPS = 1e-5
EW = 32
SUMCOL = 16
MAGIC = 12582912.0
LN255 = 5.541263545158426
K3_AT = (3, 9, 15, 21)
LOADS = 14
SLOTW = 6144
BANKS = 3
TILES3 = NB + 3
TILES2 = 2 * NB + 15
TRASH = NT

ROWS = [("g_xattn", 4), ("g_ffn", 4), ("gamma", 1), ("rscale", 1), ("bv0", 128), ("bv2", 256),
        ("bo2", 256), ("lng", 256), ("lnb", 256), ("bq3", 256), ("bk3", 256), ("bp3", 256),
        ("ds1", 256), ("br3", 4), ("gb2", 16)]
COLS = [("bq0", 1), ("bk0", 1), ("bo0", 1), ("bq2", 2), ("bk2", 2), ("bv3", 2), ("gs1", 6), ("us1", 6)]
CONST = [("ident", 128), ("before", 128), ("ones", 128), ("desc", 16), ("base", 8), ("trash", 8),
         ("mhalf", 1), ("sumsel", 32), ("tiles", 32), ("zero", 1)]


def offsets(items):
    at, out = 0, {}
    for name, n in items:
        out[name] = (at, at + n)
        at += n
    return out, at


def attn(layer, heads, d, units, batches, tcs, chunks, has_max):
    return Layer(layer=layer, H=heads, d=d, U=units, nb=batches, TC=tcs, T=tcs * P,
                           NC=chunks, has_max=has_max, G=heads // 4, halves=heads * d // P, parts=2 if layer == 3 else 1)


ATT = [attn(0, 16, 8, 8, 1, 2, 2, True), attn(1, 8, 16, 8, 1, 2, 2, True),
       attn(2, 16, 16, 8, 1, 1, 1, False), attn(3, 16, 16, 4, 2, 2, 8, True)]


def ffn_blocks(layer):
    if layer == 1:
        return [Blk(widths=[128] * 5 + [64], item=8, off=0, F=704)]
    return [Blk(widths=[128] * 2, item=9, off=0, F=256)]


def merge(*streams):
    order = []
    for k, (thunks, start, end) in enumerate(streams):
        for i, thunk in enumerate(thunks):
            order.append((start + (end - start) * (i + 0.5) / len(thunks), k, i, thunk))
    for _, _, _, thunk in sorted(order, key=lambda x: x[:3]):
        thunk()


TIMES = [
    dict(front=0.339, store=0.638, packs=0.799, max=1.019, max_end=1.768, neg=1.872, body=2.312, end=3.927, start=0.37, span=1.018, max_first=1.418),
    dict(front=0.315, store=0.667, packs=1.343, max=1.871, max_end=2.607, neg=2.791, body=3.334, end=5.361, start=0.069, span=0.983, max_first=1.89),
    dict(front=0.498, store=0.58, packs=0.683, body=1.604, end=3.227, start=0.084, span=1.053),
    dict(front=0.077, store=0.137, packs=0.636, max=1.011, max_end=1.855, neg=1.934, body=1.639, end=3.415, start=0.276, span=1.008, max_first=1.117)]


def plan():
    steps = []
    n = dict(sg3=0, B=0, T=0, P=0, O=0, unit=0, stat=0, xn=0, q=0, k=0, neg=0, sg=0, clip=0, round=0, quant=0, exp=0)
    stat_of, item_free, s_count, packed = {}, {}, [0] * BANKS, [0, 0]
    last = dict(onorm=None, norm={}, neg={}, out_y=None, quant_t=None)

    def take(ring):
        ring = "B" if ring in "MS" else ring
        n[ring] += 1
        if ring == "B":
            s_count[(n["B"] - 1) % BANKS] = (n["B"] - 1) // BANKS + 1
        return n[ring] - 1

    def add(kind, **k):
        s = Record(kind=kind, **k)
        steps.append(s)
        return s

    def stats(b, after=None):
        stat_of[b] = take("stat")
        add("stats", b=b, i=stat_of[b], after=after)

    def normed(b):
        return Norm(b=b, stat=stat_of[b], i=take("xn"))

    def barrier():
        add("barrier", stats=n["stat"])

    def wload(i):
        add("wload", item=i, free=item_free.get(i - 2))

    def eload(e, part):
        add("eload", i=e, j=part, free=item_free.get((e - 4, part)))

    def quant(r, scaled):
        s = add("quant", un=r, s=scaled, prev_m=last["quant_t"])
        s.i = take("quant")
        return s.i

    def keys_ahead():
        A = ATT[3]
        out = []

        def unit(u):
            r = Record(A=A, u=u, k=take("k"))

            def kp(j):
                def f():
                    r.m_v = (r.m_v or []) + [add("kp", un=r, u=u, j=j, m=take("M")).m]
                return f

            def q():
                r.i = quant(r, False)

            def kt(m):
                def f():
                    s = add("kt", un=r, c=m, i=r.i, m=take("M"))
                    r.m = (r.m or []) + [s.m]
                    last["quant_t"] = s.m
                return f

            def ks():
                add("split", un=r, A=A, kind_of="k")

            def store():
                add("store", un=r, A=A, kind_of="k")
            return [kp(0), kp(1), q, kt(0), kt(1), ks, store]
        for u in range(4):
            out += unit(u)
        return out

    def values_ahead():
        for u in range(4):
            for c in range(2):
                m = add("vp", u=u, c=c, m=take("M")).m
        return m

    def values_turned():
        last_turn = []

        def turn(c):
            return lambda: last_turn.append(add("vturn", c=c, m=take("M")).m)
        return [turn(c) for c in range(NB)] + [lambda: add("vstore", m=last_turn[-1])]

    def attention(A, later, before):
        if A.layer == 2:
            barrier()
        add("attn_begin", A=A)
        units = []

        def front(u):
            b0 = u * A.nb
            r = Record(A=A, b0=b0, u=u, g=take("unit"), k=take("k") if A.layer < 3 else None)
            units.append(r)
            r.packed_before = packed[r.g % 2]
            packed[r.g % 2] += 16 * (6 if A.layer == 1 else 3)
            r.packed = packed[r.g % 2]

            def fn(j):
                def f():
                    if A.layer == 0:
                        stats(u)
                    xs = normed(b0 + j)
                    if A.layer >= 2:
                        s = add("fx", A=A, un=r, j=j, xn=xs, m=take("M"))
                        r.m_x = s.m
                    else:
                        add("fn", xn=xs)
                        r.xn = xs
                return f

            def proj(kind):
                def f():
                    s = add(kind, A=A, un=r, m=take("M"))
                    if kind == "fv":
                        r.m_v = s.m
                        s.done_before = done()
                    else:
                        r.m = (r.m or []) + [s.m]
                return f

            def done():
                assert u < 3 or units[u - 3].last_P is not None
                return units[u - 3].last_P if u >= 3 else -1

            def fq3(j):
                def f():
                    r.m_v = (r.m_v or []) + [add("fq3", A=A, un=r, j=j, m=take("M"), m_prev=r.m_x).m]
                return f

            def q3():
                r.i = quant(r, True)

            def fqt(m):
                def f():
                    s = add("fqt", un=r, c=m, i=r.i, m=take("M"))
                    r.m = (r.m or []) + [s.m]
                    last["quant_t"] = s.m
                return f

            def split():
                add("split", un=r, A=A, kind_of="qk")

            def store():
                add("store", un=r, A=A, kind_of="qk")

            def packs():
                add("packs", un=r, A=A, done_before=done())
            out = [fn(j) for j in range(A.nb)]
            if A.layer in (0, 2):
                out += [proj("fq"), proj("fk"), split]
            elif A.layer == 1:
                out += [split]
            else:
                out += [fq3(j) for j in range(A.nb)] + [q3, fqt(0), fqt(1), split]
            return out, [store], [packs] + ([proj("fv")] if A.layer in (0, 2) else [])

        def maxes(r):
            out = []
            r.neg = []
            per = A.H * A.NC * P // 512 // A.parts
            for part in range(A.parts):
                tiles = []
                for tc in range(A.TC):
                    for j in range(part * per, (part + 1) * per):
                        def f(tc=tc, j=j):
                            r.last_S = add("smax", A=A, un=r, tc=tc, j=j, first=(tc == 0 and j == 0), n=take("S")).n
                        tiles.append(f)

                def split(part=part):
                    r.neg.append(take("neg"))
                    add("negsplit", A=A, un=r, j=part, i=r.neg[part], last_S=r.last_S,
                        m_prev2=last["neg"].get(r.neg[part] - 2))

                def turn(part=part):
                    last["neg"][r.neg[part]] = add("negmax", A=A, un=r, j=part, i=r.neg[part], m=take("M")).m
                out.append((tiles, split, turn))
            return out

        def body(r):
            tiles = [(g, c) for g in range(A.G) for c in range(A.NC)]
            made, out = {}, []
            lag = (1, 1, 2, 3)[A.layer]

            def st(i):
                g, c = tiles[i]
                s = add("st", A=A, un=r, g=g, c=c, first=(i == 0), n=take("T"), p=take("P"))
                if A.has_max and c == 0 and g % (A.G // A.parts) == 0:
                    s.neg = r.neg[g * A.parts // A.G]
                s.clip = take("clip") if A.layer == 2 else None
                made[i] = s

            def rnd(i):
                made[i].clip3 = take("round")
                add("round", A=A, n=made[i].n, p=made[i].p)

            def pv(i):
                s = made[i]
                if s.c == 0:
                    r.o = take("O")
                add("pv", A=A, un=r, g=s.g, c=s.c, n=s.n, p=s.p, o=r.o, clip=s.clip, clip3=s.clip3)
                r.last_P = s.p if i == len(tiles) - 1 else None
                last["P3"] = s.p
                if s.c == A.NC - 1:
                    add("oev", A=A, o=r.o, p=s.p, m_prev2=last["norm"].get(r.o - 2))

            def onorm(i):
                s = made[i]
                m = take("M")
                last["norm"][s.un.o_of[s.g]] = m
                r.m_last_norm = m
                add("onorm", A=A, un=r, g=s.g, o=s.un.o_of[s.g], m=m, m_prev=last["onorm"])
                last["onorm"] = m
            r.o_of = {}
            for i in range(len(tiles) + lag + 1):
                def f(i=i):
                    if i < len(tiles):
                        st(i)
                    if A.layer == 3 and 0 <= i - 1 < len(tiles):
                        rnd(i - 1)
                    k = i - lag
                    if 0 <= k - 1 < len(tiles) and tiles[k - 1][1] == A.NC - 1:
                        onorm(k - 1)
                    if 0 <= k < len(tiles):
                        pv(k)
                        r.o_of[tiles[k][0]] = r.o
                out.append(f)
            return out

        def finish(r):
            def ot(m):
                def f():
                    s = add("ot", A=A, un=r, c=m, m=take("M"), m_last_norm=r.m_last_norm, m_prev=last["out_y"])
                    r.m_t = (r.m_t or []) + [s.m]
                return f

            def oy(j):
                def f():
                    s = add("oy", A=A, un=r, j=j, m=take("M"))
                    last["out_y"] = s.m
                    if A.layer != 2:
                        stats(r.b0 + j)
                return f

            def oz():
                add("oz", un=r)
                stats(r.u)
            if A.layer == 1:
                def f():
                    add("ot", A=A, un=r, c=0, m=take("M"), m_last_norm=r.m_last_norm)
                    stats(r.u)
                return [f]
                return [f]
            return ([ot(m) for m in range(A.halves)] if A.layer == 3 else [ot(0)]) + [oy(j) for j in range(A.nb)] \
                + ([oz] if A.layer == 2 else [])

        at = TIMES[A.layer]
        streams = [([thunk], time, time) for thunk, time in before]
        for u in range(A.U):
            first, store, packs = front(u)
            streams += [(first, u, u + at["front"]), (store, u + at["store"], u + at["store"]),
                        (packs, u + at["packs"], u + at["packs"] + 0.02)]
            if A.layer == 0 and u == 0:
                streams += [([lambda i=i: add("zero", i=i)], w, w)
                            for i, w in ((0, 0.5 * at["front"]), (1, at["max"] + 0.2), (2, at["max"] + 0.5))]
                streams += [([lambda: add("prepare")], at["front"], at["front"]),
                            ([lambda i=i: add("loads", i=i) for i in range(LOADS)], 2.0, 9.5)]
            if A.has_max:
                begin = u + at["max"] if u else at["max_first"]
                step = (u + at["max_end"] - begin) / A.parts
                for tiles, split, turn in maxes(units[u]):
                    begin += step
                    streams += [(tiles, begin - step, begin), ([split], begin, begin),
                                ([turn], begin + at["neg"] - at["max_end"], begin + at["neg"] - at["max_end"])]
            body_end = u + at["body"] + at["span"]
            batches = range(units[u].b0, units[u].b0 + A.nb)
            streams += [(body(units[u]), u + at["body"], body_end), (finish(units[u]), body_end + at["start"], u + at["end"]),
                        ([f for b in batches for f in later(b)], u + at["end"] + 0.1, u + at["end"] + 0.9)]
        merge(*streams)

    def turned(layer):
        def thunks(b):
            def f():
                add("xt", layer=layer, xn=normed(b), m=take("M"))

            def g():
                last["lm"] = add("xl", layer=layer, b=b, m=take("M"), m_prev=steps_m(b)).m

            def steps_m(b):
                return [s.m for s in steps if s.kind == "xt" and s.xn.b == b][-1]
            return [f, g] if layer != 1 else [f]
        return thunks

    def route(layer, m):
        add("route", layer=layer, m=m, lm=last["lm"], exp_i=take("exp"))

    def moe_capacity():
        barrier()
        for e in (2, 3):
            eload(e, 0)
            eload(e, 1)
        route(0, take("M"))
        v_last = values_ahead()
        for b in range(NB):
            add("scatter", b=b)
        add("vscale", last_m=v_last)
        out, rec = [], {}

        def ext(e):
            def f():
                rec[e] = add("ext", i=e, m=take("M"))
            return f

        def exu(e):
            def f():
                rec[e, "u"] = add("exu", i=e, m=rec[e].m, n=take("T"))
                item_free[e, 0] = rec[e, "u"].n
                if e + 4 < 8:
                    eload(e + 4, 0)
            return f

        def exd(e):
            def f():
                s = add("exd", i=e, n=rec[e, "u"].n, s=take("S"))
                item_free[e] = s.s
                if e + 4 < 8:
                    item_free[e, 1] = s.s
                    eload(e + 4, 1)
                if e == 5:
                    add("wload", item=8, free=s.s)
            return f
        for e in range(8):
            out += [ext(e), exu(e)] + ([exd(e - 1)] if e else [])
        out.append(exd(7))
        keys = keys_ahead()
        merge((out, 0.0, 1.0), (values_turned(), 0.2, 0.5), (keys, 0.05, 0.9))
        add("w3load", item="w_at2")
        for b in range(NB):
            add("gather", b=b)

        def combine(b):
            def f():
                add("combine", b=b)
                stats(b)
            return f
        return [(combine(b), 0.35 * b - 0.01) for b in range(NB)] + [(lambda: add("vblocks"), 0.5)]

    def sorted_experts():
        add("w3first", p=last["P3"])
        barrier()
        route(3, take("M"))
        for b in range(NB):
            add("scatter3", b=b)
        tiles = []

        def sx(t):
            tiles.append(Record(i=t, sg=[], g=[]))
            tiles[t].m_x = add("sx", i=t, m=take("M")).m

        def su(t, j):
            r = tiles[t]
            g, m_x = take("sg3"), r.m_x
            r.g.append(g)
            add("su", i=t, j=j, m_x=m_x, g=g, n=take("T"), sg=take("sg"), un=r)

        def sh(t, j):
            r = tiles[t]
            r.m = (r.m or []) + [add("sh", i=t, j=j, g=r.g[j], m=take("M"), m_prev=tiles[t - 2].s if t >= 2 else None).m]

        def sd(t):
            r = tiles[t]
            r.s = add("sd", i=t, un=r, s=take("M")).s
        add("sx_load", i=None)
        sx(0)
        for t in range(TILES3):
            su(t, 0)
            if t >= 1:
                sh(t - 1, 1)
            if t + 1 < TILES3:
                sx(t + 1)
            su(t, 1)
            if t >= 1:
                sd(t - 1)
            sh(t, 0)
        sh(TILES3 - 1, 1)
        sd(TILES3 - 1)
        for b in range(NB):
            add("gather3", b=b)
        for b in range(NB):
            add("combine3", b=b)

    def sorted_pairs():
        barrier()
        add("wload", item=11, free=None)
        add("w3load", item="w_at3")
        route(2, take("M"))
        for b in range(NB):
            add("scatter2", b=b)
        shared = dense(2)
        add("t_load")
        tiles = {}

        def tx(t):
            tiles[t] = Record(i=t)
            tiles[t].m_x = add("tx", i=t, m=take("M")).m

        def tu(t):
            add("tu", i=t, un=tiles[t], m_x=tiles[t].m_x, n=take("T"), sg=take("sg"))

        def th(t):
            tiles[t].m = add("th", i=t, m=take("M")).m

        def td(t):
            tiles[t].s = add("td", i=t, un=tiles[t], m=tiles[t].m, s=take("M")).s
        for t in range(-2, TILES2 + 1):
            for part, i in ((tx, t + 2), (tu, t + 1), (th, t), (td, t - 1)):
                if 0 <= i < TILES2:
                    part(i)
            if t in K3_AT:
                add("k3load", i=K3_AT.index(t), m=shared)
        add("wload", item=12, free=tiles[TILES2 - 1].s)
        for b in range(NB):
            add("gather2", b=b)

        def combine(b):
            def f():
                add("combine2", b=b, m=shared)
                stats(b)
            return f
        return [(combine(b), 0.01 * b - 0.02 if b < 2 else 0.06 * b) for b in range(NB)]

    def dense(layer):
        if layer == 1:
            barrier()
        blocks = ffn_blocks(layer)
        pending, hcount, h_free, s_last = None, 0, {}, [None]

        def down(work):
            blk, tg, h, last_T = work
            final = blk is blocks[-1]
            for tc in range(4):
                x_after = list(s_count)
                s = add("down", layer=layer, blk=blk, tg=tg, tc=tc, h=h, last_T=last_T, x_after=x_after, n=take("S"))
                if final and layer == 1:
                    stats(tg * 4 + tc, list(s_count))
            h_free[h] = s.n
            s_last[0] = item_free[blk.item] = s.n
            if tg == 1:
                if layer == 1:
                    wload(9)
                    wload(10)

        xt_last = [s.m for s in steps if s.kind == "xt"][-1]
        for blk in blocks:
            for tg in range(2):
                h = hcount
                hcount += 1
                for ch, width in enumerate(blk.widths):
                    s = add("gu", layer=layer, blk=blk, tg=tg, ch=ch, width=width, h=h, m=xt_last,
                            h_free=h_free.get(h - 2), n=take("T"), sg=take("sg"))
                if pending:
                    down(pending)
                pending = (blk, tg, h, s.n)
        down(pending)
        return s_last[0] if layer == 2 else []

    before = []
    for i, A in enumerate(ATT):
        attention(A, turned(A.layer), before)
        before = (moe_capacity, lambda: dense(1), sorted_pairs, sorted_experts)[i]()
    return steps


def flamingo(nc, t, out):
    steps = plan()
    ext_m = {s.i: s.m for s in steps if s.kind == "ext"}
    hidden_turned = {s.g: s.m for s in steps if s.kind == "sh"}
    row_at, row_n = offsets(ROWS)
    col_at, col_n = offsets(COLS)
    cst_at, cst_n = offsets(CONST)

    with ExitStack() as ctx:
        def sb(name, shape, dt=F32):
            return ctx.enter_context(nc.sbuf_tensor(name, shape, dt))

        def pb(name, shape, dt=F32):
            return ctx.enter_context(nc.psum_tensor(name, shape, dt))

        def sem(name):
            return ctx.enter_context(nc.semaphore(name))

        def ring(name):
            return [sem(f"{name}{i}") for i in range(BANKS)]

        def pair(name):
            return [sem(f"{name}{i}") for i in range(2)]

        x = sb("x", [P, NB, D])
        xn = sb("xn", [P, NB, D])
        ctx_t = sb("ctx_t", [P, 2, NT])
        xn_t = sb("xn_t", [P, 2, NT])
        whole = sb("whole", [P, SLOTW + 17408 + NB * D])
        w0 = whole[:, 0:SLOTW]
        arena = whole[:, SLOTW:SLOTW + 17408]
        ctx_s = whole[:, SLOTW + 17408:].rearrange("p (b n) -> p b n", b=NB)
        QP = arena[:, 0:6144].bitcast(BF16).rearrange("p (r n) -> p r n", r=3)
        KP = arena[:, 6144:14336].bitcast(BF16)
        VA = arena[:, 14336:17408].rearrange("p (r w e) -> p r w e", r=3, e=EW)
        VQ = arena[:, 14336:16384].bitcast(BF16).rearrange("p (w e) -> p w e", e=EW)
        VQ_made = arena[:, 0:2048].bitcast(BF16).rearrange("p (w e) -> p w e", e=EW)
        Hb = arena[:, 0:8192].rearrange("p (r c n) -> p r c n", r=2, c=8)
        vf = arena[:, 0:2048].rearrange("p (m n) -> p m n", m=2)
        vr = arena[:, 2048:4096].rearrange("p (m n) -> p m n", m=2)
        vi = arena[:, 4096:5120].bitcast(BF16).rearrange("p (m n) -> p m n", m=2)
        W_AT = {8: 0, 9: SLOTW + 12288, 10: 0, 11: SLOTW, 12: 0}
        Hb2 = arena[:, 6144:8192].rearrange("p (r c n) -> p r c n", r=2, c=2)
        EXPERT_AT = [[0, 1024, 2048, 3072], [4096, 5120, SLOTW + 12288, SLOTW + 13312],
                     [SLOTW + 8192, SLOTW + 9216, SLOTW + 10240, SLOTW + 11264],
                     [SLOTW + 14336, SLOTW + 15360, SLOTW + 16384, SLOTW + 7168]]

        def expert(e, word, n):
            at = EXPERT_AT[e % 4][word // 1024] + word % 1024
            return whole[:, at:at + n]
        Pt = sb("Pt", [P, 3, 1024])
        nb_t = sb("nb_t", [P, 2, 512])
        nb16 = nb_t[:, :, :].rearrange("p r n -> p (r n)").bitcast(BF16).rearrange("p (r n) -> p r n", r=2)
        sq = sb("sq", [P, 2, 3, 512], BF16)
        sk = sb("sk", [P, 2, 3, 512], BF16)
        qf = sb("qf", [P, 2, 512])
        kf = sb("kf", [P, 2, 512])
        rem = sb("rem", [P, 512])
        Oe = sb("Oe", [P, 2, 256])
        On = sb("On", [P, 2, 512])
        OnT = sb("OnT", [P, 2, 256])
        w_at0 = sb("w_at0", [P, 4, 128])
        late = w_at0[:, :, :].rearrange("p k n -> p (k n)")
        earlier = late[:, 0:256]
        powers = late[:, 400:432]
        te = late[:, 256:264].bitcast(I32)
        wts = late[:, 288:304].rearrange("p (k b) -> p k b", k=2)
        qs = late[:, 304:400].rearrange("p (k h) -> p k h", k=3)
        w_at2 = sb("w_at2", [P, 4, 2, 256])
        wr = sb("wr", [P, 2, 28])
        rows = sb("rows", [P, row_n])
        cols = sb("cols", [P, col_n])
        cst = sb("cst", [P, cst_n])
        ident16 = sb("ident16", [P, P], BF16)
        mask_i = sb("mask_i", [P, NB], I32)
        att = sb("att", [P, NB])
        att_b = sb("att_b", [P, NB])
        tg = sb("tg", [P, 16])
        colx = sb("colx", [P, 4])
        st6 = sb("st6", [P, 6])
        mv = sb("mv", [P, NB, 2])
        vare = sb("vare", [P, NB])
        rstd = sb("rstd", [P, NB])
        mv2 = sb("mv2", [P, 2])
        vare2 = sb("vare2", [P, 1])
        rstd2 = sb("rstd2", [P, 1])
        mxp = sb("mxp", [P, 2, 64])
        nm = sb("nm", [P, 2, 32])
        npt = sb("npt", [P, 2, 2 * 3 * 16], BF16)
        nmT = sb("nmT", [48, 2, 256], BF16)
        rden = sb("rden", [P, 2, 4])
        tmp = sb("tmp", [P, 512])
        tmp2 = sb("tmp2", [P, 512])
        y_t = sb("y_t", [P, 256])
        vs = sb("vs", [P, 3, 2])
        lg = sb("lg", [P, NB, 16])
        r8 = sb("r8", [P, 6, NB])
        idx = sb("idx", [P, 2, NB], I32)

        psB = pb("psB", [P, BANKS, 512])
        psT = pb("psT", [P, 2, 1024])
        psO = pb("psO", [P, 2, 256])

        ra, rb, rc, oh, cm = [Pt[:, 2, 128 * i:128 * (i + 1)].rearrange("p (b e) -> p b e", b=NB)
                              for i in range(5)]
        sg = Pt[:, 0:2, 0:512]
        xe = qf[:, :, 0:256]
        xeT = qf[:, :, 256:512].rearrange("p r (k n) -> p r k n", k=2)
        eo = Oe

        sx = xn[:, 0:4, :]
        so = xn[:, 4:8, :]
        htok = Pt[:, 0:2, 512:1024]
        hT = ctx_t
        gathered_x = xn_t[:, :, :].rearrange("p k n -> p (k n)").rearrange("p (b n) -> p b n", b=NB)

        htok2 = Pt[:, 0:2, 512:640]
        hT2 = Pt[:, 0:2, 640:768]
        ge2 = [ctx_s, ctx_t[:, :, :].rearrange("p k n -> p (k n)").rearrange("p (b n) -> p b n", b=NB)]

        more = whole[:, SLOTW + 17408:]

        xd = nc.dram_tensor("scr_sorted", [TILES2 * P, D], F32).ap()
        sod = nc.dram_tensor("scr_sorted_out", [TILES2 * P, D], F32).ap()
        dq = [nc.dram_tensor(f"scr_q{i}", [3, 2 * P, 256], BF16).ap() for i in range(2)]
        dk = [nc.dram_tensor(f"scr_k{i}", [3, 2 * P, 256], BF16).ap() for i in range(2)]
        dk3 = nc.dram_tensor("scr_k3", [3, 2 * P, NT], BF16).ap()
        dv3 = nc.dram_tensor("scr_v3", [P, NB * 16, EW], BF16).ap()
        eod = nc.dram_tensor("scr_expert_out", [NT, D], F32).ap()

        def row(name):
            return rows[:, row_at[name][0]:row_at[name][1]]

        def col(name, j=0, n=P):
            return cols[0:n, col_at[name][0] + j:col_at[name][0] + j + 1]

        def const(name):
            return cst[:, cst_at[name][0]:cst_at[name][1]]

        first_in = sem("first_in")
        const_in = sem("const_in")
        rest_in = sem("rest_in")
        cols_done = sem("cols_done")
        q_zeroed, k_zeroed = sem("q_zeroed"), sem("k_zeroed")
        expert_in = [[sem(f"expert_in{j}_{i}") for i in range(4)] for j in range(2)]
        w_in = pair("w_in")
        earlier_in = sem("earlier_in")
        ctx_in = sem("ctx_in")
        w3_in = sem("w3_in")
        var_ready = sem("var_ready")
        rstd_ready = sem("rstd_ready")
        xn_ready = sem("xn_ready")
        bank_ready, bank_used = ring("bank_ready"), ring("bank_used")
        T_ready, T_used = pair("T_ready"), pair("T_used")
        O_used = pair("O_used")
        PV_done = sem("PV_done")
        parts_q = sem("parts_q")
        parts_k = sem("parts_k")
        v_blocks = sem("v_blocks")
        V_copied = sem("V_copied")
        q_stored, k_stored = pair("q_stored"), pair("k_stored")
        q_packed, k_packed = pair("q_packed"), pair("k_packed")
        v3_stored = sem("v3_stored")
        v3_in = sem("v3_in")
        k3_in = sem("k3_in")
        k_ones = sem("k_ones")
        neg_split = sem("neg_split")
        neg_in = pair("neg_in")
        exp_done = sem("exp_done")
        clipped = sem("clipped")
        rounded = sem("rounded")
        quant_q = sem("quant_q")
        v_quant = sem("v_quant")
        delta_var = sem("delta_var")
        delta_rstd = sem("delta_rstd")
        silu_done = sem("silu_done")
        gates_done = sem("gates_done")
        route_a = sem("route_a")
        route_b = sem("route_b")
        route_pe = sem("route_pe")
        routed = sem("routed")
        zero_in = sem("zero_in")
        scattered = sem("scattered")
        xe_in = pair("xe_in")
        eo_out = pair("eo_out")
        gathered = [sem(f"gathered{b}") for b in range(NB)]
        combined = sem("combined")
        sorted_in = [sem(f"sorted_in{i}") for i in range(4)]
        sorted_out = [sem(f"sorted_out{i}") for i in range(4)]
        scattered2, scattered3 = sem("scattered2"), sem("scattered3")
        gathered2 = [sem(f"gathered2_{b}") for b in range(NB)]
        routed2, hidden2 = sem("routed2"), sem("hidden2")
        combined2 = sem("combined2")
        gathered3 = [sem(f"gathered3_{b}") for b in range(NB)]
        routed3 = sem("routed3")
        experts_in = sem("experts_in")
        hidden3 = sem("hidden3")
        combined3 = sem("combined3")
        out_done = sem("out_done")
        dve_chain = sem("dve_chain")
        pool_chain = sem("pool_chain")

        def hidden(layer):
            return Hb if layer == 1 else Hb2

        def uses2(i):
            return (TILES2 - 1 - i) // 4 + 1

        def turn(eng, ready, n):
            eng.wait_ge(ready[n % len(ready)], n // len(ready) + 1)

        def free(eng, used, n):
            if n >= len(used):
                eng.wait_ge(used[n % len(used)], n // len(used))

        def o_slot(A, n):
            return psT[:, n % 2, 512:512 + A.T] if A.layer == 2 else psO[:, n % 2, 0:A.T]

        def p_slot(A, n):
            return more[:, 0:1024] if A.layer == 3 and n % 4 == 3 else Pt[:, n % (4 if A.layer == 3 else 3), :]

        def n_slot(n):
            return more[:, 1024:1536].bitcast(BF16) if n % 3 == 2 else nb16[:, n % 3, :]

        def m_slot(n):
            return psB[:, n % BANKS, 0:256]

        def evacuated(eng, n):
            turn(eng, bank_used, n)

        def scratch(tiles, A, g):
            if A.halves == 2:
                return tiles[g % 2]
            return tiles[g % 2].rearrange("c p n -> (c p) n")[0:3 * P, :].rearrange("(c p) n -> c p n", p=P)

        def kslot(A, u):
            return KP[:, :] if A.layer == 3 else KP[:, 4096 * (u.g % 3):4096 * (u.g % 3 + 1)]

        def wait_packs(pe, s):
            g = s.un.g
            pe.wait_ge(q_packed[g % 2], s.un.packed)
            if s.A.layer < 3:
                pe.wait_ge(k_packed[g % 2], s.un.packed)
            else:
                pe.wait_ge(k3_in, 48 * len(K3_AT))

        block = ctx.enter_context(nc.Block())

        @block.sync
        def _(sp):
            sp.dma_start(x[:, 0, :], t["x"][0]).then_inc(first_in, 16)
            sp.dma_start(cst[:, :], t["cst"]).then_inc(first_in, 16)
            sp.dma_start(cols[:, :], t["cols"]).then_inc(first_in, 16)
            sp.dma_start(w_at0[:, :, :], t["w_at0"]).then_inc(first_in, 16)
            sp.dma_start(ctx_s[:, 0, :], t["ctx"][0]).then_inc(first_in, 16)
            sp.dma_start(ident16[:, :], t["ident16"]).then_inc(const_in, 16)
            sp.dma_start(rows[:, :], t["rows"].partition_broadcast(P)).then_inc(const_in, 16)
            sp.dma_start(mask_i[:, :], t["mask"]).then_inc(const_in, 16)
            sp.dma_start(x[:, 1:2, :], t["x"][1:2].rearrange("b p d -> p b d")).then_inc(const_in, 16)
            sp.dma_start(ctx_s[:, 1:2, :], t["ctx"][1:2].rearrange("b p d -> p b d")).then_inc(const_in, 16)
            sp.dma_start(wr[:, :, :], t["wr"]).then_inc(const_in, 16)
            for s in steps:
                if s.kind == "barrier":
                    sp.wait_ge(rstd_ready, s.stats)
                elif s.kind == "attn_begin":
                    A = s.A
                    if A.has_max:
                        for r in range(4 if A.layer == 3 else 3):
                            sp.dma_start(KP[96:99, 4096 * r:4096 * (r + 1)], t["ones3"]).then_inc(k_ones, 16)
                elif s.kind == "vstore":
                    turn(sp, bank_used, s.m)
                    sp.dma_start(dv3, VQ_made[:, :, :]).then_inc(v3_stored, 16)
                elif s.kind == "w3load":
                    sp.dma_start(w_at2[:, :, :, :], t[s.item]).then_inc(w3_in, 16)
                    if s.item == "w_at2":
                        sp.dma_start(earlier, t["earlier"]).then_inc(earlier_in, 16)
                        sp.dma_start(powers, t["powers"]).then_inc(earlier_in, 16)
                elif s.kind == "wload":
                    i, slot = s.item, s.item % 2
                    if s.free is not None:
                        turn(sp, bank_ready, s.free)
                    if i == 11:
                        sp.wait_ge(w_in[1], 16)
                    w = t[f"w{i}"]
                    sp.dma_start(whole[:, W_AT[i]:W_AT[i] + w.shape[1]], w).then_inc(w_in[slot], 16)
                elif s.kind == "t_load":
                    sp.wait_ge(scattered2, 16 * 2 * NB)
                    for i in range(4):
                        sp.dma_start(sx[:, i, :], xd[i * P:(i + 1) * P, :]).then_inc(sorted_in[i], 16)
                elif s.kind == "k3load":
                    if s.i == 0:
                        turn(sp, bank_ready, s.m)
                        sp.wait_ge(v3_stored, 16)
                        sp.dma_start(VQ[:, :, :], dv3).then_inc(v3_in, 16)
                    pack(sp, ATT[3], KP[:, :], dk3, NT, k3_in, is_q=False, heads=(4 * s.i, 4 * s.i + 4))
                elif s.kind == "tx":
                    if s.i + 4 < TILES2:
                        turn(sp, bank_ready, s.m)
                        sp.dma_start(sx[:, s.i % 4, :], xd[(s.i + 4) * P:(s.i + 5) * P, :]).then_inc(sorted_in[s.i % 4], 16)
                elif s.kind == "td":
                    turn(sp, bank_used, s.s)
                    sp.dma_start(sod[s.i * P:(s.i + 1) * P, :], so[:, s.i % 4, :]).then_inc(sorted_out[s.i % 4], 16)
                elif s.kind == "loads":
                    i = s.i
                    if i < 8:
                        e, q = i // 4, i % 4
                        sp.dma_start(expert(e, q * 1024, 1024), t[f"w{e}"][:, q * 1024:(q + 1) * 1024]
                                     ).then_inc(expert_in[q // 2][e], 16)
                    elif i == 8:
                        sp.dma_start(ctx_t[:, :, :], t["ctx_t"]).then_inc(ctx_in, 16)
                    elif i == 9:
                        sp.dma_start(w_at2[:, :, :, :], t["w_at3"]).then_inc(w3_in, 16)
                    else:
                        r0, r1 = (i - 10) * NT, min((i - 9) * NT, TILES2 * P)
                        sp.dma_start(xd[r0:r1, :], t["zeros"][0:r1 - r0, :]).then_inc(zero_in, 16)
                elif s.kind == "eload":
                    if s.free is not None:
                        turn(sp, bank_ready if s.j else T_ready, s.free)
                    for q in (2 * s.j, 2 * s.j + 1):
                        sp.dma_start(expert(s.i, q * 1024, 1024), t[f"w{s.i}"][:, q * 1024:(q + 1) * 1024]
                                     ).then_inc(expert_in[s.j][s.i % 4], 16)
                elif s.kind == "store":
                    A, u = s.A, s.un
                    w = A.halves * A.T // 2

                    def store(dst, src, sem):
                        for m in range(2):
                            rows_ = slice(m * P, (m + 1) * P) if A.halves == 2 else slice(0, P)
                            at = 0 if A.halves == 2 else m * w
                            sp.dma_start(dst[:, rows_, at:at + w].rearrange("c p n -> p c n"),
                                         src[:, :, m * w:(m + 1) * w]).then_inc(sem, 16)
                    if s.kind_of == "qk":
                        sp.wait_ge(parts_q, u.g + 1)
                        if u.g >= 2:
                            sp.wait_ge(q_packed[u.g % 2], u.packed_before)
                        store(scratch(dq, A, u.g), sq[:, u.g % 2], q_stored[u.g % 2])
                    if u.k is not None:
                        sp.wait_ge(parts_k, u.k + 1)
                        if s.kind_of == "k":
                            store(dk3[:, :, u.u * 256:(u.u + 1) * 256], sk[:, u.k % 2], k_stored[u.k % 2])
                        else:
                            if u.g >= 2:
                                sp.wait_ge(k_packed[u.g % 2], u.packed_before)
                            store(scratch(dk, A, u.g), sk[:, u.k % 2], k_stored[u.k % 2])
                elif s.kind == "packs":
                    A, u = s.A, s.un
                    if s.done_before >= 0:
                        sp.wait_ge(PV_done, s.done_before + 1)
                    sp.wait_ge(q_stored[u.g % 2], 32 * (u.g // 2 + 1))
                    if A.layer == 0 and u.u < 3:
                        sp.wait_ge(q_zeroed, u.u + 1)
                        sp.wait_ge(k_zeroed, 2 * (u.u + 1))
                    pack(sp, A, QP[:, u.g % 3, :], scratch(dq, A, u.g), A.T, q_packed[u.g % 2], is_q=True)
                    if u.k is not None:
                        sp.wait_ge(k_stored[u.k % 2], 32 * (u.k // 2 + 1))
                        pack(sp, A, KP[:, 4096 * (u.g % 3):4096 * (u.g % 3 + 1)], scratch(dk, A, u.g), A.T,
                             k_packed[u.g % 2], is_q=False)
                    if A.layer == 0 and u.u == 0:
                        sp.dma_start(x[:, 2:NB, :], t["x"][2:NB].rearrange("b p d -> p b d")).then_inc(rest_in, 16)
                        sp.dma_start(ctx_s[:, 2:NB, :], t["ctx"][2:NB].rearrange("b p d -> p b d")).then_inc(rest_in, 16)
                elif s.kind == "negmax":
                    A = s.A
                    turn(sp, bank_used, s.m)
                    for p3 in range(3):
                        r = 96 + p3
                        HP = A.H // A.parts
                        sp.dma_start(QP[r:r + 1, s.un.g % 3, s.j * HP * A.T:(s.j + 1) * HP * A.T],
                                     nmT[p3 * HP:(p3 + 1) * HP, s.i % 2, 0:A.T]).then_inc(neg_in[s.i % 2], 16)
                elif s.kind == "ext":
                    e = s.i
                    if e == 0:
                        sp.wait_ge(scattered, 16 * NB)
                    for k in [0, 1] if e == 0 else ([e + 1] if e + 1 < 8 else []):
                        if k >= 2:
                            turn(sp, bank_ready, ext_m[k - 2])
                        sp.dma_start(xe[:, k % 2, 0:256], xd[k * P:(k + 1) * P, :]).then_inc(xe_in[k % 2], 16)
                elif s.kind == "w3first":
                    sp.wait_ge(w_in[0], 16 * 3)
                    sp.sem_inc(experts_in, 16)
                    sp.wait_ge(PV_done, s.p + 1)
                    sp.dma_start(whole[:, SLOTW:2 * SLOTW], t["w13"]).then_inc(experts_in, 16)
                elif s.kind == "sx_load":
                    sp.wait_ge(experts_in, 32)
                    sp.dma_start(whole[:, 2 * SLOTW:3 * SLOTW], t["w14"]).then_inc(experts_in, 16)
                    sp.wait_ge(experts_in, 48)
                    sp.dma_start(whole[:, 3 * SLOTW:4 * SLOTW], t["w15"]).then_inc(experts_in, 16)
                elif s.kind == "combine3":
                    sp.wait_ge(combined3, s.b + 1)
                    sp.dma_start(out[s.b], x[:, s.b, :]).then_inc(out_done, 16)
                elif s.kind == "exd":
                    e = s.i
                    turn(sp, bank_used, s.s)
                    sp.dma_start(eod[e * P:(e + 1) * P, :], eo[:, e % 2, :]).then_inc(eo_out[e % 2], 16)
            sp.wait_ge(out_done, 16 * NB)

        @block.tensor
        def _(pe):
            ident = const("ident")

            def m_begin(n):
                free(pe, bank_used, n)
                return m_slot(n)

            def project(dst, lhs, rhs, halves):
                for kd in range(halves):
                    ins = pe.matmul(dst, lhsT=lhs(kd), rhs=rhs(kd), start=(kd == 0), stop=(kd == halves - 1))
                return ins

            def turn_x(n, xs):
                dst = m_begin(n)
                pe.wait_ge(xn_ready, xs.i + 1)
                for kd in range(2):
                    ins = pe.transpose(dst[:, kd * P:(kd + 1) * P], xn[:, xs.b, kd * P:(kd + 1) * P], ident)
                ins.then_inc(bank_ready[n % BANKS], 1)

            w_seen = set()

            def weights(item):
                if item not in w_seen:
                    w_seen.add(item)
                    pe.wait_ge(w_in[item % 2], 16 * ((item - 8) // 2 + 1))

            word = [None]

            def tile_expert(i, most):
                if i % 4 == 0:
                    word[0] = pe.value_load(te[0:1, i // 4:i // 4 + 1], min_val=0, max_val=65535)
                return pe.snap((word[0] // 16 ** (i % 4)) % (most + 1), min_val=0, max_val=most)

            pe.wait_ge(first_in, 16 * 5)
            for s in steps:
                if s.kind == "barrier":
                    pe.wait_ge(rstd_ready, s.stats)
                elif s.kind == "attn_begin":
                    if s.A.layer == 2:
                        pe.wait_ge(w3_in, 32)
                    if s.A.layer == 3:
                        pe.wait_ge(w3_in, 48)
                elif s.kind == "prepare":
                    pe.wait_ge(const_in, 16 * 6)
                elif s.kind == "kp":
                    dst = m_begin(s.m)
                    tok = (2 * s.u + s.j) * P
                    project(dst, lambda kd: ctx_t[:, kd, tok:tok + P], lambda kd: w_at2[:, 1, kd, :], 2
                            ).then_inc(bank_ready[s.m % BANKS], 1)
                elif s.kind in ("kt", "fqt"):
                    dst = m_begin(s.m)
                    pe.wait_ge(quant_q, s.i + 1)
                    for j in range(s.un.A.nb):
                        ins = pe.transpose(dst[:, j * P:(j + 1) * P], tmp2[:, j * 256 + s.c * P:j * 256 + (s.c + 1) * P], ident)
                    ins.then_inc(bank_ready[s.m % BANKS], 1)
                elif s.kind == "vp":
                    dst = m_begin(s.m)
                    if s.u == 0 and s.c == 0:
                        pe.wait_ge(ctx_in, 16)
                        pe.wait_ge(w3_in, 16)
                    tok = 2 * s.u * P
                    project(dst, lambda kd: w_at2[:, 2, kd, s.c * P:(s.c + 1) * P],
                            lambda kd: ctx_t[:, kd, tok:tok + 256], 2).then_inc(bank_ready[s.m % BANKS], 1)
                elif s.kind == "vturn":
                    dst = m_begin(s.m).bitcast(BF16)
                    pe.wait_ge(v_quant, 2)
                    for m in range(2):
                        ins = pe.transpose(dst[:, m * P:(m + 1) * P], vi[:, m, s.c * P:(s.c + 1) * P], ident16[:, :])
                    ins.then_inc(bank_ready[s.m % BANKS], 1)
                elif s.kind in ("fx", "xt"):
                    turn_x(s.m, s.xn)
                elif s.kind in ("fq", "fk") and s.A.layer == 0:
                    dst = m_begin(s.m)
                    if s.kind == "fq":
                        pe.wait_ge(xn_ready, s.un.xn.i + 1)
                    if s.un.u == 2:
                        pe.wait_ge(rest_in, 32)
                    k, src = (0, xn) if s.kind == "fq" else (1, ctx_s)
                    pe.matmul(dst, lhsT=w_at0[:, k, :], rhs=src[:, s.un.u, :], start=True, stop=True
                              ).then_inc(bank_ready[s.m % BANKS], 1)
                elif s.kind == "fv" and s.A.layer == 0:
                    dst = m_begin(s.m)
                    for c in range(2):
                        ins = pe.matmul(dst[:, c * P:(c + 1) * P], lhsT=ctx_s[:, s.un.u, c * P:(c + 1) * P],
                                        rhs=w_at0[:, 2, :], start=True, stop=True)
                    ins.then_inc(bank_ready[s.m % BANKS], 1)
                elif s.kind in ("fq", "fk"):
                    dst = m_begin(s.m)
                    k, src = (0, xn_t) if s.kind == "fq" else (1, ctx_t)
                    if k == 0:
                        evacuated(pe, s.un.m_x)
                    tok = s.un.u * P
                    for m in range(2):
                        ins = project(dst[:, m * P:(m + 1) * P], lambda kd: w_at2[:, k, kd, m * P:(m + 1) * P],
                                      lambda kd: src[:, kd, tok:tok + P], 2)
                    ins.then_inc(bank_ready[s.m % BANKS], 1)
                elif s.kind == "fv":
                    dst = m_begin(s.m)
                    tok = s.un.u * P
                    project(dst, lambda kd: ctx_t[:, kd, tok:tok + P], lambda kd: w_at2[:, 2, kd, :], 2
                            ).then_inc(bank_ready[s.m % BANKS], 1)
                elif s.kind == "fq3":
                    dst = m_begin(s.m)
                    evacuated(pe, s.m_prev)
                    tok = (s.un.b0 + s.j) * P
                    project(dst, lambda kd: xn_t[:, kd, tok:tok + P], lambda kd: w_at2[:, 0, kd, :], 2
                            ).then_inc(bank_ready[s.m % BANKS], 1)
                elif s.kind == "smax":
                    A, u, K = s.A, s.un, 96
                    if s.first:
                        wait_packs(pe, s)
                    free(pe, bank_used, s.n)
                    dst = psB[:, s.n % BANKS, :]
                    q_at, k_at = QP[0:K, u.g % 3, :], kslot(A, u)[0:K, :]
                    if A.layer == 3:
                        h, half = s.j // 2, s.j % 2
                        ins = pe.matmul(dst, lhsT=q_at[:, h * A.T + s.tc * P:h * A.T + (s.tc + 1) * P],
                                        rhs=k_at[:, h * NT + half * 512:h * NT + (half + 1) * 512],
                                        start=True, stop=True)
                    else:
                        for i in range(2):
                            h = 2 * s.j + i
                            ins = pe.matmul(dst[:, i * 256:(i + 1) * 256],
                                            lhsT=q_at[:, h * A.T + s.tc * P:h * A.T + (s.tc + 1) * P],
                                            rhs=k_at[:, h * A.T:(h + 1) * A.T], start=True, stop=True)
                    ins.then_inc(bank_ready[s.n % BANKS], 1)
                elif s.kind == "negmax":
                    A = s.A
                    dst = m_begin(s.m).bitcast(BF16)
                    pe.wait_ge(neg_split, s.i + 1)
                    w = 3 * A.H // A.parts
                    for tc in range(A.TC):
                        ins = pe.transpose(dst[0:w, tc * P:(tc + 1) * P], npt[:, s.i % 2, tc * w:(tc + 1) * w],
                                           ident16[:, :])
                    ins.then_inc(bank_ready[s.m % BANKS], 1)
                elif s.kind == "st":
                    A, u = s.A, s.un
                    K = 99 if A.has_max else 96
                    if s.neg is not None:
                        pe.wait_ge(neg_in[s.neg % 2], 48 * (s.neg // 2 + 1))
                    if s.first:
                        if A.has_max:
                            pe.wait_ge(k_ones, 16 * {0: 3, 1: 6, 3: 10}[A.layer])
                        else:
                            wait_packs(pe, s)
                    free(pe, T_used, s.n)
                    q_at, k_at = QP[0:K, u.g % 3, :], kslot(A, u)[0:K, :]
                    kw = NT if A.layer == 3 else A.T if A.layer < 2 else P
                    for i in range(4):
                        h = 4 * s.g + i
                        ins = pe.matmul(psT[:, s.n % 2, i * A.T:(i + 1) * A.T],
                                        lhsT=k_at[:, h * kw + s.c * P:h * kw + (s.c + 1) * P],
                                        rhs=q_at[:, h * A.T:(h + 1) * A.T], start=True, stop=True)
                    ins.then_inc(T_ready[s.n % 2], 1)
                elif s.kind == "pv":
                    A, u = s.A, s.un
                    if A.layer == 2:
                        pe.wait_ge(exp_done, s.clip + 1)
                    else:
                        turn(pe, T_used, s.n)
                    if A.layer == 3:
                        pe.wait_ge(rounded, s.clip3 + 1)
                    if s.g == 0 and s.c == 0:
                        if A.layer == 0:
                            evacuated(pe, u.m_v)
                        elif A.layer == 1:
                            pe.wait_ge(V_copied, u.u + 1)
                        elif A.layer == 2:
                            evacuated(pe, u.m_v)
                        else:
                            pe.wait_ge(v3_in, 16)
                    if s.c == 0 and A.layer == 2:
                        free(pe, O_used, s.o)
                    elif s.c == 0 and s.o >= 1:
                        turn(pe, O_used, s.o - 1)
                    for i in range(4):
                        h = 4 * s.g + i
                        dst = o_slot(A, s.o)[32 * i:32 * (i + 1), :]
                        pr = p_slot(A, s.p)[:, i * A.T:(i + 1) * A.T]
                        first, last = s.c == 0, s.c == A.NC - 1
                        if A.layer < 3:
                            ins = pe.matmul(dst, lhsT=VA[:, u.g % 3, s.c * A.H + h, :], rhs=pr, start=first, stop=last)
                        else:
                            pe.matmul(dst, lhsT=VQ[:, s.c * A.H + h, :], rhs=n_slot(s.p)[:, i * A.T:(i + 1) * A.T],
                                      start=first, stop=False)
                    if A.layer == 3:
                        for i in range(4):
                            dst = o_slot(A, s.o)[32 * i:32 * (i + 1), :]
                            pr = p_slot(A, s.p)[:, i * A.T:(i + 1) * A.T]
                            ins = pe.matmul(dst, lhsT=const("sumsel"), rhs=pr, start=False, stop=last)
                    ins.then_inc(PV_done, 1)
                elif s.kind == "onorm":
                    A = s.A
                    turn(pe, O_used, s.o)
                    dst = m_begin(s.m)
                    for tc in range(A.TC):
                        ins = pe.transpose(dst[:, tc * P:(tc + 1) * P], Oe[:, s.o % 2, tc * P:(tc + 1) * P], ident)
                    ins.then_inc(bank_ready[s.m % BANKS], 1)
                elif s.kind == "ot":
                    A, u = s.A, s.un
                    dst = m_begin(s.m)
                    evacuated(pe, s.m_last_norm)
                    HD = A.H * A.d
                    for j in range(2):
                        at = j * P if A.layer == 2 else j * HD + s.c * P
                        ins = pe.transpose(dst[:, j * P:(j + 1) * P], On[:, u.g % 2, at:at + P], ident)
                    ins.then_inc(bank_ready[s.m % BANKS], 1)
                elif s.kind == "oy":
                    A = s.A
                    dst = m_begin(s.m)
                    for m in s.un.m_t:
                        evacuated(pe, m)
                    if A.layer == 0:
                        ins = pe.matmul(dst, lhsT=w_at0[:, 3, :], rhs=OnT[:, 0, :], start=True, stop=True)
                    elif A.layer == 2:
                        ins = project(dst, lambda m: OnT[:, 0, m * P:(m + 1) * P], lambda m: w_at2[:, 3, m, :], 2)
                    else:
                        ins = project(dst, lambda m: OnT[:, m, s.j * P:(s.j + 1) * P], lambda m: w_at2[:, 3, m, :], 2)
                    ins.then_inc(bank_ready[s.m % BANKS], 1)
                elif s.kind == "xl":
                    dst = m_begin(s.m)
                    evacuated(pe, s.m_prev)
                    a, n = {0: (0, 8), 2: (8, 16), 3: (24, 4)}[s.layer]
                    tok = s.b * P
                    project(dst[:, 0:n], lambda kd: xn_t[:, kd, tok:tok + P], lambda kd: wr[:, kd, a:a + n], 2
                            ).then_inc(bank_ready[s.m % BANKS], 1)
                elif s.kind == "route" and s.layer == 0:
                    dst = m_begin(s.m)
                    pe.wait_ge(route_pe, 1)
                    pe.matmul(dst[:, 0:64], lhsT=const("before"), rhs=oh[:, :, 0:8], start=True, stop=False)
                    pe.matmul(dst[:, 0:64], lhsT=const("ones"), rhs=rc[:, :, 0:8], start=False, stop=True
                              ).then_inc(bank_ready[s.m % BANKS], 1)
                elif s.kind == "route" and s.layer == 2:
                    dst = m_begin(s.m)
                    pe.wait_ge(route_pe, 2)
                    pe.matmul(dst[:, 0:128], lhsT=const("before"), rhs=cm[:, :, :], start=True, stop=False)
                    pe.matmul(dst[:, 0:128], lhsT=const("ones"), rhs=rc[:, :, :], start=False, stop=True)
                    pe.matmul(dst[:, 128:144], lhsT=const("ones"), rhs=ra[:, 0, :], start=True, stop=True
                              ).then_inc(bank_ready[s.m % BANKS], 1)
                elif s.kind == "tx":
                    dst = m_begin(s.m)
                    pe.wait_ge(sorted_in[s.i % 4], 16 * (s.i // 4 + 1))
                    for kd in range(2):
                        ins = pe.transpose(dst[:, kd * P:(kd + 1) * P], sx[:, s.i % 4, kd * P:(kd + 1) * P], ident)
                    ins.then_inc(bank_ready[s.m % BANKS], 1)
                elif s.kind == "tu":
                    if s.i == 0:
                        weights(10)
                        weights(11)
                    s.un.k = tile_expert(s.i, 15)
                    evacuated(pe, s.m_x)
                    free(pe, T_used, s.n)
                    for kd in range(2):
                        ins = pe.matmul(psT[:, s.n % 2, 0:256], lhsT=xeT[:, s.i % 2, kd, :],
                                        rhs=whole[:, bass.ds(s.un.k * 768 + kd * 256, 256)], start=(kd == 0), stop=(kd == 1))
                    ins.then_inc(T_ready[s.n % 2], 1)
                elif s.kind == "th":
                    dst = m_begin(s.m)
                    pe.wait_ge(hidden2, s.i + 1)
                    pe.transpose(dst[:, 0:P], htok2[:, s.i % 2, :], ident).then_inc(bank_ready[s.m % BANKS], 1)
                elif s.kind == "td":
                    dst = m_begin(s.s)
                    evacuated(pe, s.m)
                    pe.matmul(dst, lhsT=hT2[:, s.i % 2, :], rhs=whole[:, bass.ds(s.un.k * 768 + 512, 256)],
                              start=True, stop=True).then_inc(bank_ready[s.s % BANKS], 1)
                elif s.kind == "route" and s.layer == 3:
                    dst = m_begin(s.m)
                    pe.wait_ge(route_pe, 3)
                    pe.matmul(dst[:, 0:32], lhsT=const("before"), rhs=oh[:, :, 0:4], start=True, stop=False)
                    pe.matmul(dst[:, 0:32], lhsT=const("ones"), rhs=rc[:, :, 0:4], start=False, stop=True)
                    pe.matmul(dst[:, 32:36], lhsT=const("ones"), rhs=rc[:, 0, 8:12], start=True, stop=True
                              ).then_inc(bank_ready[s.m % BANKS], 1)
                elif s.kind == "sx":
                    dst = m_begin(s.m)
                    pe.wait_ge(sorted_in[s.i % 4], 16 * (uses2(s.i % 4) + s.i // 4 + 1))
                    for kd in range(2):
                        ins = pe.transpose(dst[:, kd * P:(kd + 1) * P], sx[:, s.i % 4, kd * P:(kd + 1) * P], ident)
                    ins.then_inc(bank_ready[s.m % BANKS], 1)
                elif s.kind == "su":
                    if s.j == 0:
                        if s.i == 0:
                            pe.wait_ge(routed3, 1)
                        s.un.k = tile_expert(s.i, 3)
                        pe.wait_ge(experts_in, s.un.k * 16 + 16)
                        evacuated(pe, s.m_x)
                    free(pe, T_used, s.n)
                    for k in range(2):
                        for kd in range(2):
                            at = k * 2048 + kd * 1024 + s.j * 512
                            ins = pe.matmul(psT[:, s.n % 2, k * 512:(k + 1) * 512], lhsT=xeT[:, s.i % 2, kd, :],
                                            rhs=whole[:, bass.ds(s.un.k * SLOTW + at, 512)], start=(kd == 0), stop=(kd == 1))
                    ins.then_inc(T_ready[s.n % 2], 1)
                elif s.kind == "sh":
                    free(pe, bank_used, s.m)
                    pe.wait_ge(hidden3, s.g + 1)
                    for c in range(4):
                        ins = pe.transpose(psB[:, s.m % BANKS, c * P:(c + 1) * P], htok[:, s.g % 2, c * P:(c + 1) * P], ident)
                    ins.then_inc(bank_ready[s.m % BANKS], 1)
                elif s.kind == "sd":
                    free(pe, bank_used, s.s)
                    for m in s.un.m:
                        evacuated(pe, m)
                    for c in range(8):
                        ins = pe.matmul(m_slot(s.s), lhsT=hT[:, s.i % 2, c * P:(c + 1) * P],
                                        rhs=whole[:, bass.ds(s.un.k * SLOTW + 4096 + c * 256, 256)],
                                        start=(c == 0), stop=(c == 7))
                    ins.then_inc(bank_ready[s.s % BANKS], 1)
                elif s.kind == "ext":
                    e = s.i
                    dst = m_begin(s.m)
                    pe.wait_ge(xe_in[e % 2], 16 * (e // 2 + 1))
                    for kd in range(2):
                        ins = pe.transpose(dst[:, kd * P:(kd + 1) * P], xe[:, e % 2, kd * P:(kd + 1) * P], ident)
                    ins.then_inc(bank_ready[s.m % BANKS], 1)
                elif s.kind == "exu":
                    e = s.i
                    pe.wait_ge(expert_in[0][e % 4], 32 * (e // 4 + 1))
                    free(pe, T_used, s.n)
                    evacuated(pe, s.m)
                    for ch in range(8):
                        ins = project(psT[:, s.n % 2, ch * P:(ch + 1) * P],
                                      lambda kd: expert(e, kd * 1024 + ch * P, P),
                                      lambda kd: xeT[:, e % 2, kd, :], 2)
                    ins.then_inc(T_ready[s.n % 2], 1)
                elif s.kind == "exd":
                    e = s.i
                    pe.wait_ge(expert_in[1][e % 4], 32 * (e // 4 + 1))
                    free(pe, bank_used, s.s)
                    turn(pe, T_used, s.n)
                    for ch in range(8):
                        ins = pe.matmul(psB[:, s.s % BANKS, 0:256], lhsT=Pt[:, e % 2, ch * P:(ch + 1) * P],
                                        rhs=expert(e, 2048 + ch * 256, 256), start=(ch == 0), stop=(ch == 7))
                    ins.then_inc(bank_ready[s.s % BANKS], 1)
                elif s.kind == "gu":
                    W, F, ch, w = whole[:, W_AT[s.blk.item]:], s.blk.F, s.ch, s.width
                    weights(s.blk.item)
                    if s.ch == 0:
                        evacuated(pe, s.m)
                    free(pe, T_used, s.n)
                    for k in range(2):
                        at = s.blk.off + k * 2 * F + ch * P
                        ins = project(psT[0:w, s.n % 2, k * 512:(k + 1) * 512],
                                      lambda kd: W[:, at + kd * F:at + kd * F + w],
                                      lambda kd: xn_t[:, kd, s.tg * 512:(s.tg + 1) * 512], 2)
                    ins.then_inc(T_ready[s.n % 2], 1)
                elif s.kind == "down":
                    W, off = whole[:, W_AT[s.blk.item]:], s.blk.off + 4 * s.blk.F
                    free(pe, bank_used, s.n)
                    if s.tc == 0:
                        turn(pe, T_used, s.last_T)
                        if s.last_T >= 1:
                            turn(pe, T_used, s.last_T - 1)
                    last = len(s.blk.widths) - 1
                    for ch, w in enumerate(s.blk.widths):
                        ins = pe.matmul(psB[:, s.n % BANKS, 0:256], lhsT=hidden(s.layer)[0:w, s.h % 2, ch, s.tc * P:(s.tc + 1) * P],
                                        rhs=W[0:w, off + ch * 256:off + (ch + 1) * 256], start=(ch == 0), stop=(ch == last))
                    ins.then_inc(bank_ready[s.n % BANKS], 1)

        @block.scalar
        def _(act):
            act.wait_ge(first_in, 16 * 5)
            act.wait_ge(cols_done, 1)
            for s in steps:
                if s.kind == "barrier":
                    act.wait_ge(rstd_ready, s.stats)
                elif s.kind == "prepare":
                    act.wait_ge(const_in, 16 * 6)
                    act.activation(tg[:, 0:8], rows[:, 0:8], ACT.Tanh).then_inc(gates_done, 1)
                elif s.kind == "zero":
                    at = 6144 + 2048 * s.i
                    for p in (32, 64):
                        act.activation(arena[p:p + 32, at:at + 2048], const("zero")[p:p + 32, :].to_broadcast([32, 2048]),
                                       ACT.Copy).then_inc(k_zeroed, 1)
                elif s.kind == "kt":
                    if s.un.k >= 2:
                        act.wait_ge(parts_k, s.un.k - 1)
                    turn(act, bank_ready, s.m)
                    act.activation(kf[:, s.un.k % 2, s.c * 256:(s.c + 1) * 256], m_slot(s.m), ACT.Copy
                                   ).then_inc(bank_used[s.m % BANKS], 1)
                elif s.kind == "vp":
                    turn(act, bank_ready, s.m)
                    act.activation(vf[:, s.c, s.u * 256:(s.u + 1) * 256], m_slot(s.m), ACT.Identity,
                                   bias=col("bv3", s.c)).then_inc(bank_used[s.m % BANKS], 1)
                elif s.kind in ("fx", "xt"):
                    b = s.xn.b
                    turn(act, bank_ready, s.m)
                    act.activation(xn_t[:, :, b * P:(b + 1) * P], m_slot(s.m).rearrange("p (k n) -> p k n", k=2),
                                   ACT.Copy).then_inc(bank_used[s.m % BANKS], 1)
                elif s.kind in ("fq", "fk"):
                    A, is_q = s.A, s.kind == "fq"
                    i = s.un.g if is_q else s.un.k
                    if i >= 2:
                        act.wait_ge(parts_q if is_q else parts_k, i - 1)
                    dst = (qf if is_q else kf)[:, i % 2, :]
                    scale = float(A.d) ** -0.5 if is_q else 1.0
                    turn(act, bank_ready, s.m)
                    if A.layer == 0:
                        ins = act.activation(dst[:, 0:256], m_slot(s.m), ACT.Identity, scale=scale,
                                             bias=colx[:, 0:1] if is_q else col("bk0"))
                    else:
                        for m in range(2):
                            ins = act.activation(dst[:, m * P:(m + 1) * P], m_slot(s.m)[:, m * P:(m + 1) * P],
                                                 ACT.Identity, scale=scale,
                                                 bias=colx[:, 1 + m:2 + m] if is_q else col("bk2", m))
                    ins.then_inc(bank_used[s.m % BANKS], 1)
                elif s.kind == "fqt":
                    if s.un.g >= 2:
                        act.wait_ge(parts_q, s.un.g - 1)
                    turn(act, bank_ready, s.m)
                    T = s.un.A.T
                    act.activation(qf[:, s.un.g % 2, s.c * T:(s.c + 1) * T], m_slot(s.m)[:, 0:T], ACT.Copy
                                   ).then_inc(bank_used[s.m % BANKS], 1)
                elif s.kind == "negmax":
                    A = s.A
                    turn(act, bank_ready, s.m)
                    if s.i >= 2:
                        act.wait_ge(neg_in[s.i % 2], 48 * (s.i // 2))
                    w = 3 * A.H // A.parts
                    act.activation(nmT[0:w, s.i % 2, 0:A.T], m_slot(s.m).bitcast(BF16)[0:w, 0:A.T],
                                   ACT.Copy).then_inc(bank_used[s.m % BANKS], 1)
                elif s.kind == "st":
                    A = s.A
                    depth = 4 if A.layer == 3 else 3
                    if s.p >= depth:
                        act.wait_ge(PV_done, s.p - depth + 1)
                    if A.layer == 2:
                        b = s.un.u
                        act.wait_ge(clipped, s.clip + 1)
                        act.activation(p_slot(A, s.p)[:, 0:512], nb_t[:, s.clip % 2, :], ACT.Exp,
                                       bias=att_b[:, b:b + 1], scale=att[:, b:b + 1]).then_inc(exp_done, 1)
                    else:
                        turn(act, T_ready, s.n)
                        act.activation(p_slot(A, s.p)[:, 0:4 * A.T], psT[:, s.n % 2, 0:4 * A.T], ACT.Exp).then_inc(T_used[s.n % 2], 1)
                elif s.kind == "oev":
                    A = s.A
                    act.wait_ge(PV_done, s.p + 1)
                    if s.m_prev2 is not None:
                        turn(act, bank_ready, s.m_prev2)
                    act.activation(Oe[:, s.o % 2, 0:A.T], o_slot(A, s.o), ACT.Copy).then_inc(O_used[s.o % 2], 1)
                elif s.kind == "ot" and s.A.layer != 1:
                    turn(act, bank_ready, s.m)
                    if s.m_prev is not None:
                        turn(act, bank_ready, s.m_prev)
                    scale = vs[:, 0, s.c:s.c + 1] if s.A.layer == 3 else 1.0
                    act.activation(OnT[:, s.c, :], m_slot(s.m), ACT.Copy, scale=scale).then_inc(bank_used[s.m % BANKS], 1)
                elif s.kind == "route":
                    act.wait_ge(route_a, s.exp_i + 1)
                    n = {0: 8, 2: 16, 3: 4}[s.layer]
                    act.activation(ra[:, :, 0:n], ra[:, :, 0:n], ACT.Exp, scale=-1.0 if s.layer == 2 else 1.0
                                   ).then_inc(route_b, 1)
                elif s.kind == "ext":
                    e = s.i
                    turn(act, bank_ready, s.m)
                    act.activation(xeT[:, e % 2, :, :], m_slot(s.m).rearrange("p (k n) -> p k n", k=2), ACT.Copy
                                   ).then_inc(bank_used[s.m % BANKS], 1)
                elif s.kind == "tx":
                    turn(act, bank_ready, s.m)
                    act.activation(xeT[:, s.i % 2, :, :], m_slot(s.m).rearrange("p (k n) -> p k n", k=2), ACT.Copy
                                   ).then_inc(bank_used[s.m % BANKS], 1)
                elif s.kind == "tu":
                    turn(act, T_ready, s.n)
                    act.activation(sg[:, s.sg % 2, 0:P], psT[:, s.n % 2, 0:P], ACT.Silu).then_inc(silu_done, 1)
                elif s.kind == "th":
                    turn(act, bank_ready, s.m)
                    act.activation(hT2[:, s.i % 2, :], m_slot(s.m)[:, 0:P], ACT.Copy).then_inc(bank_used[s.m % BANKS], 1)
                elif s.kind == "sx_load":
                    act.wait_ge(scattered3, 16 * NB)
                    for i in range(4):
                        act.dma_start(sx[:, i, :], xd[i * P:(i + 1) * P, :]).then_inc(sorted_in[i], 16)
                elif s.kind == "sx":
                    turn(act, bank_ready, s.m)
                    act.activation(xeT[:, s.i % 2, :, :], m_slot(s.m).rearrange("p (k n) -> p k n", k=2), ACT.Copy
                                   ).then_inc(bank_used[s.m % BANKS], 1)
                    if s.i + 4 < TILES3:
                        act.dma_start(sx[:, s.i % 4, :], xd[(s.i + 4) * P:(s.i + 5) * P, :]).then_inc(sorted_in[s.i % 4], 16)
                elif s.kind == "su":
                    turn(act, T_ready, s.n)
                    act.activation(sg[:, s.sg % 2, :], psT[:, s.n % 2, 0:512], ACT.Silu).then_inc(silu_done, 1)
                elif s.kind == "sh":
                    turn(act, bank_ready, s.m)
                    if s.m_prev is not None:
                        turn(act, bank_ready, s.m_prev)
                    act.activation(hT[:, s.i % 2, s.j * 512:(s.j + 1) * 512], psB[:, s.m % BANKS, :], ACT.Copy
                                   ).then_inc(bank_used[s.m % BANKS], 1)
                elif s.kind == "sd":
                    turn(act, bank_used, s.s)
                    act.dma_start(sod[s.i * P:(s.i + 1) * P, :], so[:, s.i % 4, :]).then_inc(sorted_out[s.i % 4], 16)
                elif s.kind == "exu":
                    turn(act, T_ready, s.n)
                    act.activation(Pt[:, s.i % 2, :], psT[:, s.n % 2, :], ACT.Gelu_apprx_tanh
                                   ).then_inc(T_used[s.n % 2], 1)
                elif s.kind == "gu":
                    w = s.width
                    turn(act, T_ready, s.n)
                    sc = col("gs1", s.ch, w) if s.layer == 1 else 1.0
                    act.activation(sg[0:w, s.sg % 2, :], psT[0:w, s.n % 2, 0:512], ACT.Silu, scale=sc
                                   ).then_inc(silu_done, 1)

        @block.vector
        def _(dve):
            chained = [0]

            def link(ins):
                chained[0] += 1
                ins.then_inc(dve_chain, 1)
                dve.wait_ge(dve_chain, chained[0])

            def normalise(xs):
                dve.wait_ge(rstd_ready, xs.stat + 1)
                dve.tensor_scalar(xn[:, xs.b, :], x[:, xs.b, :], mv[:, xs.b, 0:1], rstd[:, xs.b:xs.b + 1],
                                  ALU.subtract, ALU.mult).then_inc(xn_ready, 1)

            def bc(ap, shape):
                return ap.to_broadcast(shape)

            def quantise(src, dst, H, n):
                s4 = src.rearrange("p (j d h) -> p j h d", j=n, h=H)
                scale = qs[:, 0, 0:n * H].rearrange("p (j h) -> p j h", j=n)
                link(dve.tensor_reduce(scale, s4, AX.X, ALU.max, apply_absolute_value=True))
                link(dve.tensor_scalar(qs[:, 1, 0:n * H], qs[:, 0, 0:n * H], 1.0 / 127.0, 1e-8, ALU.mult, ALU.max))
                link(dve.reciprocal(qs[:, 2, 0:n * H], qs[:, 1, 0:n * H]))
                for j in range(n):
                    v = src[:, j * 256:(j + 1) * 256].rearrange("p (d h) -> p d h", h=H)
                    o = dst[:, j * 256:(j + 1) * 256].rearrange("p (d h) -> p d h", h=H)
                    r = qs[:, 2, j * H:(j + 1) * H].rearrange("p (o h) -> p o h", o=1)
                    ins = dve.tensor_tensor(o, v, r.to_broadcast([P, 16, H]), ALU.mult)
                link(ins)
                link(dve.tensor_scalar(dst, dst, MAGIC, MAGIC, ALU.add, ALU.subtract))
                for j in range(n):
                    o = dst[:, j * 256:(j + 1) * 256].rearrange("p (d h) -> p d h", h=H)
                    r = qs[:, 1, j * H:(j + 1) * H].rearrange("p (o h) -> p o h", o=1)
                    ins = dve.tensor_tensor(o, o, r.to_broadcast([P, 16, H]), ALU.mult)
                ins.then_inc(quant_q, 1)

            def pack_tiles(src, n):
                link(dve.tensor_tensor(tmp[:, 0:n], src, powers[:, 0:n], ALU.mult))
                link(dve.tensor_reduce(tmp2[:, 0:n // 4], tmp[:, 0:n].rearrange("p (w t) -> p w t", t=4), AX.X, ALU.add))
                link(dve.tensor_copy(te[:, 0:n // 4], tmp2[:, 0:n // 4]))

            def first_max(src, E, onehot):
                link(dve.tensor_reduce(r8[:, 0, :], src, AX.X, ALU.max))
                mx = r8[:, 0, :].unsqueeze(2).to_broadcast([P, NB, E])
                link(dve.tensor_tensor(rb[:, :, 0:E], src, mx, ALU.is_equal))
                desc = const("desc")[:, 0:E].unsqueeze(1).to_broadcast([P, NB, E])
                link(dve.tensor_tensor(rb[:, :, 0:E], rb[:, :, 0:E], desc, ALU.mult))
                link(dve.tensor_reduce(r8[:, 1, :], rb[:, :, 0:E], AX.X, ALU.max))
                m2 = r8[:, 1, :].unsqueeze(2).to_broadcast([P, NB, E])
                link(dve.tensor_tensor(onehot, rb[:, :, 0:E], m2, ALU.is_equal))

            dve.wait_ge(first_in, 16 * 5)
            link(dve.tensor_scalar(colx[:, 0:1], col("bq0"), float(ATT[0].d) ** -0.5, None, ALU.mult))
            dve.tensor_scalar(colx[:, 1:3], cols[:, col_at["bq2"][0]:col_at["bq2"][1]], float(ATT[2].d) ** -0.5, None,
                              ALU.mult).then_inc(cols_done, 1)
            for s in steps:
                if s.kind == "barrier":
                    dve.wait_ge(rstd_ready, s.stats)
                elif s.kind == "stats":
                    b = s.b
                    if b == 2:
                        dve.wait_ge(rest_in, 32)
                    if s.after is not None:
                        for i in range(BANKS):
                            if s.after[i]:
                                dve.wait_ge(bank_used[i], s.after[i])
                    link(dve.bn_stats(st6[:, :], x[:, b, :]))
                    link(dve.bn_aggr(mv[:, b, :], st6[:, :]))
                    dve.tensor_scalar(vare[:, b:b + 1], mv[:, b, 1:2], EPS, None, ALU.add).then_inc(var_ready, 1)
                elif s.kind == "zero":
                    at = 2048 * s.i
                    link(dve.memset(arena[32:64, at:at + 2048], 0.0))
                    dve.memset(arena[64:96, at:at + 2048], 0.0).then_inc(q_zeroed, 1)
                    link(dve.memset(VA[:, s.i, :, :], 0.0))
                    link(dve.memset(VA[:, s.i, :, SUMCOL:SUMCOL + 1], 1.0))
                elif s.kind == "vblocks":
                    link(dve.memset(VA[:, :, :, :], 0.0))
                    dve.memset(VA[:, :, :, SUMCOL:SUMCOL + 1], 1.0).then_inc(v_blocks, 1)
                    dve.wait_ge(v_blocks, 1)
                elif s.kind == "prepare":
                    dve.wait_ge(const_in, 16 * 6)
                    dve.wait_ge(gates_done, 1)
                    link(dve.tensor_scalar(att[:, :], mask_i[:, :], 0.5, None, ALU.is_gt))
                    link(dve.tensor_scalar(att_b[:, :], att[:, :], 50.0, -50.0, ALU.mult, ALU.add))
                    link(dve.tensor_scalar(tg[:, 8:9], row("gamma"), tg[:, 1:2], None, ALU.mult))
                    link(dve.tensor_scalar(tg[:, 9:10], row("rscale"), 0.0, 0.3, ALU.max, ALU.min))
                    link(dve.tensor_scalar(tg[:, 10:11], tg[:, 6:7], 0.1, None, ALU.mult))
                elif s.kind == "kp":
                    turn(dve, bank_ready, s.m)
                    dve.tensor_tensor(tmp[:, s.j * 256:(s.j + 1) * 256], m_slot(s.m), row("bk3"), ALU.add
                                      ).then_inc(bank_used[s.m % BANKS], 1)
                elif s.kind == "fq3":
                    turn(dve, bank_ready, s.m)
                    dve.tensor_tensor(tmp[:, s.j * 256:(s.j + 1) * 256], m_slot(s.m), row("bq3"), ALU.add
                                      ).then_inc(bank_used[s.m % BANKS], 1)
                elif s.kind == "quant":
                    if s.prev_m is not None:
                        turn(dve, bank_ready, s.prev_m)
                    for m in s.un.m_v:
                        evacuated(dve, m)
                    w = 256 * s.un.A.nb
                    if s.s:
                        link(dve.tensor_scalar(tmp[:, 0:w], tmp[:, 0:w], 0.25, None, ALU.mult))
                    quantise(tmp[:, 0:w], tmp2[:, 0:w], 16, s.un.A.nb)
                elif s.kind == "vscale":
                    evacuated(dve, s.last_m)
                    link(dve.tensor_reduce(vs[:, 2, :], vf[:, :, :], AX.X, ALU.max, apply_absolute_value=True))
                    link(dve.tensor_scalar(vs[:, 0, :], vs[:, 2, :], 1.0 / 127.0, 1e-8, ALU.mult, ALU.max))
                    link(dve.reciprocal(vs[:, 1, :], vs[:, 0, :]))
                    for m in range(2):
                        ins = dve.tensor_scalar(vr[:, m, :], vf[:, m, :], vs[:, 1, m:m + 1], MAGIC, ALU.mult, ALU.add)
                    link(ins)
                    dve.tensor_scalar(vi[:, :, :], vr[:, :, :], MAGIC, None, ALU.subtract).then_inc(v_quant, 1)
                    dve.memset(VQ_made[:, :, :], 0.0).then_inc(v_quant, 1)
                    dve.wait_ge(v_quant, 2)
                elif s.kind == "vturn":
                    turn(dve, bank_ready, s.m)
                    src = m_slot(s.m).bitcast(BF16)[:, 0:256].rearrange("p (h d) -> p h d", d=16)
                    dve.tensor_copy(VQ_made[:, s.c * 16:(s.c + 1) * 16, 0:16], src).then_inc(bank_used[s.m % BANKS], 1)
                elif s.kind in ("fn", "fx", "xt"):
                    normalise(s.xn)
                elif s.kind == "fv":
                    A, n = s.A, s.m
                    turn(dve, bank_ready, n)
                    if s.done_before >= 0:
                        dve.wait_ge(PV_done, s.done_before + 1)
                    if A.layer == 0:
                        for c in range(2):
                            ins = dve.tensor_tensor(VA[:, s.un.g % 3, c * 16:(c + 1) * 16, 0:8],
                                                    m_slot(n)[:, c * P:(c + 1) * P].rearrange("p (h d) -> p h d", d=8),
                                                    row("bv0").rearrange("p (h d) -> p h d", d=8), ALU.add)
                    else:
                        ins = dve.tensor_tensor(VA[:, s.un.g % 3, 0:16, 0:16],
                                                m_slot(n).rearrange("p (h d) -> p h d", d=16),
                                                row("bv2").rearrange("p (h d) -> p h d", d=16), ALU.add)
                    ins.then_inc(bank_used[n % BANKS], 1)
                elif s.kind == "smax":
                    A = s.A
                    turn(dve, bank_ready, s.n)
                    if A.layer == 3:
                        at = s.tc * 32 + s.j
                        dve.tensor_reduce(mxp[:, s.un.g % 2, at:at + 1], psB[:, s.n % BANKS, :], AX.X, ALU.max
                                          ).then_inc(bank_used[s.n % BANKS], 1)
                    else:
                        at = s.tc * A.H + 2 * s.j
                        dve.tensor_reduce(mxp[:, s.un.g % 2, at:at + 2],
                                          psB[:, s.n % BANKS, :].rearrange("p (h n) -> p h n", h=2), AX.X, ALU.max
                                          ).then_inc(bank_used[s.n % BANKS], 1)
                elif s.kind == "negsplit":
                    A, HP = s.A, s.A.H // s.A.parts
                    w = A.TC * HP
                    turn(dve, bank_used, s.last_S)
                    mx = mxp[:, s.un.g % 2, 0:w]
                    if A.layer == 3:
                        halves_ = mxp[:, s.un.g % 2, :].rearrange("p (t h n) -> p t h n", t=A.TC, n=2)
                        link(dve.tensor_reduce(nm[:, 1, 0:w].rearrange("p (t h) -> p t h", t=A.TC),
                                               halves_[:, :, s.j * HP:(s.j + 1) * HP, :], AX.X, ALU.max))
                        mx = nm[:, 1, 0:w]
                    link(dve.tensor_scalar(nm[:, 0, 0:w], mx, -1.0, LN255 if A.layer == 3 else 0.0, ALU.mult, ALU.add))
                    if s.m_prev2 is not None:
                        turn(dve, bank_ready, s.m_prev2)
                    part = npt[:, s.i % 2, 0:3 * w].rearrange("p (t c h) -> p c t h", t=A.TC, c=3)
                    src = nm[:, 0, 0:w].rearrange("p (t h) -> p t h", t=A.TC)
                    left = nm[:, 1, 0:w].rearrange("p (t h) -> p t h", t=A.TC)
                    link(dve.tensor_copy(part[:, 0], src))
                    link(dve.tensor_tensor(left, src, part[:, 0], ALU.subtract))
                    link(dve.tensor_copy(part[:, 1], left))
                    dve.tensor_tensor(part[:, 2], left, part[:, 1], ALU.subtract).then_inc(neg_split, 1)
                elif s.kind == "st" and s.A.layer == 2:
                    turn(dve, T_ready, s.n)
                    if s.clip >= 2:
                        dve.wait_ge(exp_done, s.clip - 1)
                    dve.tensor_scalar(nb_t[:, s.clip % 2, :], psT[:, s.n % 2, 0:512], 50.0, -50.0, ALU.min, ALU.max
                                      ).then_inc(T_used[s.n % 2], 1)
                    turn(dve, T_used, s.n)
                    dve.sem_inc(clipped, 1)
                elif s.kind == "round":
                    w = 4 * s.A.T
                    turn(dve, T_used, s.n)
                    if s.p >= 3:
                        dve.wait_ge(PV_done, s.p - 2)
                    dve.tensor_scalar(n_slot(s.p)[:, 0:w], p_slot(s.A, s.p)[:, 0:w], MAGIC, MAGIC, ALU.add, ALU.subtract
                                      ).then_inc(rounded, 1)
                elif s.kind == "onorm":
                    A = s.A
                    turn(dve, bank_ready, s.m)
                    if s.m_prev is not None:
                        evacuated(dve, s.m_prev)
                    src = m_slot(s.m)[:, 0:A.T].rearrange("p (t h e) -> p t h e", t=A.TC, h=4)
                    link(dve.reciprocal(rden[:, 0:A.TC, :].unsqueeze(3), src[:, :, :, SUMCOL:SUMCOL + 1]))
                    for tc in range(A.TC):
                        HD = A.H * A.d
                        dst = On[:, s.un.g % 2, tc * HD + s.g * 4 * A.d:tc * HD + (s.g + 1) * 4 * A.d]
                        ins = dve.tensor_tensor(dst.rearrange("p (h d) -> p h d", h=4), src[:, tc, :, 0:A.d],
                                                rden[:, tc, :].unsqueeze(2).to_broadcast([P, 4, A.d]), ALU.mult)
                    ins.then_inc(bank_used[s.m % BANKS], 1)
                elif s.kind == "ot" and s.A.layer == 1:
                    u = s.un.u
                    turn(dve, bank_ready, s.m)
                    dve.scalar_tensor_tensor(out=x[:, u, :], in0=m_slot(s.m), scalar=tg[:, 8:9],
                                             in1=x[:, u, :], op0=ALU.mult, op1=ALU.add).then_inc(bank_used[s.m % BANKS], 1)
                    evacuated(dve, s.m)
                elif s.kind == "oy":
                    A, u = s.A, s.un.u
                    turn(dve, bank_ready, s.m)
                    if A.layer == 0:
                        dve.tensor_scalar(y_t[:, :], m_slot(s.m), col("bo0"), tg[:, 0:1], ALU.add, ALU.mult
                                          ).then_inc(bank_used[s.m % BANKS], 1)
                        evacuated(dve, s.m)
                        link(dve.tensor_tensor(x[:, u, :], x[:, u, :], y_t[:, :], ALU.add))
                    elif A.layer == 2:
                        dve.tensor_tensor(y_t[:, :], m_slot(s.m), row("bo2"), ALU.add).then_inc(bank_used[s.m % BANKS], 1)
                        evacuated(dve, s.m)
                        link(dve.tensor_scalar(y_t[:, :], y_t[:, :], tg[:, 9:10], None, ALU.mult))
                        link(dve.bn_stats(st6[:, :], y_t[:, :]))
                        link(dve.bn_aggr(mv2[:, :], st6[:, :]))
                        dve.tensor_scalar(vare2[:, :], mv2[:, 1:2], EPS, None, ALU.add).then_inc(delta_var, 1)
                    else:
                        b = s.un.b0 + s.j
                        dve.tensor_tensor(y_t[:, :], m_slot(s.m), row("bp3"), ALU.add).then_inc(bank_used[s.m % BANKS], 1)
                        evacuated(dve, s.m)
                        link(dve.scalar_tensor_tensor(out=x[:, b, :], in0=y_t[:, :], scalar=tg[:, 3:4],
                                                      in1=x[:, b, :], op0=ALU.mult, op1=ALU.add))
                elif s.kind == "oz":
                    u = s.un.u
                    dve.wait_ge(delta_rstd, u + 1)
                    link(dve.tensor_scalar(tmp2[:, 0:256], y_t[:, :], mv2[:, 0:1], rstd2[:, :], ALU.subtract, ALU.mult))
                    link(dve.tensor_tensor(tmp[:, 0:256], tmp2[:, 0:256], row("lng"), ALU.mult))
                    link(dve.tensor_tensor(tmp2[:, 0:256], tmp[:, 0:256], row("lnb"), ALU.add))
                    link(dve.scalar_tensor_tensor(out=x[:, u, :], in0=tmp2[:, 0:256], scalar=tg[:, 2:3],
                                                  in1=x[:, u, :], op0=ALU.mult, op1=ALU.add))
                elif s.kind == "xl":
                    n = {0: 8, 2: 16, 3: 4}[s.layer]
                    turn(dve, bank_ready, s.m)
                    dve.tensor_copy(lg[:, s.b, 0:n], m_slot(s.m)[:, 0:n]).then_inc(bank_used[s.m % BANKS], 1)
                elif s.kind == "route":
                    evacuated(dve, s.lm)
                    n = {0: 8, 2: 16, 3: 4}[s.layer]
                    L = lg[:, :, 0:n]
                    if s.layer == 3:
                        link(dve.tensor_tensor(L, L, row("br3").unsqueeze(1).to_broadcast([P, NB, n]), ALU.add))
                    if s.layer in (0, 3):
                        first_max(L, n, oh[:, :, 0:n])
                        mx = r8[:, 0, :].unsqueeze(2).to_broadcast([P, NB, n])
                        dve.tensor_tensor(ra[:, :, 0:n], L, mx, ALU.subtract).then_inc(route_a, 1)
                        dve.wait_ge(route_b, s.exp_i + 1)
                        link(dve.tensor_reduce(r8[:, 2, :], ra[:, :, 0:n], AX.X, ALU.add))
                        link(dve.reciprocal(r8[:, 3, :], r8[:, 2, :]))
                        link(dve.tensor_scalar(r8[:, 3, :], r8[:, 3, :], tg[:, 4 + s.layer:5 + s.layer], None, ALU.mult))
                    if s.layer == 3:
                        link(dve.memset(rc[:, 0, 0:4], 0.0))
                        for b in range(1, NB):
                            link(dve.tensor_tensor(rc[:, b, 0:4], rc[:, b - 1, 0:4], oh[:, b - 1, 0:4], ALU.add))
                        link(dve.tensor_tensor(rc[:, 0, 8:12], rc[:, NB - 1, 0:4], oh[:, NB - 1, 0:4], ALU.add))
                        dve.sem_inc(route_pe, 1)
                        turn(dve, bank_ready, s.m)
                        link(dve.tensor_tensor(rb[:, :, 0:4], m_slot(s.m)[:, 0:32].rearrange("p (b e) -> p b e", b=NB),
                                               oh[:, :, 0:4], ALU.mult))
                        dve.tensor_scalar(r8[:, 5, 0:4], m_slot(s.m)[:, 32:36], 1.0 / P, 0.5 - 0.5 / P, ALU.mult, ALU.add
                                          ).then_inc(bank_used[s.m % BANKS], 1)
                        turn(dve, bank_used, s.m)
                        link(dve.tensor_scalar(r8[:, 5, 0:4], r8[:, 5, 0:4], MAGIC, MAGIC, ALU.add, ALU.subtract))
                        link(dve.tensor_reduce(r8[:, 4, :], rb[:, :, 0:4], AX.X, ALU.add))
                        link(dve.memset(ra[:, 0, 0:4], 0.0))
                        for e in range(1, 4):
                            link(dve.tensor_tensor(ra[:, 0, e:e + 1], ra[:, 0, e - 1:e], r8[:, 5, e - 1:e], ALU.add))
                        link(dve.tensor_scalar(ra[:, 1, :], const("tiles")[:, 0:16], ra[:, 0, 1:2], None, ALU.is_ge))
                        for e in range(2, 4):
                            link(dve.scalar_tensor_tensor(out=ra[:, 1, :], in0=const("tiles")[:, 0:16], scalar=ra[:, 0, e:e + 1],
                                                          in1=ra[:, 1, :], op0=ALU.is_ge, op1=ALU.add))
                        pack_tiles(ra[:, 1, :], 16)
                        link(dve.tensor_tensor(rb[:, :, 0:4], oh[:, :, 0:4],
                                               ra[:, 0, 0:4].unsqueeze(1).to_broadcast([P, NB, 4]), ALU.mult))
                        link(dve.tensor_reduce(r8[:, 5, :], rb[:, :, 0:4], AX.X, ALU.add))
                        link(dve.tensor_scalar(r8[:, 5, :], r8[:, 5, :], float(P), None, ALU.mult))
                        link(dve.tensor_tensor(r8[:, 5, :], r8[:, 5, :], r8[:, 4, :], ALU.add))
                        dve.tensor_copy(idx[:, 0, :], r8[:, 5, :]).then_inc(routed3, 1)
                    elif s.layer == 0:
                        link(dve.memset(rc[:, 0, 0:8], 0.0))
                        for b in range(1, NB):
                            link(dve.tensor_tensor(rc[:, b, 0:8], rc[:, b - 1, 0:8], oh[:, b - 1, 0:8], ALU.add))
                        dve.sem_inc(route_pe, 1)
                        turn(dve, bank_ready, s.m)
                        dve.tensor_tensor(rb[:, :, 0:8], m_slot(s.m)[:, 0:64].rearrange("p (b e) -> p b e", b=NB),
                                          oh[:, :, 0:8], ALU.mult).then_inc(bank_used[s.m % BANKS], 1)
                        turn(dve, bank_used, s.m)
                        link(dve.tensor_reduce(r8[:, 4, :], rb[:, :, 0:8], AX.X, ALU.add))
                        link(dve.tensor_tensor(rb[:, :, 0:8], oh[:, :, 0:8],
                                               const("base").unsqueeze(1).to_broadcast([P, NB, 8]), ALU.mult))
                        link(dve.tensor_reduce(r8[:, 5, :], rb[:, :, 0:8], AX.X, ALU.add))
                        link(dve.tensor_tensor(r8[:, 5, :], r8[:, 5, :], r8[:, 4, :], ALU.add))
                        link(dve.tensor_scalar(r8[:, 4, :], r8[:, 4, :], float(P), None, ALU.is_lt))
                        link(dve.tensor_tensor(r8[:, 5, :], r8[:, 5, :], r8[:, 4, :], ALU.mult))
                        link(dve.tensor_copy(idx[:, 1, :], r8[:, 5, :]))
                        link(dve.tensor_scalar(r8[:, 1, :], r8[:, 4, :], -1.0, 1.0, ALU.mult, ALU.add))
                        link(dve.tensor_tensor(r8[:, 1, :], r8[:, 1, :], const("trash"), ALU.mult))
                        link(dve.tensor_tensor(r8[:, 5, :], r8[:, 5, :], r8[:, 1, :], ALU.add))
                        link(dve.tensor_tensor(r8[:, 3, :], r8[:, 3, :], r8[:, 4, :], ALU.mult))
                        dve.tensor_copy(idx[:, 0, :], r8[:, 5, :]).then_inc(routed, 1)
                    else:
                        link(dve.tensor_scalar(ra[:, :, :], L, -87.0, None, ALU.max))
                        dve.sem_inc(route_a, 1)
                        dve.wait_ge(route_b, s.exp_i + 1)
                        link(dve.tensor_scalar(rc[:, :, :], ra[:, :, :], 1.0, None, ALU.add))
                        link(dve.reciprocal(ra[:, :, :], rc[:, :, :]))
                        gb = row("gb2").unsqueeze(1).to_broadcast([P, NB, 16])
                        link(dve.tensor_tensor(rc[:, :, :], ra[:, :, :], gb, ALU.add))
                        first_max(rc[:, :, :], 16, oh[:, :, :])
                        link(dve.tensor_scalar(lg[:, :, :], oh[:, :, :], -1e30, None, ALU.mult))
                        link(dve.tensor_tensor(rc[:, :, :], rc[:, :, :], lg[:, :, :], ALU.add))
                        first_max(rc[:, :, :], 16, lg[:, :, :])
                        for k, pick in enumerate((oh, lg)):
                            link(dve.tensor_tensor(cm[:, :, :], pick[:, :, :], ra[:, :, :], ALU.mult))
                            link(dve.tensor_reduce(wts[:, k, :], cm[:, :, :], AX.X, ALU.add))
                        link(dve.tensor_tensor(r8[:, 2, :], wts[:, 0, :], wts[:, 1, :], ALU.add))
                        link(dve.tensor_scalar(r8[:, 2, :], r8[:, 2, :], 1e-9, None, ALU.add))
                        link(dve.reciprocal(r8[:, 3, :], r8[:, 2, :]))
                        link(dve.tensor_scalar(r8[:, 3, :], r8[:, 3, :], tg[:, 6:7], None, ALU.mult))
                        link(dve.tensor_tensor(wts[:, :, :], wts[:, :, :], r8[:, 3, :].unsqueeze(1).to_broadcast([P, 2, NB]),
                                               ALU.mult))
                        link(dve.tensor_tensor(cm[:, :, :], oh[:, :, :], lg[:, :, :], ALU.add))
                        link(dve.memset(rc[:, 0, :], 0.0))
                        for b in range(1, NB):
                            link(dve.tensor_tensor(rc[:, b, :], rc[:, b - 1, :], cm[:, b - 1, :], ALU.add))
                        link(dve.tensor_tensor(ra[:, 0, :], rc[:, NB - 1, :], cm[:, NB - 1, :], ALU.add))
                        dve.sem_inc(route_pe, 1)
                        turn(dve, bank_ready, s.m)
                        link(dve.tensor_copy(rb[:, :, :], m_slot(s.m)[:, 0:128].rearrange("p (b e) -> p b e", b=NB)))
                        dve.tensor_scalar(ra[:, 1, :], m_slot(s.m)[:, 128:144], 1.0 / P, 0.5 - 0.5 / P, ALU.mult, ALU.add
                                          ).then_inc(bank_used[s.m % BANKS], 1)
                        turn(dve, bank_used, s.m)
                        link(dve.tensor_scalar(ra[:, 1, :], ra[:, 1, :], MAGIC, MAGIC, ALU.add, ALU.subtract))
                        dve.wait_ge(earlier_in, 32)
                        grid = tmp[:, 0:256].rearrange("p (e f) -> p e f", e=16)
                        link(dve.tensor_tensor(grid, earlier.rearrange("p (e f) -> p e f", e=16),
                                               ra[:, 1, :].unsqueeze(1).to_broadcast([P, 16, 16]), ALU.mult))
                        link(dve.tensor_reduce(ra[:, 2, :], grid, AX.X, ALU.add))
                        grid = tmp[:, :].rearrange("p (t e) -> p t e", t=32)
                        link(dve.tensor_tensor(grid, const("tiles").unsqueeze(2).to_broadcast([P, 32, 16]),
                                               ra[:, 2, :].unsqueeze(1).to_broadcast([P, 32, 16]), ALU.is_ge))
                        link(dve.tensor_reduce(tmp2[:, 0:32], grid, AX.X, ALU.add))
                        link(dve.tensor_scalar(tmp2[:, 0:32], tmp2[:, 0:32], 1.0, None, ALU.subtract))
                        pack_tiles(tmp2[:, 0:32], 32)
                        link(dve.tensor_scalar(ra[:, 2, :], ra[:, 2, :], float(P), None, ALU.mult))
                        link(dve.tensor_tensor(rb[:, :, :], rb[:, :, :], ra[:, 2, :].unsqueeze(1).to_broadcast([P, NB, 16]),
                                               ALU.add))
                        for k, pick in enumerate((oh, lg)):
                            link(dve.tensor_tensor(cm[:, :, :], pick[:, :, :], rb[:, :, :], ALU.mult))
                            link(dve.tensor_reduce(r8[:, 5, :], cm[:, :, :], AX.X, ALU.add))
                            link(dve.tensor_copy(idx[:, k, :], r8[:, 5, :]))
                        dve.sem_inc(routed2, 1)
                elif s.kind == "exd":
                    e = s.i
                    turn(dve, bank_ready, s.s)
                    if e >= 2:
                        dve.wait_ge(eo_out[e % 2], 16 * (e // 2))
                    dve.tensor_copy(eo[:, e % 2, :], psB[:, s.s % BANKS, 0:256]).then_inc(bank_used[s.s % BANKS], 1)
                elif s.kind == "tu":
                    turn(dve, T_ready, s.n)
                    dve.wait_ge(silu_done, s.sg + 1)
                    dve.tensor_tensor(htok2[:, s.i % 2, :], psT[:, s.n % 2, P:2 * P], sg[:, s.sg % 2, 0:P], ALU.mult
                                      ).then_inc(T_used[s.n % 2], 1)
                    turn(dve, T_used, s.n)
                    dve.sem_inc(hidden2, 1)
                elif s.kind == "td":
                    turn(dve, bank_ready, s.s)
                    if s.i >= 4:
                        dve.wait_ge(sorted_out[s.i % 4], 16 * (s.i // 4))
                    dve.tensor_copy(so[:, s.i % 4, :], m_slot(s.s)).then_inc(bank_used[s.s % BANKS], 1)
                elif s.kind == "combine2":
                    b = s.b
                    dve.wait_ge(gathered2[b], 32)
                    evacuated(dve, s.m)
                    for k in range(2):
                        link(dve.scalar_tensor_tensor(out=x[:, b, :], in0=ge2[k][:, b, :], scalar=wts[:, k, b:b + 1],
                                                      in1=x[:, b, :], op0=ALU.mult, op1=ALU.add))
                elif s.kind == "su":
                    turn(dve, T_ready, s.n)
                    dve.wait_ge(silu_done, s.sg + 1)
                    if s.g >= 2:
                        turn(dve, bank_ready, hidden_turned[s.g - 2])
                    dve.tensor_tensor(htok[:, s.g % 2, :], psT[:, s.n % 2, 512:1024], sg[:, s.sg % 2, :], ALU.mult
                                      ).then_inc(T_used[s.n % 2], 1)
                    turn(dve, T_used, s.n)
                    dve.sem_inc(hidden3, 1)
                elif s.kind == "sd":
                    turn(dve, bank_ready, s.s)
                    dve.wait_ge(sorted_out[s.i % 4], 16 * (uses2(s.i % 4) + s.i // 4))
                    dve.tensor_copy(so[:, s.i % 4, :], m_slot(s.s)).then_inc(bank_used[s.s % BANKS], 1)
                elif s.kind == "combine3":
                    b = s.b
                    dve.wait_ge(gathered3[b], 16)
                    dve.scalar_tensor_tensor(out=x[:, b, :], in0=gathered_x[:, b, :], scalar=r8[:, 3, b:b + 1],
                                             in1=x[:, b, :], op0=ALU.mult, op1=ALU.add).then_inc(combined3, 1)
                elif s.kind == "combine":
                    b = s.b
                    dve.wait_ge(gathered[b], 16)
                    dve.scalar_tensor_tensor(out=x[:, b, :], in0=gathered_x[:, b, :], scalar=r8[:, 3, b:b + 1],
                                             in1=x[:, b, :], op0=ALU.mult, op1=ALU.add).then_inc(combined, 1)
                    dve.wait_ge(combined, b + 1)
                elif s.kind == "gu":
                    w = s.width
                    if s.ch == 0 and s.h_free is not None:
                        turn(dve, bank_ready, s.h_free)
                    dve.wait_ge(silu_done, s.sg + 1)
                    up = psT[0:w, s.n % 2, 512:1024]
                    dst = hidden(s.layer)[0:w, s.h % 2, s.ch, :]
                    if s.layer == 1:
                        ins = dve.scalar_tensor_tensor(out=dst, in0=up, scalar=col("us1", s.ch, w),
                                                       in1=sg[0:w, s.sg % 2, :], op0=ALU.mult, op1=ALU.mult)
                    else:
                        ins = dve.tensor_tensor(dst, up, sg[0:w, s.sg % 2, :], ALU.mult)
                    ins.then_inc(T_used[s.n % 2], 1)
                elif s.kind == "down":
                    b = s.tg * 4 + s.tc
                    turn(dve, bank_ready, s.n)
                    for i in range(BANKS):
                        if s.x_after[i]:
                            dve.wait_ge(bank_used[i], s.x_after[i])
                    src = psB[:, s.n % BANKS, 0:256]
                    if s.layer == 1:
                        link(dve.tensor_tensor(tmp[:, 0:256], src, row("ds1"), ALU.mult))
                        src, w = tmp[:, 0:256], tg[:, 5:6]
                    else:
                        w = tg[:, 10:11]
                    dve.scalar_tensor_tensor(out=x[:, b, :], in0=src, scalar=w, in1=x[:, b, :],
                                             op0=ALU.mult, op1=ALU.add).then_inc(bank_used[s.n % BANKS], 1)

        @block.gpsimd
        def _(pool):
            chained = [0]

            def link(ins):
                chained[0] += 1
                ins.then_inc(pool_chain, 1)
                pool.wait_ge(pool_chain, chained[0])

            def split(src, dst, w, order, done):
                high, middle, low = [dst[:, i, 0:w] for i in order]
                link(pool.tensor_scalar(high, src, 1.0, 0.0, ALU.mult, ALU.add))
                link(pool.tensor_tensor(rem[:, 0:w], src, high, ALU.subtract))
                link(pool.tensor_scalar(middle, rem[:, 0:w], 1.0, 0.0, ALU.mult, ALU.add))
                pool.tensor_tensor(low, rem[:, 0:w], middle, ALU.subtract).then_inc(done, 1)

            pool.wait_ge(first_in, 16 * 5)
            for s in steps:
                if s.kind == "barrier":
                    pool.wait_ge(rstd_ready, s.stats)
                elif s.kind == "stats":
                    pool.wait_ge(var_ready, s.i + 1)
                    pool.tensor_tensor(rstd[:, s.b:s.b + 1], vare[:, s.b:s.b + 1], const("mhalf"), ALU.pow
                                       ).then_inc(rstd_ready, 1)
                elif s.kind == "split":
                    A, u = s.A, s.un
                    w = A.halves * A.T
                    if s.kind_of == "qk":
                        if u.g >= 1:
                            pool.wait_ge(parts_q, u.g)
                        if A.layer == 1:
                            pool.wait_ge(xn_ready, u.xn.i + 1)
                            link(pool.tensor_scalar(qf[:, u.g % 2, 0:256], xn[:, u.u, :], 0.25, 0.0, ALU.mult, ALU.add))
                        else:
                            evacuated(pool, u.m[0])
                            evacuated(pool, u.m[1])
                        if u.g >= 2:
                            pool.wait_ge(q_stored[u.g % 2], 32 * (u.g // 2))
                        split(qf[:, u.g % 2, 0:w], sq[:, u.g % 2], w, (2, 1, 0), parts_q)
                        pool.wait_ge(parts_q, u.g + 1)
                    if u.k is not None:
                        if A.layer != 1:
                            evacuated(pool, u.m[1])
                        if s.kind_of == "k":
                            evacuated(pool, u.m[0])
                        if u.k >= 2:
                            pool.wait_ge(k_stored[u.k % 2], 32 * (u.k // 2))
                        src = ctx_s[:, u.u, :] if A.layer == 1 else kf[:, u.k % 2, 0:w]
                        split(src, sk[:, u.k % 2], w, (0, 1, 2), parts_k)
                        pool.wait_ge(parts_k, u.k + 1)
                elif s.kind == "prepare":
                    pool.wait_ge(const_in, 16 * 6)
                elif s.kind == "packs" and s.A.layer == 1:
                    u = s.un
                    if s.done_before >= 0:
                        pool.wait_ge(PV_done, s.done_before + 1)
                    pool.wait_ge(v_blocks, 1)
                    for c in range(2):
                        ins = pool.tensor_copy(VA[:, u.g % 3, c * 8:(c + 1) * 8, 0:16],
                                               ctx_t[:, c, u.u * P:(u.u + 1) * P].rearrange("p (h d) -> p h d", d=16))
                    ins.then_inc(V_copied, 1)
                elif s.kind == "oy" and s.A.layer == 2:
                    pool.wait_ge(delta_var, s.un.u + 1)
                    pool.tensor_tensor(rstd2[:, :], vare2[:, :], const("mhalf"), ALU.pow).then_inc(delta_rstd, 1)
                elif s.kind == "scatter":
                    if s.b == 0:
                        pool.wait_ge(routed, 1)
                        pool.wait_ge(zero_in, 16 * 4)
                    pool.indirect_dma_start(xd, bass.IndirectOffsetOnAxis(ap=idx[:, 0, s.b:s.b + 1].bitcast(U32), axis=0),
                                            xn[:, s.b, :], None).then_inc(scattered, 16)
                elif s.kind == "scatter2":
                    if s.b == 0:
                        pool.wait_ge(routed2, 1)
                    for k in range(2):
                        pool.indirect_dma_start(xd, bass.IndirectOffsetOnAxis(ap=idx[:, k, s.b:s.b + 1].bitcast(U32), axis=0),
                                                xn[:, s.b, :], None).then_inc(scattered2, 16)
                elif s.kind == "gather2":
                    if s.b == 0:
                        for i in range(4):
                            pool.wait_ge(sorted_out[i], 16 * uses2(i))
                    for k in range(2):
                        pool.indirect_dma_start(ge2[k][:, s.b, :], None, sod,
                                                bass.IndirectOffsetOnAxis(ap=idx[:, k, s.b:s.b + 1].bitcast(U32), axis=0)
                                                ).then_inc(gathered2[s.b], 16)
                elif s.kind == "scatter3":
                    if s.b == 0:
                        pool.wait_ge(routed3, 1)
                    pool.indirect_dma_start(xd, bass.IndirectOffsetOnAxis(ap=idx[:, 0, s.b:s.b + 1].bitcast(U32), axis=0),
                                            xn[:, s.b, :], None).then_inc(scattered3, 16)
                elif s.kind == "gather3":
                    if s.b == 0:
                        for i in range(4):
                            pool.wait_ge(sorted_out[i], 16 * (uses2(i) + (TILES3 - 1 - i) // 4 + 1))
                    pool.indirect_dma_start(gathered_x[:, s.b, :], None, sod,
                                            bass.IndirectOffsetOnAxis(ap=idx[:, 0, s.b:s.b + 1].bitcast(U32), axis=0)
                                            ).then_inc(gathered3[s.b], 16)
                elif s.kind == "gather":
                    if s.b == 0:
                        for i in range(2):
                            pool.wait_ge(eo_out[i], 16 * 4)
                    pool.indirect_dma_start(gathered_x[:, s.b, :], None, eod,
                                            bass.IndirectOffsetOnAxis(ap=idx[:, 1, s.b:s.b + 1].bitcast(U32), axis=0)
                                            ).then_inc(gathered[s.b], 16)


def pack(sp, A, dst, src, width, sem, is_q, heads=None):
    at, (h0, h1) = 0, heads or (0, A.H)
    for first in range(3):
        n = 3 - first
        c0 = first if is_q else 0
        rows = dst[at * A.d:(at + n) * A.d, 0:A.H * width].rearrange("r (h n) -> r h n", h=A.H)
        at += n
        if A.layer == 1:
            for c in range(n):
                sp.dma_start(rows[c * A.d:(c + 1) * A.d], src[c0 + c, :, 0:width].rearrange("(h d) n -> d h n", d=A.d)
                             ).then_inc(sem, 16)
        else:
            sp.dma_start(rows[:, h0:h1, :], src[c0:c0 + n, :, 0:width].rearrange("c (d h) n -> (c d) h n", d=A.d)[:, h0:h1, :]
                         ).then_inc(sem, 16)


def kernel(**inputs):
    import numpy as np
    import concourse.bacc as bacc
    from concourse.bass_utils import run_bass_kernel_spmd as run

    a = {k: np.asarray(v) for k, v in inputs.items()}

    def halves(w):
        k, n = w.shape
        c = -(-k // P)
        full = np.zeros((c * P, n), w.dtype)
        full[:k] = w
        return full.reshape(c, P, n).transpose(1, 0, 2)

    def flat(*ws):
        return np.ascontiguousarray(np.concatenate([halves(w).reshape(P, -1) for w in ws], axis=1))

    def d_major(w, heads):
        n = w.shape[-1] // heads
        return w.reshape(*w.shape[:-1], heads, n).swapaxes(-1, -2).reshape(w.shape)

    arrays = {"x": a["x"], "ctx": a["ctx_2048"]}
    arrays["ctx_t"] = halves(a["ctx_2048"].reshape(NT, D).T)
    arrays["mask"] = a["mask_BxS2_ik0"].T
    vals = {"g_xattn": a["g_xattn"], "g_ffn": a["g_ffn"], "gamma": a["L1_xattn_gamma"].reshape(1),
            "rscale": a["L2_xattn_residual_scale"].reshape(1), "bv0": a["L0_xattn_bv"], "bv2": a["L2_xattn_bv"],
            "bo2": a["L2_xattn_bo"], "lng": a["L2_xattn_ln_gamma"], "lnb": a["L2_xattn_ln_beta"],
            "bq3": d_major(a["L3_xattn_bq"], 16), "bk3": d_major(a["L3_xattn_bkv"][:256], 16),
            "bp3": a["L3_xattn_bp"], "ds1": a["L1_ffn_down_s"], "br3": a["L3_ffn_br"], "gb2": a["L2_ffn_gate_bias"]}
    arrays["rows"] = np.concatenate([vals[n].reshape(-1) for n, _ in ROWS])
    cvals = {"bq0": d_major(a["L0_xattn_bq"], 16), "bk0": d_major(a["L0_xattn_bk"], 16), "bo0": a["L0_xattn_bo"],
             "bq2": d_major(a["L2_xattn_bq"], 16), "bk2": d_major(a["L2_xattn_bk"], 16),
             "bv3": a["L3_xattn_bkv"][256:], "gs1": a["L1_ffn_gate_s"], "us1": a["L1_ffn_up_s"]}
    arrays["cols"] = np.concatenate([halves(cvals[n].reshape(-1, 1)).reshape(P, -1) for n, _ in COLS], axis=1)
    part = np.arange(P, dtype=np.float32)
    sumsel = np.zeros((P, EW), np.float32)
    sumsel[:, SUMCOL] = 1.0
    arrays["cst"] = np.concatenate([
        np.eye(P, dtype=np.float32), np.triu(np.ones((P, P), np.float32), 1), np.ones((P, P), np.float32),
        np.tile(16.0 - np.arange(16, dtype=np.float32), (P, 1)), np.tile(128.0 * np.arange(8, dtype=np.float32), (P, 1)),
        TRASH + part[:, None] + P * np.arange(NB, dtype=np.float32), np.full((P, 1), -0.5, np.float32), sumsel,
        np.tile(np.arange(32, dtype=np.float32), (P, 1)), np.zeros((P, 1), np.float32)], axis=1)
    arrays["earlier"] = np.tile(np.tril(np.ones((16, 16), np.float32), -1).reshape(1, -1), (P, 1))
    arrays["powers"] = np.tile((16.0 ** (np.arange(32) % 4)).astype(np.float32), (P, 1))
    b16 = mybir.dt.np(BF16)
    arrays["ident16"] = np.eye(P).astype(b16)
    arrays["zeros"] = np.zeros((NT, D), np.float32)
    arrays["ones3"] = np.ones((3, 4096), b16)
    arrays["w_at0"] = np.stack([d_major(a["L0_xattn_Wq"].T, 16), d_major(a["L0_xattn_Wk"].T, 16),
                                a["L0_xattn_Wv"].T, a["L0_xattn_Wo"].T], axis=1)
    arrays["w_at2"] = np.stack([halves(w) for w in (d_major(a["L2_xattn_Wq"].T, 16), d_major(a["L2_xattn_Wk"].T, 16),
                                                    a["L2_xattn_Wv"].T, a["L2_xattn_Wo"].T)], axis=1)
    wkv = a["L3_xattn_Wkv"]
    arrays["w_at3"] = np.stack([halves(w) for w in (d_major(a["L3_xattn_Wq"], 16), d_major(wkv[:, :256], 16),
                                                    wkv[:, 256:], a["L3_xattn_Wp"])], axis=1)
    arrays["wr"] = np.concatenate([halves(a["L0_ffn_w_gate"]), halves(a["L2_ffn_centroids"].T), halves(a["L3_ffn_Wr"])],
                                  axis=2)
    for e in range(8):
        arrays[f"w{e}"] = flat(a["L0_ffn_w1"][e], a["L0_ffn_w2"][e])
    arrays["w8"] = flat(a["L1_ffn_gate_w"].T, a["L1_ffn_up_w"].T, a["L1_ffn_down_w"].T)
    arrays["w9"] = flat(a["L2_ffn_wg_s"], a["L2_ffn_wu_s"], a["L2_ffn_wd_s"])
    for g in range(2):
        arrays[f"w{10 + g}"] = np.concatenate([
            np.concatenate([halves(a["L2_ffn_wg"][e]), halves(a["L2_ffn_wu"][e])], axis=2).reshape(P, -1)
            if part == 0 else a["L2_ffn_wd"][e] for e in range(8 * g, 8 * g + 8) for part in range(2)], axis=1)
    for e in range(4):
        arrays[f"w{12 + e}"] = flat(a["L3_ffn_Wg"][e], a["L3_ffn_Wu"][e], a["L3_ffn_Wd"][e])

    nc = bacc.Bacc("TRN2", target_bir_lowering=False, num_devices=1)
    feeds, views = {}, {}
    for name, v in arrays.items():
        v = np.ascontiguousarray(v)
        feeds[f"in_{name}"] = v
        views[name] = nc.dram_tensor(f"in_{name}", v.shape, mybir.dt.from_np(v.dtype), kind="ExternalInput").ap()
    out = nc.dram_tensor("out_x", [NB, S, D], F32, kind="ExternalOutput").ap()
    flamingo(nc, views, out)
    r = run(nc, [feeds], core_ids=[0])
    return r.results[0]["out_x"]
```
